# Optimizing a Trainium2 kernel written in Bass

```python
import numpy as np
import jax
import jax.numpy as jnp

def _softmax(x, axis=-1):
    return jax.nn.softmax(x, axis=axis)

def _gelu(x):
    return jax.nn.gelu(x, approximate=True)

def _silu(x):
    return jax.nn.silu(x)

def _sigmoid(x):
    return jax.nn.sigmoid(x)

def _layernorm(x, axis=-1, eps=1e-05):
    m = jnp.mean(x, axis=axis, keepdims=True)
    v = jnp.var(x, axis=axis, keepdims=True)
    return (x - m) / jnp.sqrt(v + eps)

def _scatter_add(tgt, idx, src, axis=0):
    return tgt.at[idx].add(src)

def _segment_sum(src, seg, n):
    return jax.ops.segment_sum(src, seg, n)
kernel_name = 'mk_gps_d1_gnn_r32_2c7c95'

def setup_inputs(seed: int=0):
    np.random.seed(seed)
    _w = jnp.asarray

    def _rec_inputs():
        import jax
        import jax.numpy as jnp
        _gk = jax.random.key(seed)
        x = -0.0003713 + 1 * jax.random.normal(jax.random.fold_in(_gk, 1), (3125, 256), jnp.float32)
        src = jax.random.randint(jax.random.fold_in(_gk, 2), (50000,), 0, 3125, jnp.int32)
        dst = jnp.minimum((3125 * jax.random.uniform(jax.random.fold_in(_gk, 3), (50000,)) ** 2.0).astype(jnp.int32), 99999)
        _o = jnp.argsort(dst, stable=True)
        src = src[_o]
        dst = dst[_o]
        edge_type_8 = jax.random.randint(jax.random.fold_in(_gk, 12), (50000,), 0, 8, jnp.int32)
        edge_weight = jax.random.uniform(jax.random.fold_in(_gk, 13), (50000,), jnp.float32, 0.0, 1)
        return (x, src, dst, edge_type_8, edge_weight)
    x, src, dst, edge_type_8, edge_weight = _rec_inputs()

    def _L0_gnn_setup():
        import jax, jax.numpy as jnp
        import numpy as np
        N_NODES = 50000
        N_EDGES = 25000
        IN_FEAT = 256
        OUT_FEAT = 256
        NUM_RELS = 8
        NUM_BASES = 8
        SUBMAT_IN = IN_FEAT // NUM_BASES
        SUBMAT_OUT = OUT_FEAT // NUM_BASES
        key = jax.random.key(seed)
        k_h, k_w, k_src, k_dst, k_rel, k_norm = jax.random.split(key, 6)
        h = jax.random.normal(k_h, (N_NODES, IN_FEAT), dtype=jnp.float32)
        weight = jax.random.normal(k_w, (NUM_RELS, NUM_BASES * SUBMAT_IN * SUBMAT_OUT), dtype=jnp.float32) * 0.05
        edge_src = jax.random.randint(k_src, (N_EDGES,), 0, N_NODES, dtype=jnp.int32)
        edge_dst = jax.random.randint(k_dst, (N_EDGES,), 0, N_NODES, dtype=jnp.int32)
        edge_rel = jax.random.randint(k_rel, (N_EDGES,), 0, NUM_RELS, dtype=jnp.int32)
        edge_norm = jax.random.uniform(k_norm, (N_EDGES,), dtype=jnp.float32)
        return {'h': h, 'weight': weight, 'edge_src': edge_src, 'edge_dst': edge_dst, 'edge_rel': edge_rel, 'edge_norm': edge_norm}
    _L0_gnn_all = _L0_gnn_setup()
    _L0_gnn_in = {k: v for k, v in _L0_gnn_all.items() if k in ('weight',)}
    del _L0_gnn_all

    def _L0_mix_setup():
        import jax, jax.numpy as jnp
        import numpy as np
        N, F, C, H = (32, 128, 256, 8)
        D = C // H
        EPS_ATTN = 1e-06
        EPS_LN = 1e-05

        def layer_norm(x, g, b):
            mu = jnp.mean(x, axis=-1, keepdims=True)
            var = jnp.var(x, axis=-1, keepdims=True)
            return (x - mu) * jax.lax.rsqrt(var + EPS_LN) * g + b
        key = jax.random.key(seed)
        ks = jax.random.split(key, 8)
        s = 1.0 / np.sqrt(C)
        return {'x': jax.random.normal(ks[0], (N, F, C), jnp.float32), 'Wqkv': jax.random.uniform(ks[1], (3 * C, C), jnp.float32, -s, s), 'ln1_g': jnp.ones((C,), jnp.float32), 'ln1_b': jnp.zeros((C,), jnp.float32), 'W1': jax.random.uniform(ks[2], (C, C), jnp.float32, -s, s), 'b1': jax.random.uniform(ks[3], (C,), jnp.float32, -s, s), 'W2': jax.random.uniform(ks[4], (C, C), jnp.float32, -s, s), 'b2': jax.random.uniform(ks[5], (C,), jnp.float32, -s, s), 'ln2_g': jnp.ones((C,), jnp.float32), 'ln2_b': jnp.zeros((C,), jnp.float32)}
    _L0_mix_all = _L0_mix_setup()
    _L0_mix_in = {k: v for k, v in _L0_mix_all.items() if k in ('Wqkv', 'ln1_g', 'ln1_b', 'W1', 'b1', 'W2', 'b2', 'ln2_g', 'ln2_b')}
    del _L0_mix_all

    def _L0_ffn_setup():
        import jax, jax.numpy as jnp
        import numpy as np
        TOP_K = 2
        key = jax.random.key(seed)
        ks = jax.random.split(key, 4)
        B, L, D, H, E = (8, 128, 256, 1024, 8)
        s = 0.02
        return {'x': jax.random.normal(ks[0], (B, L, D), jnp.float32), 'Wg': jax.random.normal(ks[1], (D, E), jnp.float32) * s, 'bg': jnp.zeros((E,), jnp.float32), 'W1': jax.random.normal(ks[2], (E, D, H), jnp.float32) * s, 'b1': jnp.zeros((E, H), jnp.float32), 'W2': jax.random.normal(ks[3], (E, H, D), jnp.float32) * s, 'b2': jnp.zeros((E, D), jnp.float32)}
    _L0_ffn_all = _L0_ffn_setup()
    _L0_ffn_in = {k: v for k, v in _L0_ffn_all.items() if k in ('Wg', 'bg', 'W1', 'b1', 'W2', 'b2')}
    del _L0_ffn_all
    return {'x': x, 'src': src, 'dst': dst, 'edge_type_8': edge_type_8, 'edge_weight': edge_weight, 'L0_gnn_weight': _L0_gnn_in['weight'], 'L0_mix_Wqkv': _L0_mix_in['Wqkv'], 'L0_mix_ln1_g': _L0_mix_in['ln1_g'], 'L0_mix_ln1_b': _L0_mix_in['ln1_b'], 'L0_mix_W1': _L0_mix_in['W1'], 'L0_mix_b1': _L0_mix_in['b1'], 'L0_mix_W2': _L0_mix_in['W2'], 'L0_mix_b2': _L0_mix_in['b2'], 'L0_mix_ln2_g': _L0_mix_in['ln2_g'], 'L0_mix_ln2_b': _L0_mix_in['ln2_b'], 'L0_ffn_Wg': _L0_ffn_in['Wg'], 'L0_ffn_bg': _L0_ffn_in['bg'], 'L0_ffn_W1': _L0_ffn_in['W1'], 'L0_ffn_b1': _L0_ffn_in['b1'], 'L0_ffn_W2': _L0_ffn_in['W2'], 'L0_ffn_b2': _L0_ffn_in['b2']}

def reference(x, src, dst, edge_type_8, edge_weight, L0_gnn_weight, L0_mix_Wqkv, L0_mix_ln1_g, L0_mix_ln1_b, L0_mix_W1, L0_mix_b1, L0_mix_W2, L0_mix_b2, L0_mix_ln2_g, L0_mix_ln2_b, L0_ffn_Wg, L0_ffn_bg, L0_ffn_W1, L0_ffn_b1, L0_ffn_W2, L0_ffn_b2):
    import jax
    import jax.numpy as jnp

    def _L0_gnn_ref(h, weight, edge_src, edge_dst, edge_rel, edge_norm):
        import jax, jax.numpy as jnp
        import numpy as np
        N_NODES = 50000
        N_EDGES = 25000
        IN_FEAT = 256
        OUT_FEAT = 256
        NUM_RELS = 8
        NUM_BASES = 8
        SUBMAT_IN = IN_FEAT // NUM_BASES
        SUBMAT_OUT = OUT_FEAT // NUM_BASES
        'RGCNBlockLayer forward (self_loop=False, bias=None, activation=None).\n\n            Per relation r: agg_r[v] = sum_{(u->v) in rel r} norm_e * h[u]\n            then block-diagonal matmul out_r = blockmm(agg_r, W_r); output = sum_r out_r.\n            '
        N, in_feat = h.shape
        R = weight.shape[0]
        msg = h[edge_src] * edge_norm[:, None]
        seg = edge_rel * N + edge_dst
        agg = jax.ops.segment_sum(msg, seg, num_segments=R * N)
        agg = agg.reshape(R, N, NUM_BASES, SUBMAT_IN)
        W = weight.reshape(R, NUM_BASES, SUBMAT_IN, SUBMAT_OUT)
        out = jnp.einsum('rnbi,rbio->nbo', agg, W)
        return out.reshape(N, NUM_BASES * SUBMAT_OUT)

    def _L0_mix_ref(x, Wqkv, ln1_g, ln1_b, W1, b1, W2, b2, ln2_g, ln2_b):
        import jax, jax.numpy as jnp
        import numpy as np
        N, F, C, H = (32, 128, 256, 8)
        D = C // H
        EPS_ATTN = 1e-06
        EPS_LN = 1e-05

        def layer_norm(x, g, b):
            mu = jnp.mean(x, axis=-1, keepdims=True)
            var = jnp.var(x, axis=-1, keepdims=True)
            return (x - mu) * jax.lax.rsqrt(var + EPS_LN) * g + b
        n, f, c = x.shape
        qkv = jnp.einsum('nfc,oc->nfo', x, Wqkv)
        q, k, v = jnp.split(qkv, 3, axis=-1)
        q = q.reshape(n, f, H, D)
        k = k.reshape(n, f, H, D)
        v = v.reshape(n, f, H, D)
        q = jax.nn.elu(q) + 1.0
        k = jax.nn.elu(k) + 1.0
        kv = jnp.einsum('nshd,nshm->nhmd', k, v)
        ksum = jnp.sum(k, axis=1)
        z = 1.0 / (jnp.einsum('nlhd,nhd->nlh', q, ksum) + EPS_ATTN)
        t = jnp.einsum('nlhd,nhmd,nlh->nlhm', q, kv, z)
        t = t.reshape(n, f, c)
        x1 = layer_norm(t + x, ln1_g, ln1_b)
        h = jax.nn.gelu(jnp.einsum('nfc,oc->nfo', x1, W1) + b1, approximate=False)
        y = jnp.einsum('nfc,oc->nfo', h, W2) + b2
        return layer_norm(y + x1, ln2_g, ln2_b)

    def _L0_ffn_ref(x, Wg, bg, W1, b1, W2, b2):
        import jax, jax.numpy as jnp
        import numpy as np
        TOP_K = 2
        B, L, D = x.shape
        E = W1.shape[0]
        xf = x.reshape(-1, D)
        gate_logits = xf @ Wg + bg
        top_w, top_i = jax.lax.top_k(gate_logits, TOP_K)
        top_w = jax.nn.softmax(top_w, axis=-1)
        w_dense = jnp.sum(jax.nn.one_hot(top_i, E, dtype=xf.dtype) * top_w[..., None], axis=1)
        out = jnp.zeros_like(xf)
        for e in range(E):
            h = jax.nn.gelu(xf @ W1[e] + b1[e], approximate=False)
            out = out + w_dense[:, e:e + 1] * (h @ W2[e] + b2[e])
        return out.reshape(B, L, D)
    xn = _layernorm(x, axis=-1)
    x = x + _L0_gnn_ref(xn, L0_gnn_weight, src, dst, edge_type_8, edge_weight) + _L0_mix_ref(xn[None], L0_mix_Wqkv, L0_mix_ln1_g, L0_mix_ln1_b, L0_mix_W1, L0_mix_b1, L0_mix_W2, L0_mix_b2, L0_mix_ln2_g, L0_mix_ln2_b)[0]
    x = x + _L0_ffn_ref(_layernorm(x, axis=-1)[None], L0_ffn_Wg, L0_ffn_bg, L0_ffn_W1, L0_ffn_b1, L0_ffn_W2, L0_ffn_b2)[0]
    return x

_drawn_inputs = setup_inputs


def setup_inputs(seed=0):
    import zlib

    import numpy as np

    out = dict(_drawn_inputs(seed))
    spreads = {'L0_mix_ln1_g': (1.0, 0.2),
     'L0_mix_ln1_b': (0.0, 0.1),
     'L0_mix_ln2_g': (1.0, 0.2),
     'L0_mix_ln2_b': (0.0, 0.1),
     'L0_ffn_bg': (0.0, 0.336),
     'L0_ffn_b1': (0.0, 0.643),
     'L0_ffn_b2': (0.0, 0.1)}
    factors = {'L0_mix_Wqkv': 8.0, 'L0_mix_b1': 8.0, 'L0_mix_b2': 3.196}
    for name, (base, spread) in spreads.items():
        noise = np.random.default_rng([zlib.crc32(name.encode()), seed]).standard_normal(out[name].shape)
        drawn = base * np.exp(spread * noise) if base else spread * noise
        out[name] = jnp.asarray(drawn.astype(out[name].dtype))
    for name, factor in factors.items():
        out[name] = (out[name] * factor).astype(out[name].dtype)
    return out
```

```python
from contextlib import ExitStack

import concourse.bass as bass
from concourse import mybir

F32 = mybir.dt.float32
I32 = mybir.dt.int32
U32 = mybir.dt.uint32
ALU = mybir.AluOpType
ACT = mybir.ActivationFunctionType
AX_X = mybir.AxisListType.X

P = 128
N, C = 3125, 256
NT = -(-N // P)
NP = NT * P
CC = C // P
E = 50000
GT = 4
NG = -(-E // (GT * P))
SLOTS = 6
ROUNDS = NG // SLOTS
TAIL = NG % SLOTS
GP = (ROUNDS + 1) * SLOTS
R = 8
HEADS = 8
HC = HEADS // CC
HD = C // HEADS
KW = P + HC
X = 8
HID = 1024
MC = HID // P
EPS_LN = 1e-5
EPS_ATTN = 1e-6
LG = 5
KEY_ROUNDS = (NT - 1) // SLOTS
CAP = NP + P
ROW = 264
TOK, WT, EX = C, C + 1, C + 3


ARENA = 2 * LG * C + LG * C + CC * R * P + LG * R * C


def build(nc, a, out):
    assert NT == LG * LG and NT % 2 and TAIL == 2 and ROUNDS % 2 == 0
    assert KEY_ROUNDS * SLOTS == NT - 1 and ROUNDS - KEY_ROUNDS == NT // 2
    ctx = ExitStack()
    with ctx:
        def sb(name, shape, dt=F32):
            return ctx.enter_context(nc.sbuf_tensor(name, shape, dt))

        def pb(name, shape):
            return ctx.enter_context(nc.psum_tensor(name, shape, F32))

        def sem(name):
            return ctx.enter_context(nc.semaphore(name))

        y_dram = nc.dram_tensor("rel_messages", [NP * R, C], F32, kind="Internal").ap()
        range_dram = nc.dram_tensor("group_ranges", [NG, 2], I32, kind="Internal").ap()
        slot_dram = nc.dram_tensor("expert_rows", [X * CAP, ROW], F32, kind="Internal").ap()

        acc = sb("acc", [P, NT, C])
        xn = sb("xn", [P, NT, C])
        xnT = sb("xnT", [P, NT, CC, P])
        ident = sb("ident", [P, P])
        upper = sb("upper", [P, P])
        ones = sb("ones", [P, P])
        blockmask = sb("blockmask", [P, KW])
        nodemask = sb("nodemask", [P, NT])
        vecs = sb("vecs", [P, 5, C])
        b1T = sb("b1T", [P, CC])
        wqT = sb("wqT", [P, CC, C])
        wkvT = sb("wkvT", [P, CC, 2 * C])
        w1T = sb("w1T", [P, CC, C])
        w2T = sb("w2T", [P, CC, C])
        wg = sb("wg", [P, CC, X])
        bg = sb("bg", [P, X])
        eb1T = sb("eb1T", [P, X, MC])
        eb2 = sb("eb2", [P, X, C])
        capcol = sb("capcol", [P, X])
        iota8 = sb("iota8", [P, X])
        padrows = sb("padrows", [P, ROW])
        srcT = sb("srcT", [P, GP * GT], I32)
        relT = sb("relT", [P, GP * GT], I32)
        dstT = sb("dstT", [P, GP * GT], I32)
        idx = sb("idx", [P, GP * GT], I32)
        dstf = sb("dstf", [P, GP * GT])
        ew = sb("ew", [P, GP * GT])
        dstrow = sb("dstrow", [NG, GT * P], I32)
        rng2 = sb("rng2", [NG, 2], I32)
        rng3 = sb("rng3", [NG, 2], I32)
        ranges = sb("ranges", [1, NG * 2], I32)
        iota = sb("iota", [P, NP])
        tokid = sb("tokid", [P, NT])
        zeros = sb("zeros", [P, C])
        gidx = sb("gidx", [P, 2, SLOTS * GT], I32)
        oh = sb("oh", [P, GT, P])
        st = sb("st", [P, LG, 6])
        mv = sb("mv", [P, LG, 2])
        rs = sb("rs", [P, LG])
        st2 = sb("st2", [P, 2, 6])
        mv2 = sb("mv2", [P, 2, 2])
        rs2 = sb("rs2", [P, 2])
        eps = sb("eps", [P, 1])
        var = sb("var", [P, LG])
        minus_half = sb("minus_half", [P, LG])
        arena = sb("arena", [P, ARENA])

        def view(lo, n):
            return arena[:, lo:lo + n]
        xs = view(0, 2 * LG * C).rearrange("p (j c) -> p j c", j=2 * LG)
        o = 2 * LG * C
        xTs = view(o, LG * C).rearrange("p (s c n) -> p s c n", s=LG, c=CC)
        o += LG * C
        wblk = view(o, CC * R * P).rearrange("p (c r o) -> p c r o", c=CC, r=R)
        o += CC * R * P
        ys = view(o, LG * R * C).rearrange("p (j r c) -> p j r c", j=LG, r=R)
        assert o + LG * R * C <= ARENA
        ring = view(0, SLOTS * GT * C).rearrange("p (s j c) -> p s j c", s=SLOTS, j=GT)
        o = SLOTS * GT * C
        kvx = view(o, C).rearrange("p (c n) -> p c n", c=CC)
        ek = view(o + C, 2 * C)
        ks = view(o + 3 * C, C)
        vs = view(o + 4 * C, C)
        kvr = view(o + 5 * C, CC * KW).rearrange("p (c k) -> p c k", c=CC)
        o += 5 * C + CC * KW
        qs = view(o, 2 * C).rearrange("p (m n) -> p m n", m=CC)
        u = view(o + 2 * C, 2 * C).rearrange("p (i c) -> p i c", i=2)
        x1 = view(o + 4 * C, 2 * C).rearrange("p (i c) -> p i c", i=2)
        x1T = view(o + 6 * C, 2 * C).rearrange("p (i c n) -> p i c n", i=2, c=CC)
        hs = view(o + 8 * C, 2 * C).rearrange("p (m n) -> p m n", m=CC)
        u2 = view(o + 10 * C + 2 * HEADS, 2 * C).rearrange("p (i c) -> p i c", i=2)
        z = view(o + 10 * C, 2 * HEADS).rearrange("p (i h) -> p i h", i=2)
        assert o + 12 * C + 2 * HEADS <= ARENA
        ew_sets = []
        rows = view(0, 2 * LG * ROW).rearrange("p (s j c) -> p s j c", s=2, j=LG)
        o = 2 * LG * ROW
        xfT = view(o, LG * C).rearrange("p (j c n) -> p j c n", j=LG, c=CC)
        o += LG * C
        lg = view(o, LG * X).rearrange("p (j e) -> p j e", j=LG)
        mx = view(o + 40, LG * 8).rearrange("p (j e) -> p j e", j=LG)
        oh1 = view(o + 80, LG * X).rearrange("p (j e) -> p j e", j=LG)
        oh2 = view(o + 120, LG * X).rearrange("p (j e) -> p j e", j=LG)
        both = view(o + 160, LG * X).rearrange("p (j e) -> p j e", j=LG)
        before = view(o + 200, (LG + 1) * X).rearrange("p (j e) -> p j e", j=LG + 1)
        place = view(o + 248, LG * X).rearrange("p (j e) -> p j e", j=LG)
        pick = view(o + 288, LG * X).rearrange("p (j e) -> p j e", j=LG)
        gap = view(o + 328, LG)
        ex = view(o + 333, LG)
        den = view(o + 338, LG)
        slotf = view(o + 344, 2 * LG).rearrange("p (s j) -> p s j", s=2)
        countf = view(o + 354, X)
        o += 368
        ix = sb("ix", [P, LG, 8], U32)
        sloti = sb("sloti", [P, 2, 2, LG], I32)
        counti = sb("counti", [P, X], I32)
        tilesi = sb("tilesi", [P, X], I32)
        toki = sb("toki", [P, 1], I32)
        meta = view(o, ROW - C)
        o += ROW - C
        xin = view(o, ROW)
        xeT = view(o + ROW, C).rearrange("p (c n) -> p c n", c=CC)
        h = view(o + ROW + C, MC * P).rearrange("p (m n) -> p m n", m=MC)
        yt = view(o + ROW + C + MC * P, C)
        yo = view(o + ROW + 2 * C + MC * P, C)
        same = view(o + ROW + 3 * C + MC * P, 2)
        wsel = view(o + ROW + 3 * C + MC * P + 4, 3)
        o += ROW + 3 * C + MC * P + 8
        assert o <= ARENA
        xn_flat = xn[:, :, :].rearrange("p t c -> p (t c)")
        xnT_flat = xnT[:, :, :, :].rearrange("p t c n -> p (t c n)")
        for flat in (xn_flat, xnT_flat):
            ew_sets.append((flat[:, 0:CC * HID].rearrange("p (c h) -> p c h", c=CC),
                            flat[:, CC * HID:CC * HID + MC * C].rearrange("p (m f) -> p m f", m=MC)))

        pg = pb("pg", [P, 4, 512])
        p4 = pb("p4", [P, 512])
        p5 = pb("p5", [P, 512])
        p6 = pb("p6", [P, 512])
        p7 = pb("p7", [P, 512])

        hbank = [pg[:, 0, :], pg[:, 1, :], pg[:, 3, :], p5[:, :]]

        x_first, x_rest = sem("x_first"), sem("x_rest")
        msg_w_loaded, const_loaded, edges_loaded = sem("msg_w_loaded"), sem("const_loaded"), sem("edges_loaded")
        ranges_stored, ranges_loaded = sem("ranges_stored"), sem("ranges_loaded")
        iota_ready, idx_ready, ranges_ready, zeros_ready = (sem("iota_ready"), sem("idx_ready"),
                                                            sem("ranges_ready"), sem("zeros_ready"))
        dve_a = sem("dve_a")
        xs_ready, xs_turned, xT_kept, xT_ready = sem("xs_ready"), sem("xs_turned"), sem("xT_kept"), sem("xT_ready")
        xn_kept, bias_added = sem("xn_kept"), sem("bias_added")
        y0_made, y1_made, y0_kept, y1_kept = sem("y0_made"), sem("y1_made"), sem("y0_kept"), sem("y1_kept")
        y_stored = [sem(f"y_stored{j}") for j in range(LG)]
        gathered = [sem(f"gathered{s}") for s in range(SLOTS)]
        group_used = [sem(f"group_used{s}") for s in range(SLOTS)]
        onehot_ready, onehot_used, pair_done, pair_added = (sem("onehot_ready"), sem("onehot_used"),
                                                            sem("pair_done"), sem("pair_added"))
        kvx_ready, kv_made, ek_ready, v_ready, k_ready, kv_summed = (
            sem("kvx_ready"), sem("kv_made"), sem("ek_ready"), sem("v_ready"), sem("k_ready"), sem("kv_summed"))
        kvr_ready = sem("kvr_ready")
        q_made, eq_ready, q_ready, t_made = sem("q_made"), sem("eq_ready"), sem("q_ready"), sem("t_made")
        dve_c, x1_ready, x1_turned, x1T_ready = sem("dve_c"), sem("x1_ready"), sem("x1_turned"), sem("x1T_ready")
        h_made, h_ready, y_made, mix_done = sem("h_made"), sem("h_ready"), sem("y_made"), sem("mix_done")
        out_started, dve_d, rows_ready, rows_turned, rowsT_ready = (
            sem("out_started"), sem("dve_d"), sem("rows_ready"), sem("rows_turned"), sem("rowsT_ready"))
        logits_made, gap_ready, ex_ready, both_ready, rank_made, slots_ready = (
            sem("logits_made"), sem("gap_ready"), sem("ex_ready"), sem("both_ready"), sem("rank_made"),
            sem("slots_ready"))
        rows_sent = [sem(f"rows_sent{s}") for s in range(2)]
        total_ready, total_made, counts_ready, pads_sent = (sem("total_ready"), sem("total_made"),
                                                            sem("counts_ready"), sem("pads_sent"))
        weights_loaded = [sem(f"weights_loaded{s}") for s in range(2)]
        weights_used = [sem(f"weights_used{s}") for s in range(2)]
        tile_loaded, tile_turned, tileT_ready, meta_ready = (
            sem("tile_loaded"), sem("tile_turned"), sem("tileT_ready"), sem("meta_ready"))
        up_made, act_ready, down_made, dve_m, result_ready, added = (
            sem("up_made"), sem("act_ready"), sem("down_made"), sem("dve_m"), sem("result_ready"), sem("added"))
        var_ready, rs_ready, minus_ready = sem("var_ready"), sem("rs_ready"), sem("minus_ready")
        tile_added = sem("tile_added")
        rk_ready, rq_ready = sem("rk_ready"), sem("rq_ready")
        stats1, stats2, stats3, dev1, dev2, dev3 = (sem(x) for x in ("stats1", "stats2", "stats3", "dev1", "dev2", "dev3"))
        dve_s = sem("dve_s")
        dve_e, dve_f, dve_g = sem("dve_e"), sem("dve_f"), sem("dve_g")
        dve_r, dstf_ready, idx_staged, total_done, dve_d0 = (
            sem("dve_r"), sem("dstf_ready"), sem("idx_staged"), sem("total_done"), sem("dve_d0"))

        waited = {e.engine: sem(f"waited{n}") for n, e in enumerate((nc.sync, nc.gpsimd, nc.tensor, nc.vector))}

        ONE = 1

        def alone(eng):
            eng.sem_inc(waited[eng.engine], 1)

        class Chain:

            def __init__(self, eng, s, base=0):
                self.eng, self.s, self.base, self.n = eng, s, base, 0

            def step(self, ins):
                self.n += 1
                ins.then_inc(self.s, 1)

            def wait(self, apart=False):
                self.eng.wait_ge(self.s, self.base + self.n)
                if apart:
                    alone(self.eng)

            def link(self, ins, apart=False):
                self.step(ins)
                self.wait(apart)

        A_STEPS = 2 * LG
        C_STEPS = 2 + 1 + 2 + 1 + 2
        E_STEPS = 3
        F_STEPS = 1 + 2
        D_STEPS = 1 + 17 + 3 * LG

        block = ctx.enter_context(nc.Block())

        @block.sync
        def _(sp):
            x_v = a["x"].rearrange("(t p) c -> p t c", p=P)
            sp.dma_start(acc[:, 0:LG, :], x_v[:, 0:LG, :]).then_inc(x_first, 16)
            sp.dma_start(wblk, a["wblk"]).then_inc(msg_w_loaded, 16)
            sp.dma_start(ident[:, :], a["ident"]).then_inc(msg_w_loaded, 16)
            for g in range(1, NT // LG):
                sp.dma_start(acc[:, g * LG:(g + 1) * LG, :], x_v[:, g * LG:(g + 1) * LG, :]).then_inc(x_rest, 16)
            for dst, name in ((vecs, "vecs"), (b1T, "b1T"), (wqT, "wqT"), (wkvT, "wkvT"), (w1T, "w1T"),
                              (w2T, "w2T"), (wg, "wg"), (bg, "bg"), (eb1T, "eb1T"), (eb2, "eb2"), (capcol, "capcol"),
                              (iota8, "iota8"), (padrows, "padrows"), (upper, "upper"), (ones, "ones"),
                              (blockmask, "blockmask"), (nodemask, "nodemask")):
                sp.dma_start(dst[tuple(slice(None) for _ in a[name].shape)], a[name]).then_inc(const_loaded, 16)
            y_v = y_dram.rearrange("(t p r) c -> t p r c", p=P, r=R)

            def store_y(t, j):
                sp.wait_ge(y0_kept, t + (1 + ONE))
                sp.wait_ge(y1_kept, t + (1 + ONE))
                sp.dma_start(y_v[bass.ds(t, 1)].rearrange("o p r c -> (o p) r c"), ys[:, j, :, :])\
                  .then_inc(y_stored[j], 16)
            with sp.Fori(0, NT // LG) as g:
                for j in range(LG):
                    store_y(g * LG + j, j)
            out_v = out.rearrange("(t p) c -> p t c", p=P)
            sp.wait_ge(const_loaded, 16 * 17)
            sp.dma_start(out[NP:NP + P, :], padrows[:, 0:C]).then_inc(out_started, 16)
            sp.wait_ge(kvr_ready, 1)
            sp.wait_ge(mix_done, NT)
            sp.wait_ge(total_ready, 1)
            sp.dma_start(out_v[:, 0:NT, :], acc[:, :, :]).then_inc(out_started, 16)
            sp.wait_ge(counts_ready, 2)
            for e in range(X):
                n = sp.value_load(counti[0:1, e:e + 1], min_val=0, max_val=NP)
                sp.dma_start(slot_dram[bass.ds(n + e * CAP, P), :], padrows[:, :]).then_inc(pads_sent, 16)
            sp.wait_ge(pads_sent, 16 * X)
            sp.wait_ge(rows_sent[0], 16 * 2 * LG * 3)
            sp.wait_ge(rows_sent[1], 16 * 2 * LG * 2)
            k = sp.alloc_register("sp_tile")
            sp.reg_mov(k, 0)

            def load_tile(row, n):
                sp.wait_ge(tile_turned, n + ONE)
                sp.wait_ge(meta_ready, n + ONE)
                sp.dma_start(xin, slot_dram[bass.ds(row, P), :]).then_inc(tile_loaded, 16)
                sp.wait_ge(tile_loaded, 16 * n + 16)
                alone(sp)
            cnt = sp.alloc_register("sp_count")
            with sp.Fori(0, X) as e:
                sp.load(cnt, tilesi[0:1, bass.ds(e, 1)])
                with sp.Fori(0, sp.snap(cnt, min_val=1, max_val=NT)) as i:
                    n = sp.snap(k, min_val=0, max_val=X * NT)
                    load_tile(e * CAP + i * P, n)
                    sp.reg_add(k, k, 1)
            load_tile(0, sp.snap(k, min_val=0, max_val=X * NT))

        @block.gpsimd
        def _(pool):
            for counted_from_one in (tile_added,):
                pool.sem_inc(counted_from_one, ONE)

            def deviation(i, w):
                pool.wait_ge(var_ready, i + 1)
                pool.tensor_tensor(rs[:, 0:w], var[:, 0:w], minus_half[:, 0:w], ALU.pow).then_inc(rs_ready, 1)

            def keep(t, j):
                pool.wait_ge(xs_ready, t + 1)
                pool.tensor_copy(xn[:, bass.ds(t, 1), :], xs[:, bass.ds(j, 1), :]).then_inc(xn_kept, 1)
                pool.tensor_tensor(acc[:, bass.ds(t, 1), :], acc[:, bass.ds(t, 1), :], vecs[:, 4:5, :],
                                   ALU.add).then_inc(bias_added, 1)
            pool.memset(minus_half[:, :], -0.5).then_inc(minus_ready, 1)
            pool.wait_ge(minus_ready, 1)
            deviation(0, LG)
            deviation(1, LG)
            pool.iota(iota[:, :], pattern=[[1, NP]], base=0, channel_multiplier=0,
                      allow_small_or_imprecise_dtypes=True).then_inc(iota_ready, 1)
            pool.iota(tokid[:, :], pattern=[[P, NT]], base=0, channel_multiplier=1,
                      allow_small_or_imprecise_dtypes=True).then_inc(iota_ready, 1)
            pool.wait_ge(ranges_ready, 1)
            pool.dma_start(range_dram, rng3[:, :]).then_inc(ranges_stored, 16)
            pool.wait_ge(ranges_stored, 16)
            pool.dma_start(ranges[:, :], range_dram.rearrange("(o g) k -> o (g k)", o=1)).then_inc(ranges_loaded, 16)
            pool.wait_ge(const_loaded, 16 * 17)
            with pool.Fori(0, NT // LG - 2) as g:
                for j in range(LG):
                    keep(g * LG + j, (g % 2) * LG + j)
                deviation(g + 2, LG)
            with pool.Fori(NT // LG - 2, NT // LG) as g:
                for j in range(LG):
                    keep(g * LG + j, (g % 2) * LG + j)
            for j in range(LG):
                pool.wait_ge(y_stored[j], 16 * (NT // LG))
            pool.wait_ge(xn_kept, NT)
            pool.wait_ge(bias_added, NT)
            pool.wait_ge(idx_ready, 1)

            def stage(r, par):
                pool.tensor_copy(gidx[:, par, :], idx[:, bass.ds(r * (SLOTS * GT), SLOTS * GT)])\
                    .then_inc(idx_staged, 1)

            def gather(par, s):
                for j in range(GT):
                    c = s * GT + j
                    pool.indirect_dma_start(
                        out=ring[:, s, j, :], out_offset=None, in_=y_dram[:, :],
                        in_offset=bass.IndirectOffsetOnAxis(ap=gidx[:, par, c:c + 1], axis=0))\
                        .then_inc(gathered[s], 16)

            def gather_round(r, par, groups=SLOTS):
                pool.wait_ge(idx_staged, r + 1)
                for s in range(groups):
                    pool.wait_ge(group_used[s], r + (1 if s == SLOTS - 1 else 0))
                    if s == SLOTS - 1:
                        stage(r + 1, 1 - par)
                    else:
                        alone(pool)
                    gather(par, s)
            stage(0, 0)
            stage(1, 1)
            pool.wait_ge(idx_staged, 2)
            for s in range(SLOTS):
                gather(0, s)
            gather_round(1, 1)
            with pool.Fori(1, ROUNDS // 2) as k:
                gather_round(k * 2, 0)
                gather_round(k * 2 + 1, 1)
            gather_round(ROUNDS, 0, TAIL)

            def dispatch(g, s):
                pool.wait_ge(slots_ready, g + 1)
                alone(pool)
                for c in range(2):
                    for j in range(LG):
                        pool.indirect_dma_start(
                            out=slot_dram[:, :],
                            out_offset=bass.IndirectOffsetOnAxis(ap=sloti[:, s, c, j:j + 1], axis=0),
                            in_=rows[:, s, j, :], in_offset=None).then_inc(rows_sent[s], 16)
            with pool.Fori(0, NT // LG // 2) as k:
                dispatch(k * 2, 0)
                dispatch(k * 2 + 1, 1)
            dispatch(NT // LG - 1, 0)
            pool.wait_ge(out_started, 32)
            k = pool.alloc_register("pool_tile")
            pool.reg_mov(k, 0)
            cnt = pool.alloc_register("pool_count")
            pool.wait_ge(counts_ready, 2)
            with pool.Fori(0, X) as e:
                pool.load(cnt, tilesi[0:1, bass.ds(e, 1)])
                with pool.Fori(0, pool.snap(cnt, min_val=1, max_val=NT)) as i:
                    n = pool.snap(k, min_val=0, max_val=X * NT)
                    pool.wait_ge(result_ready, n + (1 + ONE))
                    alone(pool)
                    pool.indirect_dma_start(
                        out=out[:, :], out_offset=bass.IndirectOffsetOnAxis(ap=toki[:, 0:1], axis=0),
                        in_=yo, in_offset=None, compute_op=ALU.add).then_inc(added, 16)
                    pool.wait_ge(added, 16 * n + 16)
                    pool.sem_inc(tile_added, 1)
                    pool.reg_add(k, k, 1)

        @block.scalar
        def _(act):
            act.dma_start(dstrow[:, :], a["dstrow"]).then_inc(edges_loaded, 16)
            for dst, name in ((srcT, "srcT"), (relT, "relT"), (dstT, "dstT"), (ew, "ewT")):
                act.dma_start(dst[:, :], a[name]).then_inc(edges_loaded, 16)
            for counted_from_one in (xT_kept, xT_ready, y0_kept, v_ready, eq_ready, rowsT_ready, act_ready):
                act.sem_inc(counted_from_one, ONE)
            act.wait_ge(const_loaded, 16 * 17)

            def message(g, j, first=False):
                t = g * LG + j
                act.wait_ge(xs_turned, t + 1)
                if not first:
                    act.wait_ge(y1_made, t - (LG - 1))
                act.activation(xTs[:, j], p4[:, 0:C].rearrange("p (c n) -> p c n", c=CC), ACT.Copy)\
                   .then_inc(xT_ready, 1)
                act.activation(xnT[:, bass.ds(t, 1)].rearrange("p o c n -> p (o c n)"), p4[:, 0:C], ACT.Copy)\
                   .then_inc(xT_kept, 1)
                act.wait_ge(y0_made, t + 1)
                if not first:
                    act.wait_ge(y_stored[j], g * 16)
                act.activation(ys[:, j, :, 0:P], pg[:, 0:2, :].rearrange("p b (r o) -> p (b r) o", o=P),
                               ACT.Copy).then_inc(y0_kept, 1)
            for j in range(LG):
                message(0, j, True)
            with act.Fori(1, NT // LG) as g:
                for j in range(LG):
                    message(g, j)

            act.wait_ge(zeros_ready, 2)

            def keys(t):
                act.wait_ge(kv_made, t + ONE)
                act.activation(kvx, xnT[:, bass.ds(t, 1)].rearrange("p o c n -> p (o c) n"), ACT.Copy)\
                   .then_inc(kvx_ready, 1)
                act.wait_ge(kv_made, t + (1 + ONE))
                act.wait_ge(k_ready, t + ONE)
                act.activation(ek[:, 0:C], p5[:, 0:C], ACT.Relu, scale=-1.0).then_inc(rk_ready, 1)
                act.wait_ge(rk_ready, t + 1)
                act.activation(ek[:, 0:C], ek[:, 0:C], ACT.Exp, scale=-1.0).then_inc(ek_ready, 1)
                act.wait_ge(kv_summed, t + ONE)
                act.activation(vs, p5[:, C:2 * C], ACT.Copy).then_inc(v_ready, 1)
            act.wait_ge(xT_kept, NT + ONE)
            for j in range(LG):
                act.wait_ge(y_stored[j], 16 * (NT // LG))
            with act.Fori(0, NT) as t:
                keys(t)

            def two(v, w):
                return v.rearrange("p (m n) -> p m n", m=CC)[:, :, 0:w]

            def deviation(stats, seen, var, sd, made):
                act.wait_ge(stats, seen)
                act.activation(sd, var, ACT.Sqrt, bias=eps[:, :]).then_inc(made, 1)

            def mix_q(i, n):
                w = n * P
                act.wait_ge(q_made, i + 1)
                act.wait_ge(q_ready, i + ONE)
                act.activation(two(ek, w), two(p4[:, :], w), ACT.Relu, scale=-1.0).then_inc(rq_ready, 1)
                act.wait_ge(rq_ready, i + 1)
                act.activation(two(ek, w), two(ek, w), ACT.Exp, scale=-1.0).then_inc(eq_ready, 1)

            def mix_hidden(i, n):
                w = n * P
                act.wait_ge(x1_turned, i + 1)
                act.wait_ge(h_made, i + ONE)
                act.activation(x1T[:, 0:n].rearrange("p i c n -> p (i c n)"), p5[:, 0:n * C], ACT.Copy)\
                   .then_inc(x1T_ready, 1)
                act.wait_ge(h_made, i + (1 + ONE))
                act.wait_ge(y_made, i + ONE)
                for m in range(CC):
                    act.activation(hs[:, m, 0:w], p7[:, m * 2 * P:m * 2 * P + w], ACT.Gelu, bias=b1T[:, m:m + 1])\
                       .then_inc(h_ready, 1)

            def mix(i, n, before=2):
                mix_q(i, n)
                deviation(stats1, i * 2 + n, mv[:, 0:n, 1], rs[:, 0:n], dev1)
                if before:
                    deviation(stats2, i * 2, mv2[:, 0:2, 1], rs2[:, 0:2], dev2)
                mix_hidden(i, n)
            act.wait_ge(kvr_ready, 1)
            mix(0, 2, before=0)
            with act.Fori(1, NT // 2) as i:
                mix(i, 2)
            mix(NT // 2, 1)
            deviation(stats2, NT, mv2[:, 0:1, 1], rs2[:, 0:1], dev2)

            def load_weights(e, s):
                w1, w2 = ew_sets[s]
                act.dma_start(w1, a["ew1"][bass.ds(e, 1)].rearrange("o p c h -> (o p) c h")).then_inc(weights_loaded[s], 16)
                act.dma_start(w2, a["ew2"][bass.ds(e, 1)].rearrange("o p m f -> (o p) m f")).then_inc(weights_loaded[s], 16)

            def turned(g):
                act.wait_ge(rows_turned, g + 1)
                act.wait_ge(logits_made, g + ONE)
                for v, bank in ((xfT[:, 0:2], p5[:, :]), (xfT[:, 2:4], p4[:, :]), (xfT[:, 4:5], pg[:, 3, 0:C])):
                    act.activation(v.rearrange("p j c n -> p (j c n)"), bank, ACT.Copy).then_inc(rowsT_ready, 1)

            load_weights(0, 0)
            load_weights(1, 1)

            def gate(g):
                act.wait_ge(gap_ready, g + (1 + ONE))
                act.activation(ex, gap, ACT.Exp).then_inc(ex_ready, 1)
            deviation(stats3, LG, mv[:, :, 1], rs[:, :], dev3)
            for g in range(NT // LG):
                turned(g)
                if g + 1 < NT // LG:
                    deviation(stats3, LG * (g + 2), mv[:, :, 1], rs[:, :], dev3)
                gate(g)

            k = act.alloc_register("act_tile")
            act.reg_mov(k, 0)
            cnt = act.alloc_register("act_count")
            act.wait_ge(counts_ready, 2)

            def expert(e):
                act.load(cnt, tilesi[0:1, bass.ds(e, 1)])
                with act.Fori(0, act.snap(cnt, min_val=1, max_val=NT)):
                    n = act.snap(k, min_val=0, max_val=X * NT)
                    act.wait_ge(down_made, n + ONE)
                    for m in range(MC):
                        act.wait_ge(up_made, n * MC + (m + 1))
                        act.activation(h[:, m, :], hbank[m % 4][:, m // 4 * P:m // 4 * P + P], ACT.Gelu,
                                       bias=eb1T[:, bass.ds(e, 1), m:m + 1].rearrange("p a b -> p (a b)"))\
                           .then_inc(act_ready, 1)
                    act.reg_add(k, k, 1)
            with act.Fori(0, X // 2 - 1) as visit:
                for s in range(2):
                    expert(visit * 2 + s)
                    act.wait_ge(weights_used[s], visit + 1)
                    load_weights(visit * 2 + (2 + s), s)
            for s in range(2):
                expert(X - 2 + s)

        @block.tensor
        def _(pe):
            for counted_from_one in (kv_made, kv_summed, h_made, y_made, logits_made, down_made, tile_turned):
                pe.sem_inc(counted_from_one, ONE)
            pe.wait_ge(msg_w_loaded, 32)

            def message(t, j):
                pe.wait_ge(xs_ready, t + 1)
                pe.wait_ge(xT_kept, t + ONE)
                pe.wait_ge(xT_ready, t + ONE)
                for c in range(CC):
                    last = pe.transpose(p4[:, c * P:(c + 1) * P], xs[:, j, c * P:(c + 1) * P], ident[:, :])
                last.then_inc(xs_turned, 1)
                pe.wait_ge(xT_ready, t + (1 + ONE))
                for c, kept, made in ((0, y0_kept, y0_made), (1, y1_kept, y1_made)):
                    pe.wait_ge(kept, t + ONE)
                    for b in range(2):
                        last = pe.matmul(pg[:, 2 * c + b, :], xTs[:, j % LG, c, :],
                                         wblk[:, c, b * 4:b * 4 + 4, :].rearrange("p r o -> p (r o)"),
                                         start=True, stop=True)
                    last.then_inc(made, 1)
            with pe.Fori(0, NT // LG // 2) as k:
                for j in range(2 * LG):
                    message(k * (2 * LG) + j, j)
            for j in range(LG):
                message(NT - LG + j, j)

            pe.wait_ge(const_loaded, 16 * 17)
            pe.wait_ge(zeros_ready, 2)
            pe.wait_ge(y0_kept, NT + ONE)
            pe.wait_ge(y1_kept, NT + ONE)

            def keys_made(t):
                pe.wait_ge(kvx_ready, t + 1)
                pe.wait_ge(k_ready, t + ONE)
                pe.wait_ge(v_ready, t + ONE)
                for c in range(CC):
                    last = pe.matmul(p5[:, :], kvx[:, c, :], wkvT[:, c, :], start=(c == 0), stop=(c == CC - 1))
                last.then_inc(kv_made, 1)

            def keys_summed(t):
                pe.wait_ge(k_ready, t + (1 + ONE))
                pe.wait_ge(v_ready, t + (1 + ONE))
                for c in range(CC):
                    pe.matmul(p6[:, c * KW:c * KW + P], ks[:, c * P:(c + 1) * P], vs[:, c * P:(c + 1) * P],
                              start=False, stop=False, skip_group_check=True)
                    last = pe.matmul(p6[:, c * KW + P:c * KW + P + 1], ks[:, c * P:(c + 1) * P],
                                     nodemask[:, bass.ds(t, 1)], start=False, stop=False, skip_group_check=True)
                last.then_inc(kv_summed, 1)
            pe.matmul(p6[:, 0:C], zeros[:, 0:P], zeros[:, :], start=True, stop=False, skip_group_check=True)
            pe.matmul(p6[:, C:2 * C], zeros[:, 0:P], zeros[:, :], start=False, stop=False, skip_group_check=True)

            def mix_q(i, n):
                w = n * P
                pe.wait_ge(eq_ready, i + ONE)
                pe.wait_ge(q_ready, i + ONE)
                for m in range(CC):
                    for c in range(CC):
                        last = pe.matmul(p4[:, m * 2 * P:m * 2 * P + w], wqT[:, c, m * P:(m + 1) * P],
                                         xnT[:, bass.ds(2 * i, n), c, :], start=(c == 0), stop=(c == CC - 1))
                last.then_inc(q_made, 1)

            def mix_t(i, n):
                pe.wait_ge(q_ready, i + (1 + ONE))
                for k in range(n):
                    for m in range(CC):
                        last = pe.matmul(pg[:, 2 + k, m * KW:(m + 1) * KW], qs[:, m, k * P:(k + 1) * P],
                                         kvr[:, m, :], start=True, stop=True)
                last.then_inc(t_made, 1)

            def mix_turn(i, n):
                pe.wait_ge(x1_ready, 2 * i + n)
                for k in range(n):
                    for c in range(CC):
                        last = pe.transpose(p5[:, (k * CC + c) * P:(k * CC + c + 1) * P],
                                            x1[:, k, c * P:(c + 1) * P], ident[:, :])
                last.then_inc(x1_turned, 1)

            def mix_hidden(i, n):
                w = n * P
                pe.wait_ge(x1T_ready, i + 1)
                for m in range(CC):
                    for c in range(CC):
                        last = pe.matmul(p7[:, m * 2 * P:m * 2 * P + w], w1T[:, c, m * P:(m + 1) * P],
                                         x1T[:, 0:n, c, :], start=(c == 0), stop=(c == CC - 1))
                last.then_inc(h_made, 1)

            def mix_y(i, n):
                pe.wait_ge(h_ready, CC * (i + 1) if isinstance(i, int) else i * CC + CC)
                for k in range(n):
                    for m in range(CC):
                        pe.matmul(p6[:, k * C:(k + 1) * C], hs[:, m, k * P:(k + 1) * P], w2T[:, m, :],
                                  start=(m == 0), stop=False)
                    last = pe.matmul(p6[:, k * C:(k + 1) * C], ones[0:1, :], vecs[0:1, 2, :], start=False, stop=True)
                last.then_inc(y_made, 1)

            for j in range(GT - 1):
                pe.matmul(p7[:, 0:C], zeros[:, 0:P], zeros[:, :], start=True, stop=True).then_inc(onehot_used, 1)
            pe.matmul(pg[:, 1, 0:C], zeros[:, 0:P], zeros[:, :], start=True, stop=True).then_inc(pair_done, 1)
            pair = pe.alloc_register("pe_pair")
            pe.reg_mov(pair, 0)
            lo, hi = pe.alloc_register("pe_lo"), pe.alloc_register("pe_hi")
            pe.wait_ge(ranges_loaded, 16)

            def edges(r, s):
                pe.load([lo, hi], ranges[0:1, bass.ds(r * (2 * SLOTS) + 2 * s, 2)])
                pe.wait_ge(gathered[s], r * (16 * GT) + 16 * GT)
                alone(pe)
                with pe.Fori(pe.snap(lo, min_val=0, max_val=NT - 1), pe.snap(hi, min_val=1, max_val=NT)):
                    p = pe.snap(pair, min_val=0, max_val=NG * NT)
                    pe.wait_ge(pair_added, p + ONE)
                    for j in range(GT):
                        pe.wait_ge(onehot_ready, p * GT + (j + 1))
                        mm = pe.matmul(pg[:, bass.ds(p % 2, 1), 0:C], oh[:, j, :], ring[:, s, j, :],
                                       start=(j == 0), stop=(j == GT - 1))
                        if j < GT - 1:
                            mm.then_inc(onehot_used, 1)
                    mm.then_inc(pair_done, 1)
                    pe.reg_add(pair, pair, 1)

            with pe.Fori(0, KEY_ROUNDS) as r:
                for s in range(SLOTS):
                    keys_made(r * SLOTS + s)
                    edges(r, s)
                    keys_summed(r * SLOTS + s)
            keys_made(NT - 1)
            keys_summed(NT - 1)
            pe.wait_ge(kvr_ready, 1)

            def mix_round(i, r, n, before, groups=SLOTS):
                mix_q(i, n)
                edges(r, 0)
                mix_t(i, n)
                edges(r, 1)
                if before:
                    mix_y(i - 1, 2)
                for s in range(2, min(groups, SLOTS - 1)):
                    edges(r, s)
                mix_turn(i, n)
                if groups == SLOTS:
                    edges(r, SLOTS - 1)
                mix_hidden(i, n)
            mix_round(0, KEY_ROUNDS, 2, False)
            with pe.Fori(1, NT // 2) as i:
                mix_round(i, i + KEY_ROUNDS, 2, True)
            mix_round(NT // 2, ROUNDS, 1, True, TAIL)
            mix_y(NT // 2, 1)

            def dispatch(g, s):
                pe.wait_ge(rows_ready, LG * (g + 1))
                pe.wait_ge(rowsT_ready, 3 * g + ONE)
                for j in range(LG):
                    bank = (p5[:, :], p4[:, :], pg[:, 3, :])[j // 2]
                    for c in range(CC):
                        q = j % 2 * C + c * P
                        last = pe.transpose(bank[:, q:q + P], rows[:, s, j, c * P:(c + 1) * P], ident[:, :])
                last.then_inc(rows_turned, 1)
                pe.wait_ge(rowsT_ready, 3 * g + (3 + ONE))
                pe.wait_ge(gap_ready, g + ONE)
                for j in range(LG):
                    for c in range(CC):
                        last = pe.matmul(p6[:, j * X:(j + 1) * X], xfT[:, j, c, :], wg[:, c, :],
                                         start=(c == 0), stop=(c == CC - 1))
                last.then_inc(logits_made, 1)
                pe.wait_ge(both_ready, g + 1)
                pe.matmul(p7[:, 0:LG * X], upper[:, :], both.rearrange("p j e -> p (j e)"), start=True, stop=False)
                pe.matmul(p7[:, 0:LG * X], ones[:, :], before[:, 0:LG, :].rearrange("p j e -> p (j e)"),
                          start=False, stop=True).then_inc(rank_made, 1)
            for g in range(NT // LG):
                dispatch(g, g % 2)
            pe.wait_ge(total_made, 1)
            pe.matmul(p7[:, 0:X], ones[:, :], before[:, LG, :], start=True, stop=True).then_inc(total_done, 1)

            def turn(n):
                pe.wait_ge(tile_loaded, 16 * n + 16)
                pe.wait_ge(tileT_ready, n)
                for c in range(CC):
                    last = pe.transpose(p4[:, c * P:(c + 1) * P], xin[:, c * P:(c + 1) * P], ident[:, :])
                last.then_inc(tile_turned, 1)
            k = pe.alloc_register("pe_tile")
            pe.reg_mov(k, 0)
            cnt = pe.alloc_register("pe_count")
            pe.wait_ge(counts_ready, 2)
            turn(0)

            def expert(e, s, visit):
                w1, w2 = ew_sets[s]
                pe.load(cnt, tilesi[0:1, bass.ds(e, 1)])
                pe.wait_ge(weights_loaded[s], 32 * visit + 32)
                alone(pe)
                with pe.Fori(0, pe.snap(cnt, min_val=1, max_val=NT)):
                    n = pe.snap(k, min_val=0, max_val=X * NT)
                    pe.wait_ge(tileT_ready, n + 1)
                    pe.wait_ge(act_ready, n * MC + ONE)
                    for m in range(MC):
                        if m >= 4:
                            pe.wait_ge(act_ready, n * MC + (m - 3 + ONE))
                        for c in range(CC):
                            mm = pe.matmul(hbank[m % 4][:, m // 4 * P:m // 4 * P + P], w1[:, c, m * P:(m + 1) * P],
                                           xeT[:, c, :], start=(c == 0), stop=(c == CC - 1))
                        mm.then_inc(up_made, 1)
                    turn(n + 1)
                    pe.wait_ge(result_ready, n + ONE)
                    for m in range(MC):
                        pe.wait_ge(act_ready, n * MC + (m + 1 + ONE))
                        mm = pe.matmul(pg[:, 2, 0:C], h[:, m, :], w2[:, m, :], start=(m == 0), stop=(m == MC - 1))
                    mm.then_inc(down_made, 1)
                    pe.reg_add(k, k, 1)
                pe.matmul(p7[:, 0:1], zeros[:, 0:P], zeros[:, 0:1], start=True, stop=True).then_inc(weights_used[s], 1)
            with pe.Fori(0, X // 2) as visit:
                expert(visit * 2, 0, visit)
                expert(visit * 2 + 1, 1, visit)

        @block.vector
        def _(dve):
            for counted_from_one in (y1_kept, k_ready, q_ready, gap_ready, pair_added, meta_ready, result_ready):
                dve.sem_inc(counted_from_one, ONE)
            dve.memset(zeros[:, :], 0.0).then_inc(zeros_ready, 1)
            dve.memset(eps[:, :], EPS_LN).then_inc(zeros_ready, 1)

            def norm_stats(ch, tiles, w, count):
                for j in range(w):
                    ch.step(dve.bn_stats(st[:, j, :], tiles(j)))
                ch.wait(apart=True)
                for j in range(w):
                    ch.step(dve.bn_aggr(mv[:, j, :], st[:, j, :]))
                ch.wait()
                dve.tensor_scalar(var[:, 0:w], mv[:, 0:w, 1], EPS_LN, None, ALU.add).then_inc(var_ready, 1)
                dve.wait_ge(rs_ready, count)

            def stats(ch, tiles, w, st, mv, done):
                for j in range(w):
                    ch.step(dve.bn_stats(st[:, j, :], tiles(j)))
                ch.wait(apart=True)
                for j in range(w):
                    dve.bn_aggr(mv[:, j, :], st[:, j, :]).then_inc(done, 1)

            def evict(g, j):
                dve.wait_ge(y1_made, g * LG + (j + 1))
                if not isinstance(g, int):
                    dve.wait_ge(y_stored[j], g * 16)
                dve.tensor_copy(ys[:, j, :, P:2 * P], pg[:, 2:4, :].rearrange("p b (r o) -> p (b r) o", o=P))\
                   .then_inc(y1_kept, 1)

            def normed(g, at):
                ch = Chain(dve, dve_a, g * A_STEPS)
                norm_stats(ch, lambda j: acc[:, bass.ds(g * LG + j, 1), :].rearrange("p o c -> p (o c)"), LG, g + 1)
                if not isinstance(g, int) or g >= 2:
                    dve.wait_ge(xs_turned, g * LG - LG)
                    dve.wait_ge(xn_kept, g * LG - LG)
                for j in range(LG):
                    dve.tensor_scalar(xs[:, bass.ds(at + j, 1), :].rearrange("p o c -> p (o c)"), acc[:, bass.ds(g * LG + j, 1), :].rearrange("p o c -> p (o c)"),
                                      mv[:, j, 0:1], rs[:, j:j + 1], ALU.subtract, ALU.mult).then_inc(xs_ready, 1)
                assert ch.n == A_STEPS
            dve.wait_ge(x_first, 16)
            normed(0, 0)
            dve.wait_ge(edges_loaded, 80)
            dve.scalar_tensor_tensor(idx[:, :], srcT[:, :], float(R), relT[:, :], ALU.mult, ALU.add)\
               .then_inc(idx_ready, 1)
            dve.tensor_copy(dstf[:, :], dstT[:, :]).then_inc(dstf_ready, 1)
            ch = Chain(dve, dve_r)
            ch.step(dve.tensor_reduce(rng2[:, 0:1], dstrow[:, :], AX_X, ALU.min))
            ch.link(dve.tensor_reduce(rng2[:, 1:2], dstrow[:, :], AX_X, ALU.max))
            ch.link(dve.tensor_scalar(rng3[:, :], rng2[:, :], P.bit_length() - 1, None, ALU.arith_shift_right))
            dve.tensor_scalar(rng3[:, 1:2], rng3[:, 1:2], 1.0, None, ALU.add).then_inc(ranges_ready, 1)
            dve.wait_ge(x_rest, 16 * (NT // LG - 1))

            normed(1, LG)
            for j in range(LG):
                evict(0, j)
            normed(2, 0)
            with dve.Fori(1, NT // LG - 2) as g:
                for j in range(LG):
                    evict(g, j)
                normed(g + 2, (g % 2) * LG)
            with dve.Fori(NT // LG - 2, NT // LG) as g:
                for j in range(LG):
                    evict(g, j)

            pair = dve.alloc_register("dve_pair")
            dve.reg_mov(pair, 0)
            last_tile = dve.alloc_register("dve_last_tile")
            dve.reg_mov(last_tile, 0)
            lo, hi = dve.alloc_register("dve_lo"), dve.alloc_register("dve_hi")
            dve.wait_ge(ranges_loaded, 16)
            dve.wait_ge(iota_ready, 2)
            dve.wait_ge(dstf_ready, 1)
            dve.wait_ge(bias_added, NT)
            dve.wait_ge(xn_kept, NT)

            def add_pair(p):
                t = dve.snap(last_tile, min_val=0, max_val=NT - 1)
                dve.wait_ge(pair_done, p + 1)
                dve.wait_ge(pair_added, p + ONE)
                row = acc[:, bass.ds(t, 1), :]
                dve.tensor_tensor(row, row, pg[:, bass.ds((p + 1) % 2, 1), 0:C], ALU.add).then_inc(pair_added, 1)

            def edges(r, s):
                dve.load([lo, hi], ranges[0:1, bass.ds(r * (2 * SLOTS) + 2 * s, 2)])
                with dve.Fori(dve.snap(lo, min_val=0, max_val=NT - 1), dve.snap(hi, min_val=1, max_val=NT)) as d:
                    p = dve.snap(pair, min_val=0, max_val=NG * NT)
                    for j in range(GT):
                        if j < GT - 1:
                            dve.wait_ge(onehot_used, p * (GT - 1) + (j + 1))
                        else:
                            dve.wait_ge(pair_done, p + 1)
                        col = r * (SLOTS * GT) + (s * GT + j)
                        dve.tensor_scalar(oh[:, j, :], iota[:, bass.ds(d * P, P)], dstf[:, bass.ds(col, 1)],
                                          ew[:, bass.ds(col, 1)], ALU.is_equal, ALU.mult)\
                           .then_inc(onehot_ready, 1)
                    add_pair(p)
                    dve.reg_mov(last_tile, d)
                    dve.reg_add(pair, pair, 1)
                dve.sem_inc(group_used[s - 1], 1)

            def keys(t):
                dve.wait_ge(ek_ready, t + 1)
                dve.wait_ge(kv_summed, t + ONE)
                dve.wait_ge(v_ready, t + (1 + ONE))
                dve.scalar_tensor_tensor(ks, p5[:, 0:C], 0.0, ek[:, 0:C], ALU.max, ALU.add).then_inc(k_ready, 1)
            with dve.Fori(0, KEY_ROUNDS) as r:
                for s in range(SLOTS):
                    edges(r, s)
                    keys(r * SLOTS + s)
            keys(NT - 1)
            dve.wait_ge(kv_summed, NT + ONE)
            for c in range(CC):
                dve.tensor_tensor(kvr[:, c, 0:P], p6[:, c * KW:c * KW + P], blockmask[:, 0:P], ALU.mult)\
                   .then_inc(dve_r, 1)
                dve.tensor_tensor(kvr[:, c, P:KW], blockmask[:, P:KW],
                                  p6[:, c * KW + P:c * KW + P + 1].to_broadcast([P, HC]), ALU.mult).then_inc(dve_r, 1)
            dve.wait_ge(dve_r, 3 + 2 * CC)
            alone(dve)
            dve.engine_nop().then_inc(kvr_ready, 1)

            def norm_apply(ch, src, n, mean, sd, gain):
                ch.step(dve.reciprocal(sd[:, 0:n], sd[:, 0:n]))
                for k in range(n):
                    ch.step(dve.scalar_tensor_tensor(src[:, k, :], src[:, k, :], mean[:, k, 0:1], vecs[:, gain, :],
                                                     ALU.subtract, ALU.mult))
                ch.wait()

            def two(v, w):
                return v.rearrange("p (m n) -> p m n", m=CC)[:, :, 0:w]

            def mix_q(i, n):
                w = n * P
                dve.wait_ge(eq_ready, i + (1 + ONE))
                dve.scalar_tensor_tensor(qs[:, :, 0:w], two(p4[:, :], w), 0.0, two(ek, w), ALU.max, ALU.add)\
                   .then_inc(q_ready, 1)

            def mix_t(i, n):
                ch = Chain(dve, dve_c, i * C_STEPS)
                dve.wait_ge(t_made, i + 1)
                tt = [pg[:, 2 + k, 0:CC * KW].rearrange("p (m k) -> p m k", m=CC) for k in range(n)]
                for k in range(n):
                    ch.step(dve.tensor_scalar(z[:, k, :].rearrange("p (m h) -> p m h", m=CC), tt[k][:, :, P:KW],
                                              EPS_ATTN, None, ALU.add))
                ch.wait()
                ch.link(dve.reciprocal(z[:, 0:n, :], z[:, 0:n, :]))
                for k in range(n):
                    zb = z[:, k, :].rearrange("p (m h) -> p m h", m=CC).unsqueeze(3).to_broadcast([P, CC, HC, HD])
                    ch.step(dve.tensor_tensor(u[:, k, :].rearrange("p (m h d) -> p m h d", m=CC, h=HC),
                                              tt[k][:, :, 0:P].rearrange("p m (h d) -> p m h d", h=HC), zb, ALU.mult))
                ch.wait()
                ch.link(dve.tensor_tensor(u[:, 0:n, :], u[:, 0:n, :], xn[:, bass.ds(2 * i, n), :], ALU.add))
                stats(ch, lambda j: u[:, j, :], n, st, mv, stats1)
                if n == 2:
                    assert ch.n == C_STEPS, ch.n

            def mix_x1(i, n):
                ch = Chain(dve, dve_e, i * E_STEPS)
                dve.wait_ge(dev1, i + 1)
                norm_apply(ch, u, n, mv, rs, 0)
                for k in range(n):
                    dve.scalar_tensor_tensor(x1[:, k, :], u[:, k, :], rs[:, k:k + 1], vecs[:, 1, :],
                                             ALU.mult, ALU.add).then_inc(x1_ready, 1)
                if n == 2:
                    assert ch.n == E_STEPS, ch.n

            def mix_y(i, n):
                ch = Chain(dve, dve_f, i * F_STEPS)
                dve.wait_ge(y_made, i + (1 + ONE))
                ch.link(dve.tensor_tensor(u2[:, 0:n, :], p6[:, 0:n * C].rearrange("p (i c) -> p i c", i=n),
                                          x1[:, 0:n, :], ALU.add))
                stats(ch, lambda j: u2[:, j, :], n, st2, mv2, stats2)
                if n == 2:
                    assert ch.n == F_STEPS, ch.n

            def mix_out(i, n):
                ch = Chain(dve, dve_g, i * E_STEPS)
                dve.wait_ge(dev2, i + 1)
                norm_apply(ch, u2, n, mv2, rs2, 3)
                dve.wait_ge(pair_added, dve.snap(pair, min_val=0, max_val=NG * NT) + ONE)
                for k in range(n):
                    row = acc[:, bass.ds(2 * i + k, 1), :].rearrange("p o c -> p (o c)")
                    dve.scalar_tensor_tensor(row, u2[:, k, :], rs2[:, k:k + 1], row, ALU.mult, ALU.add)\
                       .then_inc(mix_done, 1)
                dve.wait_ge(mix_done, 2 * i + n)

            def mix_round(i, r, n, before, groups=SLOTS):
                edges(r, 0)
                mix_q(i, n)
                edges(r, 1)
                mix_t(i, n)
                for s in range(2, groups):
                    edges(r, s)
                    if s == 2 and before:
                        mix_y(i - 1, 2)
                    if s == 3:
                        mix_x1(i, n)
                    if s == 4 and before:
                        mix_out(i - 1, 2)
                if groups < SLOTS:
                    mix_y(i - 1, 2)
                    mix_x1(i, n)
                    mix_out(i - 1, 2)
            mix_round(0, KEY_ROUNDS, 2, False)
            with dve.Fori(1, NT // 2) as i:
                mix_round(i, i + KEY_ROUNDS, 2, True)
            mix_round(NT // 2, ROUNDS, 1, True, TAIL)
            add_pair(dve.snap(pair, min_val=0, max_val=NG * NT))
            mix_y(NT // 2, 1)
            mix_out(NT // 2, 1)
            alone(dve)
            dve.engine_nop().then_inc(total_ready, 1)

            def bc(v, n):
                return v.unsqueeze(1).to_broadcast([P, n, X])
            cd = Chain(dve, dve_d0)
            cd.link(dve.memset(before[:, LG, :], 0.0))
            cd.link(dve.memset(rows, 0.0))

            def dispatch(g, s):
                ch = Chain(dve, dve_d, g * D_STEPS)
                dve.wait_ge(dev3, g + 1)
                ch.link(dve.reciprocal(rs[:, :], rs[:, :]))
                if not isinstance(g, int) or g >= 2:
                    dve.wait_ge(rows_sent[s], (g - s) * (16 * LG))
                for j in range(LG):
                    dve.tensor_scalar(rows[:, s, j, 0:C], acc[:, bass.ds(g * LG + j, 1), :].rearrange("p o c -> p (o c)"),
                                      mv[:, j, 0:1], rs[:, j:j + 1], ALU.subtract, ALU.mult).then_inc(rows_ready, 1)
                ch.step(dve.tensor_copy(rows[:, s, :, TOK], tokid[:, bass.ds(g * LG, LG)]))
                if g + 1 < NT // LG:
                    dve.wait_ge(rows_ready, LG * (g + 1))
                    row_stats(g + 1)
                dve.wait_ge(logits_made, g + (1 + ONE))
                ch.link(dve.tensor_tensor(lg, p6[:, 0:LG * X].rearrange("p (j e) -> p j e", j=LG), bc(bg[:, :], LG),
                                          ALU.add), apart=True)
                for j in range(LG):
                    ch.step(dve.max(mx[:, j, :], lg[:, j, :]))
                ch.wait(apart=True)
                for j in range(LG):
                    ch.step(dve.max_index(ix[:, j, :], mx[:, j, :], lg[:, j, :]))
                ch.step(dve.tensor_tensor(gap, mx[:, :, 1], mx[:, :, 0], ALU.subtract))
                ch.wait()
                alone(dve)
                dve.engine_nop().then_inc(gap_ready, 1)
                ch.link(dve.tensor_copy(rows[:, s, :, EX:EX + 2], ix[:, :, 0:2]))
                for k, o1 in ((0, oh1), (1, oh2)):
                    ch.step(dve.tensor_tensor(o1, bc(iota8[:, :], LG),
                                              rows[:, s, :, EX + k:EX + k + 1].to_broadcast([P, LG, X]), ALU.is_equal))
                ch.wait()
                ch.step(dve.tensor_tensor(both, oh1, oh2, ALU.add))
                ch.link(dve.tensor_copy(before[:, 0, :], before[:, LG, :]))
                for j in range(LG):
                    ins = dve.tensor_tensor(before[:, j + 1, :], before[:, j, :], both[:, j, :], ALU.add)
                    ch.link(ins)
                alone(dve)
                dve.engine_nop().then_inc(both_ready, 1)
                dve.wait_ge(ex_ready, g + 1)
                ch.link(dve.tensor_scalar(den, ex, 1.0, None, ALU.add))
                ch.link(dve.reciprocal(rows[:, s, :, WT], den))
                ch.step(dve.tensor_tensor(rows[:, s, :, WT + 1], ex, rows[:, s, :, WT], ALU.mult))
                dve.wait_ge(rank_made, g + 1)
                ch.link(dve.tensor_tensor(place, p7[:, 0:LG * X].rearrange("p (j e) -> p j e", j=LG),
                                          bc(capcol[:, :], LG), ALU.add))
                for k, o1 in ((0, oh1), (1, oh2)):
                    ch.link(dve.tensor_tensor(pick, o1, place, ALU.mult))
                    ch.link(dve.tensor_reduce(slotf[:, k, :], pick, AX_X, ALU.add))
                ch.link(dve.tensor_copy(sloti[:, s, :, :], slotf))
                alone(dve)
                dve.engine_nop().then_inc(slots_ready, 1)
                assert ch.n == D_STEPS, ch.n
            def row_stats(g):
                stats(cs, lambda j: acc[:, g * LG + j, :], LG, st, mv, stats3)
            cs = Chain(dve, dve_s)
            row_stats(0)
            for g in range(NT // LG):
                dispatch(g, g % 2)
            alone(dve)
            dve.engine_nop().then_inc(total_made, 1)
            dve.wait_ge(total_done, 1)
            cd.link(dve.tensor_copy(countf, p7[:, 0:X]))
            dve.tensor_copy(counti[:, :], countf).then_inc(counts_ready, 1)
            cd.link(dve.tensor_scalar(countf, countf, float(P - 1), float(P), ALU.add, ALU.max))
            cd.link(dve.tensor_copy(tilesi[:, :], countf))
            dve.tensor_scalar(tilesi[:, :], tilesi[:, :], P.bit_length() - 1, None, ALU.arith_shift_right)\
               .then_inc(counts_ready, 1)

            k = dve.alloc_register("dve_tile")
            dve.reg_mov(k, 0)
            cnt = dve.alloc_register("dve_count")
            dve.wait_ge(counts_ready, 2)

            def turned(n):
                dve.wait_ge(tile_turned, n + (1 + ONE))
                dve.tensor_copy(xeT.rearrange("p c n -> p (c n)"), p4[:, 0:C]).then_inc(tileT_ready, 1)
            turned(0)

            M_STEPS = 6

            def expert(e, s, visit):
                dve.load(cnt, tilesi[0:1, bass.ds(e, 1)])
                with dve.Fori(0, dve.snap(cnt, min_val=1, max_val=NT)):
                    n = dve.snap(k, min_val=0, max_val=X * NT)
                    ch = Chain(dve, dve_m, n * M_STEPS)
                    dve.wait_ge(tile_loaded, 16 * n + 16)
                    dve.tensor_copy(meta, xin[:, C:ROW]).then_inc(meta_ready, 1)
                    dve.wait_ge(meta_ready, n + (1 + ONE))
                    ch.link(dve.tensor_scalar(same, meta[:, EX - C:EX - C + 2], iota8[:, bass.ds(e, 1)], None,
                                              ALU.is_equal))
                    ch.link(dve.tensor_tensor(wsel[:, 0:2], same, meta[:, WT - C:WT - C + 2], ALU.mult))
                    ch.link(dve.tensor_tensor(wsel[:, 2:3], wsel[:, 0:1], wsel[:, 1:2], ALU.add))
                    dve.wait_ge(up_made, n * MC + MC)
                    turned(n + 1)
                    dve.wait_ge(tile_added, n + ONE)
                    ch.step(dve.tensor_copy(toki[:, :], meta[:, TOK - C:TOK - C + 1]))
                    dve.wait_ge(down_made, n + (1 + ONE))
                    ch.link(dve.tensor_tensor(yt, pg[:, 2, 0:C], eb2[:, bass.ds(e, 1), :].rearrange("p o c -> p (o c)"),
                                              ALU.add))
                    ch.link(dve.tensor_scalar(yo, yt, wsel[:, 2:3], None, ALU.mult))
                    alone(dve)
                    dve.engine_nop().then_inc(result_ready, 1)
                    assert ch.n == M_STEPS
                    dve.reg_add(k, k, 1)
            with dve.Fori(0, X // 2) as visit:
                expert(visit * 2, 0, visit)
                expert(visit * 2 + 1, 1, visit)


def kernel(**inputs):
    import numpy as np
    import concourse.bacc as bacc
    from concourse.bass_utils import run_bass_kernel_spmd

    g = {k: np.ascontiguousarray(np.asarray(v)) for k, v in inputs.items()}
    f32 = np.float32

    def pad(v, n, fill=0):
        o = np.full((n,) + v.shape[1:], fill, v.dtype)
        o[:v.shape[0]] = v
        return o

    def turned(v):
        return np.ascontiguousarray(v.reshape(GP * GT, P).T)

    def chunks(w, n):
        return np.ascontiguousarray(w.reshape(n, P, -1).transpose(1, 0, 2))

    def rows(v):
        return np.ascontiguousarray(np.broadcast_to(v, (P,) + v.shape))

    src, rel = (pad(g[k], GP * GT * P) for k in ("src", "edge_type_8"))
    dst = pad(g["dst"], GP * GT * P, N - 1)
    gw = g["L0_gnn_weight"].reshape(R, CC, HC, HD, HD)
    wblk = np.zeros((P, CC, R, P), f32)
    for c in range(CC):
        for b in range(HC):
            for r in range(R):
                wblk[b * HD:(b + 1) * HD, c, r, b * HD:(b + 1) * HD] = gw[r, c, b]
    wqkv = g["L0_mix_Wqkv"].T
    blockmask = np.zeros((P, KW), f32)
    for b in range(HC):
        blockmask[b * HD:(b + 1) * HD, b * HD:(b + 1) * HD] = 1
        blockmask[b * HD:(b + 1) * HD, P + b] = 1
    padrows = np.zeros((P, ROW), f32)
    padrows[:, TOK] = NP + np.arange(P)
    padrows[:, EX:EX + 2] = -1
    arrays = {
        "x": pad(g["x"], NP),
        "srcT": turned(src), "relT": turned(rel), "dstT": turned(dst), "ewT": turned(pad(g["edge_weight"], GP * GT * P)),
        "dstrow": np.ascontiguousarray(dst.reshape(GP, GT * P)[0:NG]),
        "wblk": wblk,
        "ident": np.eye(P, dtype=f32), "upper": np.triu(np.ones((P, P), f32), 1), "ones": np.ones((P, P), f32),
        "blockmask": blockmask,
        "nodemask": np.ascontiguousarray((np.arange(NP) < N).astype(f32).reshape(NT, P).T),
        "vecs": rows(np.stack([g["L0_mix_ln1_g"], g["L0_mix_ln1_b"], g["L0_mix_b2"], g["L0_mix_ln2_g"],
                               g["L0_mix_ln2_b"]])),
        "b1T": np.ascontiguousarray(g["L0_mix_b1"].reshape(CC, P).T),
        "wqT": chunks(wqkv[:, 0:C], CC), "wkvT": chunks(wqkv[:, C:3 * C], CC),
        "w1T": chunks(g["L0_mix_W1"].T, CC), "w2T": chunks(g["L0_mix_W2"].T, CC),
        "wg": chunks(g["L0_ffn_Wg"], CC), "bg": rows(g["L0_ffn_bg"]),
        "eb1T": np.ascontiguousarray(g["L0_ffn_b1"].reshape(X, MC, P).transpose(2, 0, 1)),
        "capcol": rows(np.arange(X, dtype=f32) * CAP), "iota8": rows(np.arange(X, dtype=f32)),
        "padrows": padrows,
        "ew1": np.ascontiguousarray(g["L0_ffn_W1"].reshape(X, CC, P, HID).transpose(0, 2, 1, 3)),
        "ew2": np.ascontiguousarray(g["L0_ffn_W2"].reshape(X, MC, P, C).transpose(0, 2, 1, 3)),
        "eb2": rows(g["L0_ffn_b2"]),
    }
    nc = bacc.Bacc("TRN2", target_bir_lowering=False, num_devices=1)
    args = {n: nc.dram_tensor(f"in_{n}", v.shape, mybir.dt.from_np(v.dtype), kind="ExternalInput").ap()
            for n, v in arrays.items()}
    out = nc.dram_tensor("out", [NP + P, C], F32, kind="ExternalOutput").ap()
    build(nc, args, out)
    r = run_bass_kernel_spmd(nc, [{f"in_{n}": v for n, v in arrays.items()}], core_ids=[0])
    return r.results[0]["out"][0:N]
```

```python
from contextlib import ExitStack

import concourse.bass as bass
from concourse import mybir

F32 = mybir.dt.float32
I32 = mybir.dt.int32
U32 = mybir.dt.uint32
ALU = mybir.AluOpType
ACT = mybir.ActivationFunctionType
AX_X = mybir.AxisListType.X

P = 128
N, C = 3125, 256
NT = -(-N // P)
NP = NT * P
CC = C // P
E = 50000
GT = 4
HALF = GT // 2
NG = -(-E // (GT * P))
SLOTS = 6
ROUNDS = NG // SLOTS
TAIL = NG % SLOTS
LEAD = 3
LAG = 2
GP = (ROUNDS + 1) * SLOTS
R = 8
HEADS = 8
HC = HEADS // CC
HD = C // HEADS
KW = P + HC
X = 8
HID = 1024
MC = HID // P
EPS_LN = 1e-5
EPS_ATTN = 1e-6
LG = 5
KEY_ROUNDS = (NT - 1) // SLOTS
QUERY_GROUP = 3
CAP = NP + P
ROW = 264
TOK, WT, EX = C, C + 1, C + 3


ARENA = 2 * LG * C + LG * C + CC * R * P + LG * R * C


def build(nc, a, out):
    assert NT == LG * LG and NT % 2 and TAIL == 2 and ROUNDS % 2 == 0
    assert KEY_ROUNDS * SLOTS == NT - 1 and ROUNDS - KEY_ROUNDS == NT // 2
    ctx = ExitStack()
    with ctx:
        def sb(name, shape, dt=F32):
            return ctx.enter_context(nc.sbuf_tensor(name, shape, dt))

        def pb(name, shape):
            return ctx.enter_context(nc.psum_tensor(name, shape, F32))

        def sem(name):
            return ctx.enter_context(nc.semaphore(name))

        y_dram = nc.dram_tensor("rel_messages", [NP * R, C], F32, kind="Internal").ap()
        range_dram = nc.dram_tensor("group_ranges", [NG, 2], I32, kind="Internal").ap()
        slot_dram = nc.dram_tensor("expert_rows", [X * CAP, ROW], F32, kind="Internal").ap()

        acc = sb("acc", [P, NT, C])
        xn = sb("xn", [P, NT, C])
        xnT = sb("xnT", [P, NT, CC, P])
        ident = sb("ident", [P, P])
        upper = sb("upper", [P, P])
        ones = sb("ones", [P, P])
        blockmask = sb("blockmask", [P, KW])
        nodemask = sb("nodemask", [P, NT])
        vecs = sb("vecs", [P, 5, C])
        b1T = sb("b1T", [P, CC])
        wqT = sb("wqT", [P, CC, C])
        wkvT = sb("wkvT", [P, CC, 2 * C])
        w1T = sb("w1T", [P, CC, C])
        w2T = sb("w2T", [P, CC, C])
        wg = sb("wg", [P, CC, X])
        bg = sb("bg", [P, X])
        eb1T = sb("eb1T", [P, X, MC])
        eb2 = sb("eb2", [P, X, C])
        capcol = sb("capcol", [P, X])
        iota8 = sb("iota8", [P, X])
        padrows = sb("padrows", [P, ROW])
        srcT = sb("srcT", [P, GP * GT], I32)
        relT = sb("relT", [P, GP * GT], I32)
        dstT = sb("dstT", [P, GP * GT], I32)
        idx = sb("idx", [P, GP * GT], I32)
        dstf = sb("dstf", [P, GP * GT])
        ew = sb("ew", [P, GP * GT])
        dstrow = sb("dstrow", [NG, GT * P], I32)
        rng2 = sb("rng2", [NG, 2], I32)
        rng3 = sb("rng3", [NG, 2], I32)
        ranges = sb("ranges", [1, NG * 2], I32)
        iota = sb("iota", [P, NP])
        tokid = sb("tokid", [P, NT])
        zeros = sb("zeros", [P, C])
        gidx = sb("gidx", [P, 2, SLOTS * GT], I32)
        oh = sb("oh", [P, 2, GT, P])
        st = sb("st", [P, LG, 6])
        mv = sb("mv", [P, LG, 2])
        mv3 = sb("mv3", [P, NT, 2])
        rs3 = sb("rs3", [P, NT])
        shift_by = sb("shift_by", [P, NT])
        rs = sb("rs", [P, LG])
        st2 = sb("st2", [P, 2, 6])
        mv2 = sb("mv2", [P, 2, 2])
        rs2 = sb("rs2", [P, 2])
        eps = sb("eps", [P, 1])
        table_use = sb("table_use", [P, 1])
        var = sb("var", [P, LG])
        minus_half = sb("minus_half", [P, LG])
        arena = sb("arena", [P, ARENA])

        def view(lo, n):
            return arena[:, lo:lo + n]
        xs = view(0, 2 * LG * C).rearrange("p (j c) -> p j c", j=2 * LG)
        o = 2 * LG * C
        xTs = view(o, LG * C).rearrange("p (s c n) -> p s c n", s=LG, c=CC)
        o += LG * C
        wblk = view(o, CC * R * P).rearrange("p (c r o) -> p c r o", c=CC, r=R)
        o += CC * R * P
        ys = view(o, LG * R * C).rearrange("p (j r c) -> p j r c", j=LG, r=R)
        assert o + LG * R * C <= ARENA
        ring = view(0, SLOTS * GT * C).rearrange("p (s j c) -> p s j c", s=SLOTS, j=GT)
        o = SLOTS * GT * C
        kvx = view(o, C).rearrange("p (c n) -> p c n", c=CC)
        ek = view(o + C, 2 * C)
        ks = view(o + 3 * C, C)
        vs = view(o + 4 * C, C)
        kvr = view(o + 5 * C, CC * KW).rearrange("p (c k) -> p c k", c=CC)
        o += 5 * C + CC * KW
        qs = view(o, 2 * C).rearrange("p (m n) -> p m n", m=CC)
        u = view(o + 2 * C, 2 * C).rearrange("p (i c) -> p i c", i=2)
        x1 = view(o + 4 * C, 2 * C).rearrange("p (i c) -> p i c", i=2)
        x1T = view(o + 6 * C, 2 * C).rearrange("p (i c n) -> p i c n", i=2, c=CC)
        hs = view(o + 8 * C, 2 * C).rearrange("p (m n) -> p m n", m=CC)
        u2 = view(o + 10 * C + 2 * HEADS, 2 * C).rearrange("p (i c) -> p i c", i=2)
        z = view(o + 10 * C, 2 * HEADS).rearrange("p (i h) -> p i h", i=2)
        o += 12 * C + 2 * HEADS
        ew_sets = []
        rows = view(0, NT * ROW).rearrange("p (s j c) -> p s j c", s=NT // LG, j=LG)
        xfT = view(o, LG * C).rearrange("p (j c n) -> p j c n", j=LG, c=CC)
        o += LG * C
        lg = view(o, LG * X).rearrange("p (j e) -> p j e", j=LG)
        mx = view(o + 40, LG * 8).rearrange("p (j e) -> p j e", j=LG)
        oh1 = view(o + 80, LG * X).rearrange("p (j e) -> p j e", j=LG)
        oh2 = view(o + 120, LG * X).rearrange("p (j e) -> p j e", j=LG)
        both = view(o + 160, LG * X).rearrange("p (j e) -> p j e", j=LG)
        before = view(o + 200, (LG + 1) * X).rearrange("p (j e) -> p j e", j=LG + 1)
        place = view(o + 248, LG * X).rearrange("p (j e) -> p j e", j=LG)
        pick = view(o + 288, LG * X).rearrange("p (j e) -> p j e", j=LG)
        gap = view(o + 328, LG)
        ex = view(o + 333, LG)
        den = view(o + 338, LG)
        slotf = view(o + 344, 2 * LG).rearrange("p (s j) -> p s j", s=2)
        countf = view(o + 354, X)
        o += 368
        ix = sb("ix", [P, LG, 8], U32)
        sloti = sb("sloti", [P, NT // LG, 2, LG], I32)
        counti = sb("counti", [P, X], I32)
        tilesi = sb("tilesi", [P, X], I32)
        toki = sb("toki", [P, 1], I32)
        meta = view(o, ROW - C)
        o += ROW - C
        xin = view(o, ROW)
        xeT = view(o + ROW, C).rearrange("p (c n) -> p c n", c=CC)
        h = view(o + ROW + C, MC * P).rearrange("p (m n) -> p m n", m=MC)
        yt = view(o + ROW + C + MC * P, C)
        yo = view(o + ROW + 2 * C + MC * P, C)
        same = view(o + ROW + 3 * C + MC * P, 2)
        wsel = view(o + ROW + 3 * C + MC * P + 4, 3)
        o += ROW + 3 * C + MC * P + 8
        assert o <= ARENA
        xn_flat = xn[:, :, :].rearrange("p t c -> p (t c)")
        xnT_flat = xnT[:, :, :, :].rearrange("p t c n -> p (t c n)")
        for flat in (xn_flat, xnT_flat):
            ew_sets.append((flat[:, 0:CC * HID].rearrange("p (c h) -> p c h", c=CC),
                            flat[:, CC * HID:CC * HID + MC * C].rearrange("p (m f) -> p m f", m=MC)))

        pg = pb("pg", [P, 4, 512])
        p45 = pb("p45", [P, 2, 512])
        p4, p5 = p45[:, 0, :], p45[:, 1, :]
        p6 = pb("p6", [P, 512])
        p7 = pb("p7", [P, 512])

        hbank = [pg[:, 0, :], pg[:, 1, :], pg[:, 3, :], p5[:, :]]

        x_first, x_rest = sem("x_first"), sem("x_rest")
        msg_w_loaded, vecs_loaded, const_loaded, edges_loaded = (
            sem("msg_w_loaded"), sem("vecs_loaded"), sem("const_loaded"), sem("edges_loaded"))
        ranges_stored, ranges_loaded = sem("ranges_stored"), sem("ranges_loaded")
        iota_ready, idx_ready, ranges_ready, zeros_ready = (sem("iota_ready"), sem("idx_ready"),
                                                            sem("ranges_ready"), sem("zeros_ready"))
        dve_a = sem("dve_a")
        xs_ready, xs_turned, xT_kept, xT_ready = sem("xs_ready"), sem("xs_turned"), sem("xT_kept"), sem("xT_ready")
        xn_kept, bias_added = sem("xn_kept"), sem("bias_added")
        y0_made, y1_made, y0_kept, y1_kept = sem("y0_made"), sem("y1_made"), sem("y0_kept"), sem("y1_kept")
        y_stored = [sem(f"y_stored{j}") for j in range(LG)]
        gathered = [sem(f"gathered{s}") for s in range(SLOTS)]
        group_used = [sem(f"group_used{s}") for s in range(SLOTS)]
        weighed, onehot_ready, onehot_used, pair_done, pair_added = (
            sem("weighed"), sem("onehot_ready"), sem("onehot_used"), sem("pair_done"), sem("pair_added"))
        kvx_ready, kv_made, ek_ready, v_ready, k_ready, kv_summed = (
            sem("kvx_ready"), sem("kv_made"), sem("ek_ready"), sem("v_ready"), sem("k_ready"), sem("kv_summed"))
        kvr_ready = sem("kvr_ready")
        q_made, eq_ready, q_ready, t_made = sem("q_made"), sem("eq_ready"), sem("q_ready"), sem("t_made")
        dve_c, x1_ready, x1_turned, x1T_ready = sem("dve_c"), sem("x1_ready"), sem("x1_turned"), sem("x1T_ready")
        h_made, h_ready, y_made, mix_done = sem("h_made"), sem("h_ready"), sem("y_made"), sem("mix_done")
        out_started, dve_d, rows_ready, rows_turned, rowsT_ready = (
            sem("out_started"), sem("dve_d"), sem("rows_ready"), sem("rows_turned"), sem("rowsT_ready"))
        logits_made, gap_ready, ex_ready, both_ready, rank_made, slots_ready = (
            sem("logits_made"), sem("gap_ready"), sem("ex_ready"), sem("both_ready"), sem("rank_made"),
            sem("slots_ready"))
        rows_sent, rows_shift = sem("rows_sent"), sem("rows_shift")
        total_ready, total_made, counts_ready, pads_sent = (sem("total_ready"), sem("total_made"),
                                                            sem("counts_ready"), sem("pads_sent"))
        weights_loaded = [sem(f"weights_loaded{s}") for s in range(2)]
        weights_used = [sem(f"weights_used{s}") for s in range(2)]
        tile_loaded, tile_turned, tileT_ready, meta_ready = (
            sem("tile_loaded"), sem("tile_turned"), sem("tileT_ready"), sem("meta_ready"))
        up_made, act_ready, down_made, dve_m, result_ready, added = (
            sem("up_made"), sem("act_ready"), sem("down_made"), sem("dve_m"), sem("result_ready"), sem("added"))
        var_ready, rs_ready, minus_ready = sem("var_ready"), sem("rs_ready"), sem("minus_ready")
        tile_added = sem("tile_added")
        rk_ready, rq_ready = sem("rk_ready"), sem("rq_ready")
        stats1, stats2, stats3, dev1, dev2, dev3 = (sem(x) for x in ("stats1", "stats2", "stats3", "dev1", "dev2", "dev3"))
        dve_s, dve_rows = sem("dve_s"), sem("dve_rows")
        dve_e, dve_f, dve_g = sem("dve_e"), sem("dve_f"), sem("dve_g")
        dve_r, dstf_ready, idx_staged, total_done, dve_d0 = (
            sem("dve_r"), sem("dstf_ready"), sem("idx_staged"), sem("total_done"), sem("dve_d0"))

        waited = {e.engine: sem(f"waited{n}") for n, e in enumerate((nc.sync, nc.gpsimd, nc.tensor, nc.vector))}

        ONE = 1

        def alone(eng):
            eng.sem_inc(waited[eng.engine], 1)

        class Chain:

            def __init__(self, eng, s, base=0):
                self.eng, self.s, self.base, self.n = eng, s, base, 0

            def step(self, ins):
                self.n += 1
                ins.then_inc(self.s, 1)

            def wait(self, apart=False):
                self.eng.wait_ge(self.s, self.base + self.n)
                if apart:
                    alone(self.eng)

            def link(self, ins, apart=False):
                self.step(ins)
                self.wait(apart)

        A_STEPS = 2 * LG
        C_STEPS = 2 + 1 + 2 + 1 + 2
        E_STEPS = 3
        F_STEPS = 1 + 2
        D_STEPS = 16 + 3 * LG

        block = ctx.enter_context(nc.Block())

        @block.sync
        def _(sp):
            x_v = a["x"].rearrange("(t p) c -> p t c", p=P)
            sp.dma_start(acc[:, 0:LG, :], x_v[:, 0:LG, :]).then_inc(x_first, 16)
            sp.dma_start(wblk, a["wblk"]).then_inc(msg_w_loaded, 16)
            sp.dma_start(ident[:, :], a["ident"]).then_inc(msg_w_loaded, 16)
            for g in range(1, NT // LG):
                sp.dma_start(acc[:, g * LG:(g + 1) * LG, :], x_v[:, g * LG:(g + 1) * LG, :]).then_inc(x_rest, 16)
            sp.dma_start(vecs[:, :, :], a["vecs"]).then_inc(vecs_loaded, 16)
            for dst, name in ((b1T, "b1T"), (wqT, "wqT"), (wkvT, "wkvT"), (w1T, "w1T"),
                              (w2T, "w2T"), (wg, "wg"), (bg, "bg"), (eb1T, "eb1T"), (eb2, "eb2"), (capcol, "capcol"),
                              (iota8, "iota8"), (padrows, "padrows"), (upper, "upper"), (ones, "ones"),
                              (blockmask, "blockmask"), (nodemask, "nodemask")):
                sp.dma_start(dst[tuple(slice(None) for _ in a[name].shape)], a[name]).then_inc(const_loaded, 16)
            y_v = y_dram.rearrange("(t p r) c -> t p r c", p=P, r=R)

            def store_y(t, j):
                sp.wait_ge(y0_kept, t + (1 + ONE))
                sp.wait_ge(y1_kept, t + (1 + ONE))
                sp.dma_start(y_v[bass.ds(t, 1)].rearrange("o p r c -> (o p) r c"), ys[:, j, :, :])\
                  .then_inc(y_stored[j], 16)
            with sp.Fori(0, NT // LG) as g:
                for j in range(LG):
                    store_y(g * LG + j, j)
            out_v = out.rearrange("(t p) c -> p t c", p=P)
            sp.wait_ge(const_loaded, 16 * 16)
            sp.dma_start(out[NP:NP + P, :], padrows[:, 0:C]).then_inc(out_started, 16)
            sp.wait_ge(kvr_ready, 1)
            sp.wait_ge(mix_done, NT)
            sp.wait_ge(total_ready, 1)
            sp.dma_start(out_v[:, 0:NT, :], acc[:, :, :]).then_inc(out_started, 16)
            sp.wait_ge(counts_ready, 2)
            for e in range(X):
                n = sp.value_load(counti[0:1, e:e + 1], min_val=0, max_val=NP)
                sp.dma_start(slot_dram[bass.ds(n + e * CAP, P), :], padrows[:, :]).then_inc(pads_sent, 16)
            sp.wait_ge(pads_sent, 16 * X)
            sp.wait_ge(rows_sent, 16 * 2 * NT)
            k = sp.alloc_register("sp_tile")
            sp.reg_mov(k, 0)

            def load_tile(row, n):
                sp.wait_ge(tile_turned, n + ONE)
                sp.wait_ge(meta_ready, n + ONE)
                sp.dma_start(xin, slot_dram[bass.ds(row, P), :]).then_inc(tile_loaded, 16)
                sp.wait_ge(tile_loaded, 16 * n + 16)
                alone(sp)
            cnt = sp.alloc_register("sp_count")
            with sp.Fori(0, X) as e:
                sp.load(cnt, tilesi[0:1, bass.ds(e, 1)])
                with sp.Fori(0, sp.snap(cnt, min_val=1, max_val=NT)) as i:
                    n = sp.snap(k, min_val=0, max_val=X * NT)
                    load_tile(e * CAP + i * P, n)
                    sp.reg_add(k, k, 1)
            load_tile(0, sp.snap(k, min_val=0, max_val=X * NT))

        @block.gpsimd
        def _(pool):
            for counted_from_one in (tile_added,):
                pool.sem_inc(counted_from_one, ONE)

            def deviation(i, w):
                pool.wait_ge(var_ready, i + 1)
                pool.tensor_tensor(rs[:, 0:w], var[:, 0:w], minus_half[:, 0:w], ALU.pow).then_inc(rs_ready, 1)

            def keep(t, j):
                pool.wait_ge(xs_ready, t + 1)
                pool.tensor_copy(xn[:, bass.ds(t, 1), :], xs[:, bass.ds(j, 1), :]).then_inc(xn_kept, 1)
                pool.tensor_tensor(acc[:, bass.ds(t, 1), :], acc[:, bass.ds(t, 1), :], vecs[:, 4:5, :],
                                   ALU.add).then_inc(bias_added, 1)
            pool.iota(iota[:, :], pattern=[[1, NP]], base=0, channel_multiplier=0,
                      allow_small_or_imprecise_dtypes=True).then_inc(iota_ready, 1)
            pool.iota(tokid[:, :], pattern=[[P, NT]], base=0, channel_multiplier=1,
                      allow_small_or_imprecise_dtypes=True).then_inc(iota_ready, 1)
            pool.memset(minus_half[:, :], -0.5).then_inc(minus_ready, 1)
            pool.wait_ge(minus_ready, 1)
            deviation(0, LG)
            deviation(1, LG)
            pool.wait_ge(vecs_loaded, 16)
            for j in range(LG):
                keep(j, j)
            deviation(2, LG)
            with pool.Fori(1, NT // LG - 2) as g:
                for j in range(LG):
                    keep(g * LG + j, (g % 2) * LG + j)
                deviation(g + 2, LG)
            with pool.Fori(NT // LG - 2, NT // LG) as g:
                for j in range(LG):
                    keep(g * LG + j, (g % 2) * LG + j)
            pool.wait_ge(ranges_ready, 1)
            pool.dma_start(range_dram, rng3[:, :]).then_inc(ranges_stored, 16)
            pool.wait_ge(ranges_stored, 16)
            pool.dma_start(ranges[:, :], range_dram.rearrange("(o g) k -> o (g k)", o=1)).then_inc(ranges_loaded, 16)
            for j in range(LG):
                pool.wait_ge(y_stored[j], 16 * (NT // LG))
            pool.wait_ge(xn_kept, NT)
            pool.wait_ge(bias_added, NT)
            pool.wait_ge(idx_ready, 1)

            def stage(r, par):
                pool.tensor_copy(gidx[:, par, :], idx[:, bass.ds(r * (SLOTS * GT), SLOTS * GT)])\
                    .then_inc(idx_staged, 1)

            def gather(par, s):
                for j in range(GT):
                    c = s * GT + j
                    pool.indirect_dma_start(
                        out=ring[:, s, j, :], out_offset=None, in_=y_dram[:, :],
                        in_offset=bass.IndirectOffsetOnAxis(ap=gidx[:, par, c:c + 1], axis=0))\
                        .then_inc(gathered[s], 16)

            def gather_round(r, par, groups=SLOTS):
                pool.wait_ge(idx_staged, r + 1)
                for s in range(groups):
                    pool.wait_ge(group_used[s], r + (1 if s >= SLOTS - LAG else 0))
                    if s == SLOTS - 1:
                        stage(r + 1, 1 - par)
                    else:
                        alone(pool)
                    gather(par, s)
            stage(0, 0)
            stage(1, 1)
            pool.wait_ge(idx_staged, 2)
            for s in range(SLOTS):
                gather(0, s)
            gather_round(1, 1)
            with pool.Fori(1, ROUNDS // 2) as k:
                gather_round(k * 2, 0)
                gather_round(k * 2 + 1, 1)
            gather_round(ROUNDS, 0, TAIL)

            def dispatch(g):
                pool.wait_ge(slots_ready, g + 1)
                for c in range(2):
                    for j in range(LG):
                        pool.indirect_dma_start(
                            out=slot_dram[:, :],
                            out_offset=bass.IndirectOffsetOnAxis(ap=sloti[:, g, c, j:j + 1], axis=0),
                            in_=rows[:, g, j, :], in_offset=None).then_inc(rows_sent, 16)
            for g in range(NT // LG):
                dispatch(g)
            pool.wait_ge(out_started, 32)
            k = pool.alloc_register("pool_tile")
            pool.reg_mov(k, 0)
            cnt = pool.alloc_register("pool_count")
            pool.wait_ge(counts_ready, 2)
            with pool.Fori(0, X) as e:
                pool.load(cnt, tilesi[0:1, bass.ds(e, 1)])
                with pool.Fori(0, pool.snap(cnt, min_val=1, max_val=NT)) as i:
                    n = pool.snap(k, min_val=0, max_val=X * NT)
                    pool.wait_ge(result_ready, n + (1 + ONE))
                    alone(pool)
                    pool.indirect_dma_start(
                        out=out[:, :], out_offset=bass.IndirectOffsetOnAxis(ap=toki[:, 0:1], axis=0),
                        in_=yo, in_offset=None, compute_op=ALU.add).then_inc(added, 16)
                    pool.wait_ge(added, 16 * n + 16)
                    pool.sem_inc(tile_added, 1)
                    pool.reg_add(k, k, 1)

        @block.scalar
        def _(act):
            act.dma_start(dstrow[:, :], a["dstrow"]).then_inc(edges_loaded, 16)
            for dst, name in ((srcT, "srcT"), (relT, "relT"), (dstT, "dstT"), (ew, "ewT")):
                act.dma_start(dst[:, :], a[name]).then_inc(edges_loaded, 16)
            for counted_from_one in (xT_kept, xT_ready, y0_kept, v_ready, eq_ready, rowsT_ready, act_ready):
                act.sem_inc(counted_from_one, ONE)

            def turned_kept(t, j, first=False):
                act.wait_ge(xs_turned, t + 1)
                if not first:
                    act.wait_ge(y1_made, t - (LG - 1))
                bank = p45[:, bass.ds(t % 2, 1), 0:C]
                act.activation(xTs[:, j], bank.rearrange("p o (c n) -> p (o c) n", c=CC), ACT.Copy).then_inc(xT_ready, 1)
                act.activation(xnT[:, bass.ds(t, 1)].rearrange("p o c n -> p o (c n)"), bank, ACT.Copy)\
                   .then_inc(xT_kept, 1)

            def message(t, g, j):
                act.wait_ge(y0_made, t + 1)
                if g is not None:
                    act.wait_ge(y_stored[j], g * 16)
                act.activation(ys[:, j, :, 0:P], pg[:, 0:2, :].rearrange("p b (r o) -> p (b r) o", o=P),
                               ACT.Copy).then_inc(y0_kept, 1)
            turned_kept(0, 0, True)
            for j in range(1, LG):
                turned_kept(j, j, True)
                message(j - 1, None, j - 1)
            turned_kept(LG, 0)
            message(LG - 1, None, LG - 1)
            with act.Fori(1, NT // LG - 1) as g:
                for j in range(1, LG + 1):
                    turned_kept(g * LG + j, j % LG)
                    message(g * LG + (j - 1), g, j - 1)
            for t in range(NT - LG, NT):
                if t + 1 < NT:
                    turned_kept(t + 1, (t + 1) % LG)
                message(t, NT // LG - 1, t % LG)
            act.wait_ge(const_loaded, 16 * 16)
            act.wait_ge(zeros_ready, 2)

            def weigh(r, s):
                act.wait_ge(gathered[s], r * (16 * GT) + 16 * GT)
                for j in range(GT):
                    act.activation(ring[:, s, j, :], ring[:, s, j, :], ACT.Copy,
                                   scale=ew[:, bass.ds(r * (SLOTS * GT) + (s * GT + j), 1)]).then_inc(weighed, 1)

            def weigh_ahead(r, s, last=False):
                if not last or s + LEAD < SLOTS + TAIL:
                    weigh(r + (s + LEAD) // SLOTS, (s + LEAD) % SLOTS)

            def keys_turned(t):
                act.wait_ge(kv_made, t + ONE)
                act.activation(kvx, xnT[:, bass.ds(t, 1)].rearrange("p o c n -> p (o c) n"), ACT.Copy)\
                   .then_inc(kvx_ready, 1)

            def keys(t):
                act.wait_ge(kv_made, t + (1 + ONE))
                act.wait_ge(k_ready, t + ONE)
                act.activation(ek[:, 0:C], p5[:, 0:C], ACT.Relu, scale=-1.0).then_inc(rk_ready, 1)
                act.wait_ge(rk_ready, t + 1)
                act.activation(ek[:, 0:C], ek[:, 0:C], ACT.Exp, scale=-1.0).then_inc(ek_ready, 1)
                act.wait_ge(kv_summed, t + ONE)
                act.activation(vs, p5[:, C:2 * C], ACT.Copy).then_inc(v_ready, 1)
            act.wait_ge(xT_kept, NT + ONE)
            for j in range(LG):
                act.wait_ge(y_stored[j], 16 * (NT // LG))
            keys_turned(0)
            for s in range(LEAD):
                weigh(0, s)
            with act.Fori(0, KEY_ROUNDS) as r:
                for s in range(SLOTS):
                    keys(r * SLOTS + s)
                    keys_turned(r * SLOTS + (s + 1))
                    weigh_ahead(r, s)
            keys(NT - 1)

            def two(v, w):
                return v.rearrange("p (m n) -> p m n", m=CC)[:, :, 0:w]

            def deviation(stats, seen, var, sd, made):
                act.wait_ge(stats, seen)
                act.activation(sd, var, ACT.Sqrt, bias=eps[:, :]).then_inc(made, 1)

            def mix_q(i, n):
                w = n * P
                act.wait_ge(q_made, i + 1)
                act.wait_ge(q_ready, i + ONE)
                act.activation(two(ek, w), two(p4[:, :], w), ACT.Relu, scale=-1.0).then_inc(rq_ready, 1)
                act.wait_ge(rq_ready, i + 1)
                act.activation(two(ek, w), two(ek, w), ACT.Exp, scale=-1.0).then_inc(eq_ready, 1)

            def hidden_turned(i, n):
                act.wait_ge(x1_turned, i + 1)
                act.wait_ge(h_made, i + ONE)
                act.activation(x1T[:, 0:n].rearrange("p i c n -> p (i c n)"), p5[:, 0:n * C], ACT.Copy)\
                   .then_inc(x1T_ready, 1)

            def mix_hidden(i, n):
                w = n * P
                act.wait_ge(h_made, i + (1 + ONE))
                act.wait_ge(y_made, i + ONE)
                for m in range(CC):
                    act.activation(hs[:, m, 0:w], p7[:, m * 2 * P:m * 2 * P + w], ACT.Gelu, bias=b1T[:, m:m + 1])\
                       .then_inc(h_ready, 1)

            def mix(i, n, r, before=2, following=2):
                def between(*groups):
                    for s in groups:
                        if r is not None:
                            weigh_ahead(r, s, last=following == 1)
                between(*((0, ) if before else (0, 1)))
                deviation(stats1, i * 2 + n, mv[:, 0:n, 1], rs[:, 0:n], dev1)
                if before:
                    between(1)
                    deviation(stats2, i * 2, mv2[:, 0:2, 1], rs2[:, 0:2], dev2)
                between(2)
                if following:
                    mix_q(i + 1, following)
                between(3)
                hidden_turned(i, n)
                between(4)
                mix_hidden(i, n)
                between(5)
            act.wait_ge(k_ready, NT + ONE)
            mix_q(0, 2)
            mix(0, 2, KEY_ROUNDS, before=0)
            with act.Fori(1, NT // 2 - 1) as i:
                mix(i, 2, i + KEY_ROUNDS)
            mix(NT // 2 - 1, 2, ROUNDS - 1, following=1)
            def load_weights(e, s):
                w1, w2 = ew_sets[s]
                act.dma_start(w1, a["ew1"][bass.ds(e, 1)].rearrange("o p c h -> (o p) c h")).then_inc(weights_loaded[s], 16)
                act.dma_start(w2, a["ew2"][bass.ds(e, 1)].rearrange("o p m f -> (o p) m f")).then_inc(weights_loaded[s], 16)

            def turned(g):
                act.wait_ge(rows_turned, g + 1)
                act.wait_ge(logits_made, g + ONE)
                for v, bank in ((xfT[:, 0:2], p5[:, :]), (xfT[:, 2:4], p4[:, :]), (xfT[:, 4:5], pg[:, 3, 0:C])):
                    act.activation(v.rearrange("p j c n -> p (j c n)"), bank, ACT.Copy).then_inc(rowsT_ready, 1)

            def gate(g):
                act.wait_ge(gap_ready, g + (1 + ONE))
                act.activation(ex, gap, ACT.Exp).then_inc(ex_ready, 1)
            def normed_rows(g):
                act.wait_ge(rows_shift, g + 1)
                for j in range(LG):
                    act.activation(rows[:, g, j, 0:C], acc[:, g * LG + j, :], ACT.Identity,
                                   bias=shift_by[:, g * LG + j:g * LG + j + 1],
                                   scale=rs3[:, g * LG + j:g * LG + j + 1]).then_inc(rows_ready, 1)

            def row_deviation(g):
                t = slice(g * LG, (g + 1) * LG)
                deviation(stats3, LG * (g + 1), mv3[:, t, 1], rs3[:, t], dev3)
            last = NT // 2
            deviation(stats1, NT, mv[:, 0:1, 1], rs[:, 0:1], dev1)
            row_deviation(0)
            normed_rows(0)
            deviation(stats2, NT - 1, mv2[:, 0:2, 1], rs2[:, 0:2], dev2)
            turned(0)
            row_deviation(1)
            load_weights(0, 0)
            load_weights(1, 1)
            normed_rows(1)
            row_deviation(2)
            hidden_turned(last, 1)
            gate(0)
            turned(1)
            mix_hidden(last, 1)
            for g in range(1, NT // LG):
                if g + 1 < NT // LG:
                    normed_rows(g + 1)
                if g + 2 < NT // LG:
                    row_deviation(g + 2)
                gate(g)
                if g + 1 < NT // LG:
                    turned(g + 1)
                if g == 1:
                    deviation(stats2, NT, mv2[:, 0:1, 1], rs2[:, 0:1], dev2)

            k = act.alloc_register("act_tile")
            act.reg_mov(k, 0)
            cnt = act.alloc_register("act_count")
            act.activation(table_use[:, :], eps[:, :], ACT.Gelu)
            act.wait_ge(counts_ready, 2)

            def expert(e):
                act.load(cnt, tilesi[0:1, bass.ds(e, 1)])
                with act.Fori(0, act.snap(cnt, min_val=1, max_val=NT)):
                    n = act.snap(k, min_val=0, max_val=X * NT)
                    act.wait_ge(down_made, n + ONE)
                    for m in range(MC):
                        act.wait_ge(up_made, n * MC + (m + 1))
                        act.activation(h[:, m, :], hbank[m % 4][:, m // 4 * P:m // 4 * P + P], ACT.Gelu,
                                       bias=eb1T[:, bass.ds(e, 1), m:m + 1].rearrange("p a b -> p (a b)"))\
                           .then_inc(act_ready, 1)
                    act.reg_add(k, k, 1)
            with act.Fori(0, X // 2 - 1) as visit:
                for s in range(2):
                    expert(visit * 2 + s)
                    act.wait_ge(weights_used[s], visit + 1)
                    load_weights(visit * 2 + (2 + s), s)
            for s in range(2):
                expert(X - 2 + s)

        @block.tensor
        def _(pe):
            for counted_from_one in (kv_made, kv_summed, h_made, y_made, logits_made, down_made, tile_turned):
                pe.sem_inc(counted_from_one, ONE)
            pe.wait_ge(msg_w_loaded, 32)

            def turn_next(t, j):
                pe.wait_ge(xs_ready, t + 1)
                if not isinstance(t, int) or t >= 2:
                    pe.wait_ge(xT_kept, t - 1 + ONE)
                    pe.wait_ge(xT_ready, t - 1 + ONE)
                for c in range(CC):
                    last = pe.transpose(p45[:, bass.ds(t % 2, 1), c * P:(c + 1) * P].rearrange("p o n -> p (o n)"),
                                        xs[:, j, c * P:(c + 1) * P], ident[:, :])
                last.then_inc(xs_turned, 1)

            def message(t, j):
                pe.wait_ge(xT_ready, t + (1 + ONE))
                for c, kept, made in ((0, y0_kept, y0_made), (1, y1_kept, y1_made)):
                    pe.wait_ge(kept, t + ONE)
                    for b in range(2):
                        last = pe.matmul(pg[:, 2 * c + b, :], xTs[:, j % LG, c, :],
                                         wblk[:, c, b * 4:b * 4 + 4, :].rearrange("p r o -> p (r o)"),
                                         start=True, stop=True)
                    last.then_inc(made, 1)
            turn_next(0, 0)
            with pe.Fori(0, NT // LG // 2) as k:
                for j in range(2 * LG):
                    turn_next(k * (2 * LG) + (j + 1), (j + 1) % (2 * LG))
                    message(k * (2 * LG) + j, j)
            for j in range(LG):
                if j + 1 < LG:
                    turn_next(NT - LG + j + 1, j + 1)
                message(NT - LG + j, j)

            pe.wait_ge(const_loaded, 16 * 16)
            pe.wait_ge(zeros_ready, 2)
            pe.wait_ge(y0_kept, NT + ONE)
            pe.wait_ge(y1_kept, NT + ONE)

            def keys_made(t):
                pe.wait_ge(kvx_ready, t + 1)
                pe.wait_ge(k_ready, t + ONE)
                pe.wait_ge(v_ready, t + ONE)
                for c in range(CC):
                    last = pe.matmul(p5[:, :], kvx[:, c, :], wkvT[:, c, :], start=(c == 0), stop=(c == CC - 1))
                last.then_inc(kv_made, 1)

            def keys_summed(t):
                pe.wait_ge(k_ready, t + (1 + ONE))
                pe.wait_ge(v_ready, t + (1 + ONE))
                for c in range(CC):
                    pe.matmul(p6[:, c * KW:c * KW + P], ks[:, c * P:(c + 1) * P], vs[:, c * P:(c + 1) * P],
                              start=False, stop=False, skip_group_check=True)
                    last = pe.matmul(p6[:, c * KW + P:c * KW + P + 1], ks[:, c * P:(c + 1) * P],
                                     nodemask[:, bass.ds(t, 1)], start=False, stop=False, skip_group_check=True)
                last.then_inc(kv_summed, 1)
            pe.matmul(p6[:, 0:C], zeros[:, 0:P], zeros[:, :], start=True, stop=False, skip_group_check=True)
            pe.matmul(p6[:, C:2 * C], zeros[:, 0:P], zeros[:, :], start=False, stop=False, skip_group_check=True)

            def mix_q(i, n):
                w = n * P
                pe.wait_ge(eq_ready, i + ONE)
                pe.wait_ge(q_ready, i + ONE)
                for m in range(CC):
                    for c in range(CC):
                        last = pe.matmul(p4[:, m * 2 * P:m * 2 * P + w], wqT[:, c, m * P:(m + 1) * P],
                                         xnT[:, bass.ds(2 * i, n), c, :], start=(c == 0), stop=(c == CC - 1))
                last.then_inc(q_made, 1)

            def mix_t(i, n):
                pe.wait_ge(q_ready, i + (1 + ONE))
                for k in range(n):
                    for m in range(CC):
                        last = pe.matmul((p4, p7)[k][:, m * KW:(m + 1) * KW], qs[:, m, k * P:(k + 1) * P],
                                         kvr[:, m, :], start=True, stop=True)
                last.then_inc(t_made, 1)

            def mix_turn(i, n):
                pe.wait_ge(x1_ready, 2 * i + n)
                for k in range(n):
                    for c in range(CC):
                        last = pe.transpose(p5[:, (k * CC + c) * P:(k * CC + c + 1) * P],
                                            x1[:, k, c * P:(c + 1) * P], ident[:, :])
                last.then_inc(x1_turned, 1)

            def mix_hidden(i, n):
                w = n * P
                pe.wait_ge(x1T_ready, i + 1)
                for m in range(CC):
                    for c in range(CC):
                        last = pe.matmul(p7[:, m * 2 * P:m * 2 * P + w], w1T[:, c, m * P:(m + 1) * P],
                                         x1T[:, 0:n, c, :], start=(c == 0), stop=(c == CC - 1))
                last.then_inc(h_made, 1)

            def mix_y(i, n):
                pe.wait_ge(h_ready, CC * (i + 1) if isinstance(i, int) else i * CC + CC)
                for k in range(n):
                    for m in range(CC):
                        pe.matmul(p6[:, k * C:(k + 1) * C], hs[:, m, k * P:(k + 1) * P], w2T[:, m, :],
                                  start=(m == 0), stop=False)
                    last = pe.matmul(p6[:, k * C:(k + 1) * C], ones[0:1, :], vecs[0:1, 2, :], start=False, stop=True)
                last.then_inc(y_made, 1)

            pe.matmul(p7[:, 0:C], zeros[:, 0:P], zeros[:, :], start=True, stop=True).then_inc(onehot_used, 1)
            for k in range(LAG):
                pe.matmul(pg[:, 4 - LAG + k, 0:C], zeros[:, 0:P], zeros[:, :], start=True, stop=True)\
                  .then_inc(pair_done, 1)
            pair = pe.alloc_register("pe_pair")
            pe.reg_mov(pair, 0)
            bounds = [pe.alloc_register(f"pe_bound{k}") for k in range(2 * SLOTS)]

            def load_bounds(r, groups=SLOTS):
                pe.load(bounds[0:2 * groups], ranges[0:1, bass.ds(r * (2 * SLOTS), 2 * groups)])
            pe.wait_ge(ranges_loaded, 16)

            def edges(r, s):
                pe.wait_ge(weighed, r * (SLOTS * GT) + (s * GT + GT))
                alone(pe)
                with pe.Fori(pe.snap(bounds[2 * s], min_val=0, max_val=NT - 1),
                             pe.snap(bounds[2 * s + 1], min_val=1, max_val=NT)):
                    p = pe.snap(pair, min_val=0, max_val=NG * NT)
                    pe.wait_ge(pair_added, p + ONE)
                    for j in range(GT):
                        if j % HALF == 0:
                            pe.wait_ge(onehot_ready, p * (GT // HALF) + (j // HALF + 1))
                        mm = pe.matmul(pg[:, bass.ds(p % 4, 1), 0:C], oh[:, s % 2, j, :], ring[:, s, j, :],
                                       start=(j == 0), stop=(j == GT - 1))
                        if j == HALF - 1:
                            mm.then_inc(onehot_used, 1)
                    mm.then_inc(pair_done, 1)
                    pe.reg_add(pair, pair, 1)

            with pe.Fori(0, KEY_ROUNDS) as r:
                load_bounds(r)
                for s in range(SLOTS):
                    keys_made(r * SLOTS + s)
                    edges(r, s)
                    keys_summed(r * SLOTS + s)

            def mix_round(i, r, n, before, following=0, groups=SLOTS):
                load_bounds(r, groups)
                edges(r, 0)
                if before:
                    pe.wait_ge(h_ready, i * CC)
                mix_t(i, n)
                edges(r, 1)
                if before:
                    mix_y(i - 1, 2)
                for s in range(2, groups):
                    if s == QUERY_GROUP and following:
                        pe.wait_ge(stats1, i * 2 + n)
                        mix_q(i + 1, following)
                    if s == SLOTS - 1:
                        mix_turn(i, n)
                    edges(r, s)
                if groups == SLOTS:
                    mix_hidden(i, n)
            load_bounds(KEY_ROUNDS)
            keys_made(NT - 1)
            mix_q(0, 2)
            edges(KEY_ROUNDS, 0)
            keys_summed(NT - 1)
            for s in range(1, SLOTS):
                edges(KEY_ROUNDS, s)
                if s == 2:
                    pe.wait_ge(kvr_ready, 1)
                    mix_t(0, 2)
                if s == SLOTS - 2:
                    pe.wait_ge(stats1, 2)
                    mix_q(1, 2)
                    mix_turn(0, 2)
            mix_hidden(0, 2)
            with pe.Fori(1, NT // 2 - 1) as i:
                mix_round(i, i + KEY_ROUNDS, 2, True, 2)
            mix_round(NT // 2 - 1, ROUNDS - 1, 2, True, 1)
            mix_round(NT // 2, ROUNDS, 1, True, groups=TAIL)

            def rows_turn(g):
                pe.wait_ge(rows_ready, LG * (g + 1))
                pe.wait_ge(rowsT_ready, 3 * g + ONE)
                for j in range(LG):
                    bank = (p5[:, :], p4[:, :], pg[:, 3, :])[j // 2]
                    for c in range(CC):
                        q = j % 2 * C + c * P
                        last = pe.transpose(bank[:, q:q + P], rows[:, g, j, c * P:(c + 1) * P], ident[:, :])
                last.then_inc(rows_turned, 1)

            def gate(g):
                pe.wait_ge(rowsT_ready, 3 * g + (3 + ONE))
                pe.wait_ge(gap_ready, g + ONE)
                for j in range(LG):
                    for c in range(CC):
                        last = pe.matmul(pg[:, 2, j * X:(j + 1) * X], xfT[:, j, c, :], wg[:, c, :],
                                         start=(c == 0), stop=(c == CC - 1))
                last.then_inc(logits_made, 1)

            def rank(g):
                pe.wait_ge(both_ready, g + 1)
                pe.matmul(pg[:, 0, 0:LG * X], upper[:, :], both.rearrange("p j e -> p (j e)"), start=True, stop=False)
                pe.matmul(pg[:, 0, 0:LG * X], ones[:, :], before[:, 0:LG, :].rearrange("p j e -> p (j e)"),
                          start=False, stop=True).then_inc(rank_made, 1)
            rows_turn(0)
            for g in range(NT // LG):
                gate(g)
                if g == 0:
                    mix_turn(NT // 2, 1)
                    mix_hidden(NT // 2, 1)
                if g == 1:
                    mix_y(NT // 2, 1)
                if g + 1 < NT // LG:
                    rows_turn(g + 1)
                rank(g)
            pe.wait_ge(total_made, 1)
            pe.matmul(pg[:, 0, 0:X], ones[:, :], before[:, LG, :], start=True, stop=True).then_inc(total_done, 1)

            def turn(n):
                pe.wait_ge(tile_loaded, 16 * n + 16)
                pe.wait_ge(tileT_ready, n)
                for c in range(CC):
                    last = pe.transpose(p4[:, c * P:(c + 1) * P], xin[:, c * P:(c + 1) * P], ident[:, :])
                last.then_inc(tile_turned, 1)
            k = pe.alloc_register("pe_tile")
            pe.reg_mov(k, 0)
            cnt = pe.alloc_register("pe_count")
            pe.wait_ge(counts_ready, 2)
            turn(0)

            def expert(e, s, visit):
                w1, w2 = ew_sets[s]
                pe.load(cnt, tilesi[0:1, bass.ds(e, 1)])
                pe.wait_ge(weights_loaded[s], 32 * visit + 32)
                alone(pe)
                with pe.Fori(0, pe.snap(cnt, min_val=1, max_val=NT)):
                    n = pe.snap(k, min_val=0, max_val=X * NT)
                    pe.wait_ge(tileT_ready, n + 1)
                    pe.wait_ge(act_ready, n * MC + ONE)
                    for m in range(MC):
                        if m >= 4:
                            pe.wait_ge(act_ready, n * MC + (m - 3 + ONE))
                        for c in range(CC):
                            mm = pe.matmul(hbank[m % 4][:, m // 4 * P:m // 4 * P + P], w1[:, c, m * P:(m + 1) * P],
                                           xeT[:, c, :], start=(c == 0), stop=(c == CC - 1))
                        mm.then_inc(up_made, 1)
                    turn(n + 1)
                    pe.wait_ge(result_ready, n + ONE)
                    for m in range(MC):
                        pe.wait_ge(act_ready, n * MC + (m + 1 + ONE))
                        mm = pe.matmul(pg[:, 2, 0:C], h[:, m, :], w2[:, m, :], start=(m == 0), stop=(m == MC - 1))
                    mm.then_inc(down_made, 1)
                    pe.reg_add(k, k, 1)
                pe.matmul(p7[:, 0:1], zeros[:, 0:P], zeros[:, 0:1], start=True, stop=True).then_inc(weights_used[s], 1)
            with pe.Fori(0, X // 2) as visit:
                expert(visit * 2, 0, visit)
                expert(visit * 2 + 1, 1, visit)

        @block.vector
        def _(dve):
            for counted_from_one in (y1_kept, k_ready, q_ready, gap_ready, pair_added, meta_ready, result_ready):
                dve.sem_inc(counted_from_one, ONE)
            dve.memset(zeros[:, :], 0.0).then_inc(zeros_ready, 1)
            dve.memset(eps[:, :], EPS_LN).then_inc(zeros_ready, 1)

            def norm_stats(g):
                ch = Chain(dve, dve_a, g * A_STEPS)
                w = LG

                def tiles(j):
                    return acc[:, bass.ds(g * LG + j, 1), :].rearrange("p o c -> p (o c)")
                for j in range(w):
                    ch.step(dve.bn_stats(st[:, j, :], tiles(j)))
                ch.wait(apart=True)
                for j in range(w):
                    ch.step(dve.bn_aggr(mv[:, j, :], st[:, j, :]))
                ch.wait()
                dve.tensor_scalar(var[:, 0:w], mv[:, 0:w, 1], EPS_LN, None, ALU.add).then_inc(var_ready, 1)
                assert ch.n == A_STEPS

            def stats(ch, tiles, w, st, mv, done):
                for j in range(w):
                    ch.step(dve.bn_stats(st[:, j, :], tiles(j)))
                ch.wait(apart=True)
                for j in range(w):
                    dve.bn_aggr(mv[:, j, :], st[:, j, :]).then_inc(done, 1)

            def evict(g, j):
                dve.wait_ge(y1_made, g * LG + (j + 1))
                if not isinstance(g, int):
                    dve.wait_ge(y_stored[j], g * 16)
                dve.tensor_copy(ys[:, j, :, P:2 * P], pg[:, 2:4, :].rearrange("p b (r o) -> p (b r) o", o=P))\
                   .then_inc(y1_kept, 1)

            def normed(g, at):
                dve.wait_ge(rs_ready, g + 1)
                if not isinstance(g, int) or g >= 2:
                    dve.wait_ge(xs_turned, g * LG - LG)
                    dve.wait_ge(xn_kept, g * LG - LG)
                for j in range(LG):
                    dve.tensor_scalar(xs[:, bass.ds(at + j, 1), :].rearrange("p o c -> p (o c)"), acc[:, bass.ds(g * LG + j, 1), :].rearrange("p o c -> p (o c)"),
                                      mv[:, j, 0:1], rs[:, j:j + 1], ALU.subtract, ALU.mult).then_inc(xs_ready, 1)
            dve.wait_ge(x_first, 16)
            norm_stats(0)
            normed(0, 0)
            evict(0, 0)
            dve.wait_ge(x_rest, 16 * (NT // LG - 1))
            norm_stats(1)
            evict(0, 1)
            normed(1, LG)
            evict(0, 2)
            norm_stats(2)
            evict(0, 3)
            normed(2, 0)
            evict(0, 4)
            dve.wait_ge(edges_loaded, 80)
            dve.scalar_tensor_tensor(idx[:, :], srcT[:, :], float(R), relT[:, :], ALU.mult, ALU.add)\
               .then_inc(idx_ready, 1)
            dve.tensor_copy(dstf[:, :], dstT[:, :]).then_inc(dstf_ready, 1)
            ch = Chain(dve, dve_r)
            ch.step(dve.tensor_reduce(rng2[:, 0:1], dstrow[:, :], AX_X, ALU.min))
            ch.link(dve.tensor_reduce(rng2[:, 1:2], dstrow[:, :], AX_X, ALU.max))
            ch.link(dve.tensor_scalar(rng3[:, :], rng2[:, :], P.bit_length() - 1, None, ALU.arith_shift_right))
            dve.tensor_scalar(rng3[:, 1:2], rng3[:, 1:2], 1.0, None, ALU.add).then_inc(ranges_ready, 1)
            with dve.Fori(1, NT // LG - 2) as g:
                for j in range(LG):
                    if j == LG - 2:
                        norm_stats(g + 2)
                    evict(g, j)
                    if j == LG - 2:
                        normed(g + 2, (g % 2) * LG)
            with dve.Fori(NT // LG - 2, NT // LG) as g:
                for j in range(LG):
                    evict(g, j)

            pair = dve.alloc_register("dve_pair")
            dve.reg_mov(pair, 0)
            tiles = [dve.alloc_register(f"dve_tile{k}") for k in range(LAG)]
            for reg in tiles:
                dve.reg_mov(reg, 0)
            started = dve.alloc_register("dve_started")
            dve.reg_mov(started, 0)
            used = dve.alloc_register("dve_used")
            bounds = [dve.alloc_register(f"dve_bound{k}") for k in range(2 * SLOTS)]
            dve.wait_ge(ranges_loaded, 16)
            dve.wait_ge(iota_ready, 2)
            dve.wait_ge(dstf_ready, 1)
            dve.wait_ge(bias_added, NT)
            dve.wait_ge(xn_kept, NT)

            def add_pair(p):
                t = dve.snap(tiles[0], min_val=0, max_val=NT - 1)
                dve.wait_ge(pair_done, p + 1)
                dve.wait_ge(pair_added, p + ONE)
                row = acc[:, bass.ds(t, 1), :]
                dve.tensor_tensor(row, row, pg[:, bass.ds((p + (4 - LAG)) % 4, 1), 0:C], ALU.add)\
                   .then_inc(pair_added, 1)

            def shift(d):
                for k in range(LAG - 1):
                    dve.reg_mov(tiles[k], tiles[k + 1])
                if d is not None:
                    dve.reg_mov(tiles[LAG - 1], d)

            def load_bounds(r, groups=SLOTS):
                dve.load(bounds[0:2 * groups], ranges[0:1, bass.ds(r * (2 * SLOTS), 2 * groups)])

            def edges(r, s):
                dve.reg_mov(used, started)
                dve.reg_mov(started, pair)
                with dve.Fori(dve.snap(bounds[2 * s], min_val=0, max_val=NT - 1),
                              dve.snap(bounds[2 * s + 1], min_val=1, max_val=NT)) as d:
                    p = dve.snap(pair, min_val=0, max_val=NG * NT)
                    free = dve.snap(used, min_val=0, max_val=NG * NT)
                    for j in range(0, GT, HALF):
                        if j == 0:
                            dve.wait_ge(onehot_used, free + 1)
                        else:
                            dve.wait_ge(pair_done, free + LAG)
                        col = r * (SLOTS * GT) + (s * GT + j)
                        dve.tensor_tensor(oh[:, s % 2, j:j + HALF, :],
                                          iota[:, bass.ds(d * P, P)].unsqueeze(1).to_broadcast([P, HALF, P]),
                                          dstf[:, bass.ds(col, HALF)].unsqueeze(2).to_broadcast([P, HALF, P]),
                                          ALU.is_equal).then_inc(onehot_ready, 1)
                    add_pair(p)
                    shift(d)
                    dve.reg_add(pair, pair, 1)
                    dve.reg_mov(used, pair)
                dve.sem_inc(group_used[s - LAG], 1)

            def keys(t):
                dve.wait_ge(ek_ready, t + 1)
                dve.wait_ge(kv_summed, t + ONE)
                dve.wait_ge(v_ready, t + (1 + ONE))
                dve.scalar_tensor_tensor(ks, p5[:, 0:C], 0.0, ek[:, 0:C], ALU.max, ALU.add).then_inc(k_ready, 1)
            with dve.Fori(0, KEY_ROUNDS) as r:
                load_bounds(r)
                for s in range(SLOTS):
                    edges(r, s)
                    keys(r * SLOTS + s)

            def norm_apply(ch, src, n, mean, sd, gain):
                ch.step(dve.reciprocal(sd[:, 0:n], sd[:, 0:n]))
                for k in range(n):
                    ch.step(dve.scalar_tensor_tensor(src[:, k, :], src[:, k, :], mean[:, k, 0:1], vecs[:, gain, :],
                                                     ALU.subtract, ALU.mult))
                ch.wait()

            def two(v, w):
                return v.rearrange("p (m n) -> p m n", m=CC)[:, :, 0:w]

            def mix_q(i, n):
                w = n * P
                dve.wait_ge(eq_ready, i + (1 + ONE))
                dve.scalar_tensor_tensor(qs[:, :, 0:w], two(p4[:, :], w), 0.0, two(ek, w), ALU.max, ALU.add)\
                   .then_inc(q_ready, 1)

            def mix_t(i, n):
                ch = Chain(dve, dve_c, i * C_STEPS)
                dve.wait_ge(t_made, i + 1)
                tt = [(p4, p7)[k][:, 0:CC * KW].rearrange("p (m k) -> p m k", m=CC) for k in range(n)]
                for k in range(n):
                    ch.step(dve.tensor_scalar(z[:, k, :].rearrange("p (m h) -> p m h", m=CC), tt[k][:, :, P:KW],
                                              EPS_ATTN, None, ALU.add))
                ch.wait()
                ch.link(dve.reciprocal(z[:, 0:n, :], z[:, 0:n, :]))
                for k in range(n):
                    zb = z[:, k, :].rearrange("p (m h) -> p m h", m=CC).unsqueeze(3).to_broadcast([P, CC, HC, HD])
                    ch.step(dve.tensor_tensor(u[:, k, :].rearrange("p (m h d) -> p m h d", m=CC, h=HC),
                                              tt[k][:, :, 0:P].rearrange("p m (h d) -> p m h d", h=HC), zb, ALU.mult))
                ch.wait()
                ch.link(dve.tensor_tensor(u[:, 0:n, :], u[:, 0:n, :], xn[:, bass.ds(2 * i, n), :], ALU.add))
                stats(ch, lambda j: u[:, j, :], n, st, mv, stats1)
                if n == 2:
                    assert ch.n == C_STEPS, ch.n

            def mix_x1(i, n):
                ch = Chain(dve, dve_e, i * E_STEPS)
                dve.wait_ge(dev1, i + 1)
                norm_apply(ch, u, n, mv, rs, 0)
                for k in range(n):
                    dve.scalar_tensor_tensor(x1[:, k, :], u[:, k, :], rs[:, k:k + 1], vecs[:, 1, :],
                                             ALU.mult, ALU.add).then_inc(x1_ready, 1)
                if n == 2:
                    assert ch.n == E_STEPS, ch.n

            def mix_y(i, n):
                ch = Chain(dve, dve_f, i * F_STEPS)
                dve.wait_ge(y_made, i + (1 + ONE))
                ch.link(dve.tensor_tensor(u2[:, 0:n, :], p6[:, 0:n * C].rearrange("p (i c) -> p i c", i=n),
                                          x1[:, 0:n, :], ALU.add))
                stats(ch, lambda j: u2[:, j, :], n, st2, mv2, stats2)
                if n == 2:
                    assert ch.n == F_STEPS, ch.n

            def mix_out(i, n):
                ch = Chain(dve, dve_g, i * E_STEPS)
                dve.wait_ge(dev2, i + 1)
                norm_apply(ch, u2, n, mv2, rs2, 3)
                dve.wait_ge(pair_added, dve.snap(pair, min_val=0, max_val=NG * NT) + ONE)
                for k in range(n):
                    row = acc[:, bass.ds(2 * i + k, 1), :].rearrange("p o c -> p (o c)")
                    dve.scalar_tensor_tensor(row, u2[:, k, :], rs2[:, k:k + 1], row, ALU.mult, ALU.add)\
                       .then_inc(mix_done, 1)
                dve.wait_ge(mix_done, 2 * i + n)

            def mix_round(i, r, n, before, groups=SLOTS):
                load_bounds(r, groups)
                mix_q(i, n)
                for s in range(groups):
                    edges(r, s)
                    if s == 1:
                        mix_t(i, n)
                    if s == 2:
                        if before:
                            mix_y(i - 1, 2)
                    if s == 3:
                        mix_x1(i, n)
                    if s == 4:
                        if before:
                            mix_out(i - 1, 2)

            def attention_state():
                dve.wait_ge(kv_summed, NT + ONE)
                for c in range(CC):
                    dve.tensor_tensor(kvr[:, c, 0:P], p6[:, c * KW:c * KW + P], blockmask[:, 0:P], ALU.mult)\
                       .then_inc(dve_r, 1)
                    dve.tensor_tensor(kvr[:, c, P:KW], blockmask[:, P:KW],
                                      p6[:, c * KW + P:c * KW + P + 1].to_broadcast([P, HC]), ALU.mult).then_inc(dve_r, 1)
                dve.wait_ge(dve_r, 3 + 2 * CC)
                alone(dve)
                dve.engine_nop().then_inc(kvr_ready, 1)

            load_bounds(KEY_ROUNDS)
            edges(KEY_ROUNDS, 0)
            keys(NT - 1)
            edges(KEY_ROUNDS, 1)
            attention_state()
            mix_q(0, 2)
            edges(KEY_ROUNDS, 2)
            edges(KEY_ROUNDS, 3)
            mix_t(0, 2)
            edges(KEY_ROUNDS, 4)
            mix_x1(0, 2)
            edges(KEY_ROUNDS, 5)
            with dve.Fori(1, NT // 2) as i:
                mix_round(i, i + KEY_ROUNDS, 2, True)
            mix_round(NT // 2, ROUNDS, 1, True, TAIL)
            for k in range(LAG):
                add_pair(dve.snap(pair, min_val=0, max_val=NG * NT))
                shift(None)
                dve.reg_add(pair, pair, 1)

            def bc(v, n):
                return v.unsqueeze(1).to_broadcast([P, n, X])
            cd = Chain(dve, dve_d0)
            cd.link(dve.memset(before[:, LG, :], 0.0))
            cd.link(dve.memset(rows[:, :, :, C:ROW], 0.0))
            for g in range(NT // LG):
                cd.step(dve.tensor_copy(rows[:, g, :, TOK], tokid[:, g * LG:(g + 1) * LG]))

            def rows_scale(g):
                t = slice(g * LG, (g + 1) * LG)
                dve.wait_ge(dev3, g + 1)
                cr.link(dve.reciprocal(rs3[:, t], rs3[:, t]))
                cr.step(dve.scalar_tensor_tensor(shift_by[:, t], mv3[:, t, 0], -1.0, rs3[:, t], ALU.mult, ALU.mult))
                cr.wait()
                alone(dve)
                dve.engine_nop().then_inc(rows_shift, 1)

            def dispatch(g):
                s = g
                ch = Chain(dve, dve_d, g * D_STEPS)
                dve.wait_ge(logits_made, g + (1 + ONE))
                ch.link(dve.tensor_tensor(lg, pg[:, 2, 0:LG * X].rearrange("p (j e) -> p j e", j=LG), bc(bg[:, :], LG),
                                          ALU.add), apart=True)
                for j in range(LG):
                    ch.step(dve.max(mx[:, j, :], lg[:, j, :]))
                ch.wait(apart=True)
                for j in range(LG):
                    ch.step(dve.max_index(ix[:, j, :], mx[:, j, :], lg[:, j, :]))
                ch.step(dve.tensor_tensor(gap, mx[:, :, 1], mx[:, :, 0], ALU.subtract))
                ch.wait()
                alone(dve)
                dve.engine_nop().then_inc(gap_ready, 1)
                ch.link(dve.tensor_copy(rows[:, s, :, EX:EX + 2], ix[:, :, 0:2]))
                for k, o1 in ((0, oh1), (1, oh2)):
                    ch.step(dve.tensor_tensor(o1, bc(iota8[:, :], LG),
                                              rows[:, s, :, EX + k:EX + k + 1].to_broadcast([P, LG, X]), ALU.is_equal))
                ch.wait()
                ch.step(dve.tensor_tensor(both, oh1, oh2, ALU.add))
                ch.link(dve.tensor_copy(before[:, 0, :], before[:, LG, :]))
                for j in range(LG):
                    ins = dve.tensor_tensor(before[:, j + 1, :], before[:, j, :], both[:, j, :], ALU.add)
                    ch.link(ins)
                alone(dve)
                dve.engine_nop().then_inc(both_ready, 1)
                dve.wait_ge(ex_ready, g + 1)
                ch.link(dve.tensor_scalar(den, ex, 1.0, None, ALU.add))
                ch.link(dve.reciprocal(rows[:, s, :, WT], den))
                ch.step(dve.tensor_tensor(rows[:, s, :, WT + 1], ex, rows[:, s, :, WT], ALU.mult))
                dve.wait_ge(rank_made, g + 1)
                ch.link(dve.tensor_tensor(place, pg[:, 0, 0:LG * X].rearrange("p (j e) -> p j e", j=LG),
                                          bc(capcol[:, :], LG), ALU.add))
                for k, o1 in ((0, oh1), (1, oh2)):
                    ch.link(dve.tensor_tensor(pick, o1, place, ALU.mult))
                    ch.link(dve.tensor_reduce(slotf[:, k, :], pick, AX_X, ALU.add))
                ch.link(dve.tensor_copy(sloti[:, s, :, :], slotf))
                alone(dve)
                dve.engine_nop().then_inc(slots_ready, 1)
                assert ch.n == D_STEPS, ch.n
            def row_stats(g):
                stats(cs, lambda j: acc[:, g * LG + j, :], LG, st, mv3[:, g * LG:(g + 1) * LG, :], stats3)
            cs, cr = Chain(dve, dve_s), Chain(dve, dve_rows)
            last = NT // 2
            row_stats(0)
            rows_scale(0)
            mix_y(last - 1, 2)
            mix_x1(last, 1)
            row_stats(1)
            mix_out(last - 1, 2)
            rows_scale(1)
            row_stats(2)
            dispatch(0)
            rows_scale(2)
            row_stats(3)
            dispatch(1)
            mix_y(last, 1)
            rows_scale(3)
            mix_out(last, 1)
            alone(dve)
            dve.engine_nop().then_inc(total_ready, 1)
            row_stats(4)
            dispatch(2)
            rows_scale(4)
            dispatch(3)
            dispatch(4)
            alone(dve)
            dve.engine_nop().then_inc(total_made, 1)
            dve.wait_ge(total_done, 1)
            cd.link(dve.tensor_copy(countf, pg[:, 0, 0:X]))
            dve.tensor_copy(counti[:, :], countf).then_inc(counts_ready, 1)
            cd.link(dve.tensor_scalar(countf, countf, float(P - 1), float(P), ALU.add, ALU.max))
            cd.link(dve.tensor_copy(tilesi[:, :], countf))
            dve.tensor_scalar(tilesi[:, :], tilesi[:, :], P.bit_length() - 1, None, ALU.arith_shift_right)\
               .then_inc(counts_ready, 1)

            k = dve.alloc_register("dve_tile")
            dve.reg_mov(k, 0)
            cnt = dve.alloc_register("dve_count")
            dve.wait_ge(counts_ready, 2)

            def turned(n):
                dve.wait_ge(tile_turned, n + (1 + ONE))
                dve.tensor_copy(xeT.rearrange("p c n -> p (c n)"), p4[:, 0:C]).then_inc(tileT_ready, 1)

            def meta_kept(n):
                dve.wait_ge(tile_loaded, 16 * n + 16)
                dve.tensor_copy(meta, xin[:, C:ROW]).then_inc(meta_ready, 1)
            turned(0)
            meta_kept(0)

            M_STEPS = 6

            def expert(e, s, visit):
                dve.load(cnt, tilesi[0:1, bass.ds(e, 1)])
                with dve.Fori(0, dve.snap(cnt, min_val=1, max_val=NT)):
                    n = dve.snap(k, min_val=0, max_val=X * NT)
                    ch = Chain(dve, dve_m, n * M_STEPS)
                    dve.wait_ge(meta_ready, n + (1 + ONE))
                    ch.link(dve.tensor_scalar(same, meta[:, EX - C:EX - C + 2], iota8[:, bass.ds(e, 1)], None,
                                              ALU.is_equal))
                    ch.link(dve.tensor_tensor(wsel[:, 0:2], same, meta[:, WT - C:WT - C + 2], ALU.mult))
                    ch.link(dve.tensor_tensor(wsel[:, 2:3], wsel[:, 0:1], wsel[:, 1:2], ALU.add))
                    dve.wait_ge(up_made, n * MC + MC)
                    turned(n + 1)
                    dve.wait_ge(tile_added, n + ONE)
                    ch.link(dve.tensor_copy(toki[:, :], meta[:, TOK - C:TOK - C + 1]))
                    meta_kept(n + 1)
                    dve.wait_ge(down_made, n + (1 + ONE))
                    ch.link(dve.tensor_tensor(yt, pg[:, 2, 0:C], eb2[:, bass.ds(e, 1), :].rearrange("p o c -> p (o c)"),
                                              ALU.add))
                    ch.link(dve.tensor_scalar(yo, yt, wsel[:, 2:3], None, ALU.mult))
                    alone(dve)
                    dve.engine_nop().then_inc(result_ready, 1)
                    assert ch.n == M_STEPS
                    dve.reg_add(k, k, 1)
            with dve.Fori(0, X // 2) as visit:
                expert(visit * 2, 0, visit)
                expert(visit * 2 + 1, 1, visit)


def kernel(**inputs):
    import numpy as np
    import concourse.bacc as bacc
    from concourse.bass_utils import run_bass_kernel_spmd

    g = {k: np.ascontiguousarray(np.asarray(v)) for k, v in inputs.items()}
    f32 = np.float32

    def pad(v, n, fill=0):
        o = np.full((n,) + v.shape[1:], fill, v.dtype)
        o[:v.shape[0]] = v
        return o

    def turned(v):
        return np.ascontiguousarray(v.reshape(GP * GT, P).T)

    def chunks(w, n):
        return np.ascontiguousarray(w.reshape(n, P, -1).transpose(1, 0, 2))

    def rows(v):
        return np.ascontiguousarray(np.broadcast_to(v, (P,) + v.shape))

    src, rel = (pad(g[k], GP * GT * P) for k in ("src", "edge_type_8"))
    dst = pad(g["dst"], GP * GT * P, N - 1)
    gw = g["L0_gnn_weight"].reshape(R, CC, HC, HD, HD)
    wblk = np.zeros((P, CC, R, P), f32)
    for c in range(CC):
        for b in range(HC):
            for r in range(R):
                wblk[b * HD:(b + 1) * HD, c, r, b * HD:(b + 1) * HD] = gw[r, c, b]
    wqkv = g["L0_mix_Wqkv"].T
    blockmask = np.zeros((P, KW), f32)
    for b in range(HC):
        blockmask[b * HD:(b + 1) * HD, b * HD:(b + 1) * HD] = 1
        blockmask[b * HD:(b + 1) * HD, P + b] = 1
    padrows = np.zeros((P, ROW), f32)
    padrows[:, TOK] = NP + np.arange(P)
    padrows[:, EX:EX + 2] = -1
    arrays = {
        "x": pad(g["x"], NP),
        "srcT": turned(src), "relT": turned(rel), "dstT": turned(dst), "ewT": turned(pad(g["edge_weight"], GP * GT * P)),
        "dstrow": np.ascontiguousarray(dst.reshape(GP, GT * P)[0:NG]),
        "wblk": wblk,
        "ident": np.eye(P, dtype=f32), "upper": np.triu(np.ones((P, P), f32), 1), "ones": np.ones((P, P), f32),
        "blockmask": blockmask,
        "nodemask": np.ascontiguousarray((np.arange(NP) < N).astype(f32).reshape(NT, P).T),
        "vecs": rows(np.stack([g["L0_mix_ln1_g"], g["L0_mix_ln1_b"], g["L0_mix_b2"], g["L0_mix_ln2_g"],
                               g["L0_mix_ln2_b"]])),
        "b1T": np.ascontiguousarray(g["L0_mix_b1"].reshape(CC, P).T),
        "wqT": chunks(wqkv[:, 0:C], CC), "wkvT": chunks(wqkv[:, C:3 * C], CC),
        "w1T": chunks(g["L0_mix_W1"].T, CC), "w2T": chunks(g["L0_mix_W2"].T, CC),
        "wg": chunks(g["L0_ffn_Wg"], CC), "bg": rows(g["L0_ffn_bg"]),
        "eb1T": np.ascontiguousarray(g["L0_ffn_b1"].reshape(X, MC, P).transpose(2, 0, 1)),
        "capcol": rows(np.arange(X, dtype=f32) * CAP), "iota8": rows(np.arange(X, dtype=f32)),
        "padrows": padrows,
        "ew1": np.ascontiguousarray(g["L0_ffn_W1"].reshape(X, CC, P, HID).transpose(0, 2, 1, 3)),
        "ew2": np.ascontiguousarray(g["L0_ffn_W2"].reshape(X, MC, P, C).transpose(0, 2, 1, 3)),
        "eb2": rows(g["L0_ffn_b2"]),
    }
    nc = bacc.Bacc("TRN2", target_bir_lowering=False, num_devices=1)
    args = {n: nc.dram_tensor(f"in_{n}", v.shape, mybir.dt.from_np(v.dtype), kind="ExternalInput").ap()
            for n, v in arrays.items()}
    out = nc.dram_tensor("out", [NP + P, C], F32, kind="ExternalOutput").ap()
    build(nc, args, out)
    r = run_bass_kernel_spmd(nc, [{f"in_{n}": v for n, v in arrays.items()}], core_ids=[0])
    return r.results[0]["out"][0:N]
```

```python
from contextlib import ExitStack

import concourse.bass as bass
from concourse import mybir

F32 = mybir.dt.float32
I32 = mybir.dt.int32
U32 = mybir.dt.uint32
ALU = mybir.AluOpType
ACT = mybir.ActivationFunctionType
AX_X = mybir.AxisListType.X

P = 128
N, C = 3125, 256
NT = -(-N // P)
NP = NT * P
CC = C // P
E = 50000
GT = 4
HALF = GT // 2
NG = -(-E // (GT * P))
SLOTS = 6
ROUNDS = NG // SLOTS
TAIL = NG % SLOTS
LEAD = 3
LAG = 2
GP = (ROUNDS + 1) * SLOTS
R = 8
HEADS = 8
HC = HEADS // CC
HD = C // HEADS
KW = P + HC
X = 8
HID = 1024
MC = HID // P
EPS_LN = 1e-5
EPS_ATTN = 1e-6
LG = 5
KEY_ROUNDS = (NT - 1) // SLOTS
QUERY_GROUP = 3
CAP = NP + P
ROW = 264
TOK, WT, EX = C, C + 1, C + 3

ARENA = 2 * LG * C + LG * C + CC * R * P + LG * R * C


def build(nc, a, out):
    assert NT == LG * LG and NT % 2 and TAIL == 2 and ROUNDS % 2 == 0
    assert KEY_ROUNDS * SLOTS == NT - 1 and ROUNDS - KEY_ROUNDS == NT // 2
    ctx = ExitStack()
    with ctx:
        def sb(name, shape, dt=F32):
            return ctx.enter_context(nc.sbuf_tensor(name, shape, dt))

        def pb(name, shape):
            return ctx.enter_context(nc.psum_tensor(name, shape, F32))

        def sem(name):
            return ctx.enter_context(nc.semaphore(name))

        y_dram = nc.dram_tensor("rel_messages", [NP * R, C], F32, kind="Internal").ap()
        range_dram = nc.dram_tensor("group_ranges", [NG, 2], I32, kind="Internal").ap()
        slot_dram = nc.dram_tensor("expert_rows", [X * CAP, ROW], F32, kind="Internal").ap()

        acc = sb("acc", [P, NT, C])
        xn = sb("xn", [P, NT, C])
        xnT = sb("xnT", [P, NT, CC, P])
        ident = sb("ident", [P, P])
        upper = sb("upper", [P, P])
        ones = sb("ones", [P, P])
        blockmask = sb("blockmask", [P, KW])
        nodemask = sb("nodemask", [P, 1])
        vecs = sb("vecs", [P, 5, C])
        b1T = sb("b1T", [P, CC])
        wqT = sb("wqT", [P, CC, C])
        wkvT = sb("wkvT", [P, CC, 2 * C])
        w1T = sb("w1T", [P, CC, C])
        w2T = sb("w2T", [P, CC, C])
        wg = sb("wg", [P, CC, X])
        bg = sb("bg", [P, X])
        eb1T = sb("eb1T", [P, X, MC])
        eb2 = sb("eb2", [P, X, C])
        capcol = sb("capcol", [P, X])
        iota8 = sb("iota8", [P, X])
        padrows = sb("padrows", [P, ROW])
        srcT = sb("srcT", [P, GP * GT], I32)
        relT = sb("relT", [P, GP * GT], I32)
        dstT = sb("dstT", [P, GP * GT], I32)
        idx = sb("idx", [P, GP * GT], I32)
        dstf = sb("dstf", [P, GP * GT])
        ew = sb("ew", [P, GP * GT])
        dstrow = sb("dstrow", [NG, GT * P], I32)
        rng2 = sb("rng2", [NG, 2], I32)
        rng3 = sb("rng3", [NG, 2], I32)
        ranges = sb("ranges", [1, NG * 2], I32)
        iota = sb("iota", [P, NP])
        tokid = sb("tokid", [P, NT])
        zeros = sb("zeros", [P, C])
        gidx = sb("gidx", [P, 2, SLOTS * GT], I32)
        oh = sb("oh", [P, 2, GT, P])
        st = sb("st", [P, LG, 6])
        mv = sb("mv", [P, LG, 2])
        row_mv = sb("row_mv", [P, NT, 2])
        row_dev = sb("row_dev", [P, NT])
        shift_by = sb("shift_by", [P, NT])
        rs = sb("rs", [P, LG])
        st2 = sb("st2", [P, 2, 6])
        mv2 = sb("mv2", [P, 2, 2])
        rs2 = sb("rs2", [P, 2])
        eps = sb("eps", [P, 1])
        table_use = sb("table_use", [P, 1])
        var = sb("var", [P, LG])
        minus_half = sb("minus_half", [P, LG])
        arena = sb("arena", [P, ARENA])

        def view(lo, n):
            return arena[:, lo:lo + n]
        xs = view(0, 2 * LG * C).rearrange("p (j c) -> p j c", j=2 * LG)
        o = 2 * LG * C
        xTs = view(o, LG * C).rearrange("p (s c n) -> p s c n", s=LG, c=CC)
        o += LG * C
        wblk = view(o, CC * R * P).rearrange("p (c r o) -> p c r o", c=CC, r=R)
        o += CC * R * P
        ys = view(o, LG * R * C).rearrange("p (j r c) -> p j r c", j=LG, r=R)
        assert o + LG * R * C <= ARENA
        ring = view(0, SLOTS * GT * C).rearrange("p (s j c) -> p s j c", s=SLOTS, j=GT)
        o = SLOTS * GT * C
        kvx = view(o, C).rearrange("p (c n) -> p c n", c=CC)
        ek = view(o + C, 2 * C)
        ks = view(o + 3 * C, C)
        vs = view(o + 4 * C, CC * (P + 1)).rearrange("p (c k) -> p c k", c=CC)
        o += 4 * C + CC * (P + 1)
        kvr = view(o, CC * KW).rearrange("p (c k) -> p c k", c=CC)
        o += CC * KW
        qs = view(o, 2 * C).rearrange("p (m n) -> p m n", m=CC)
        u = view(o + 2 * C, 2 * C).rearrange("p (i c) -> p i c", i=2)
        x1 = view(o + 4 * C, 2 * C).rearrange("p (i c) -> p i c", i=2)
        x1T = view(o + 6 * C, 2 * C).rearrange("p (i c n) -> p i c n", i=2, c=CC)
        hs = view(o + 8 * C, 2 * C).rearrange("p (m n) -> p m n", m=CC)
        u2 = view(o + 10 * C + 2 * HEADS, 2 * C).rearrange("p (i c) -> p i c", i=2)
        z = view(o + 10 * C, 2 * HEADS).rearrange("p (i h) -> p i h", i=2)
        o += 12 * C + 2 * HEADS
        ew_sets = []
        rows = view(0, NT * ROW).rearrange("p (s j c) -> p s j c", s=NT // LG, j=LG)
        xfT = view(o, LG * C).rearrange("p (j c n) -> p j c n", j=LG, c=CC)
        o += LG * C
        lg = view(o, LG * X).rearrange("p (j e) -> p j e", j=LG)
        mx = view(o + 40, LG * 8).rearrange("p (j e) -> p j e", j=LG)
        oh1 = view(o + 80, LG * X).rearrange("p (j e) -> p j e", j=LG)
        oh2 = view(o + 120, LG * X).rearrange("p (j e) -> p j e", j=LG)
        both = view(o + 160, LG * X).rearrange("p (j e) -> p j e", j=LG)
        before = view(o + 200, (LG + 1) * X).rearrange("p (j e) -> p j e", j=LG + 1)
        place = view(o + 248, LG * X).rearrange("p (j e) -> p j e", j=LG)
        pick = view(o + 288, LG * X).rearrange("p (j e) -> p j e", j=LG)
        gap = view(o + 328, LG)
        ex = view(o + 333, LG)
        den = view(o + 338, LG)
        slotf = view(o + 344, 2 * LG).rearrange("p (s j) -> p s j", s=2)
        countf = view(o + 354, X)
        o += 368
        ix = sb("ix", [P, LG, 8], U32)
        sloti = sb("sloti", [P, NT // LG, 2, LG], I32)
        counti = sb("counti", [P, X], I32)
        tilesi = sb("tilesi", [P, X], I32)
        toki = sb("toki", [P, 1], I32)
        meta = view(o, ROW - C)
        o += ROW - C
        xin = view(o, ROW)
        xeT = view(o + ROW, C).rearrange("p (c n) -> p c n", c=CC)
        h = view(o + ROW + C, MC * P).rearrange("p (m n) -> p m n", m=MC)
        yt = view(o + ROW + C + MC * P, C)
        yo = view(o + ROW + 2 * C + MC * P, C)
        same = view(o + ROW + 3 * C + MC * P, 2)
        wsel = view(o + ROW + 3 * C + MC * P + 4, 3)
        o += ROW + 3 * C + MC * P + 8
        assert o <= ARENA
        xn_flat = xn[:, :, :].rearrange("p t c -> p (t c)")
        xnT_flat = xnT[:, :, :, :].rearrange("p t c n -> p (t c n)")
        for flat in (xn_flat, xnT_flat):
            ew_sets.append((flat[:, 0:CC * HID].rearrange("p (c h) -> p c h", c=CC),
                            flat[:, CC * HID:CC * HID + MC * C].rearrange("p (m f) -> p m f", m=MC)))

        pg = pb("pg", [P, 4, 512])
        p45 = pb("p45", [P, 2, 512])
        p4, p5 = p45[:, 0, :], p45[:, 1, :]
        p6 = pb("p6", [P, 512])
        p7 = pb("p7", [P, 512])

        hbank = [pg[:, 0, :], pg[:, 1, :], pg[:, 3, :], p5[:, :]]

        x_first, x_rest = sem("x_first"), sem("x_rest")
        msg_w_loaded, vecs_loaded, const_loaded, edges_loaded = (
            sem("msg_w_loaded"), sem("vecs_loaded"), sem("const_loaded"), sem("edges_loaded"))
        ranges_stored, ranges_loaded = sem("ranges_stored"), sem("ranges_loaded")
        iota_ready, idx_ready, ranges_ready, zeros_ready = (sem("iota_ready"), sem("idx_ready"),
                                                            sem("ranges_ready"), sem("zeros_ready"))
        norm_step = sem("norm_step")
        xs_ready, xs_turned, xT_kept, xT_ready = sem("xs_ready"), sem("xs_turned"), sem("xT_kept"), sem("xT_ready")
        xn_kept, bias_added = sem("xn_kept"), sem("bias_added")
        y0_made, y1_made, y0_kept, y1_kept = sem("y0_made"), sem("y1_made"), sem("y0_kept"), sem("y1_kept")
        y_stored = [sem(f"y_stored{j}") for j in range(LG)]
        gathered = [sem(f"gathered{s}") for s in range(SLOTS)]
        group_used = [sem(f"group_used{s}") for s in range(SLOTS)]
        weighed, onehot_ready, onehot_used, pair_done, pair_added = (
            sem("weighed"), sem("onehot_ready"), sem("onehot_used"), sem("pair_done"), sem("pair_added"))
        kvx_ready, kv_made, ek_ready, v_ready, k_ready, kv_summed = (
            sem("kvx_ready"), sem("kv_made"), sem("ek_ready"), sem("v_ready"), sem("k_ready"), sem("kv_summed"))
        kvr_ready = sem("kvr_ready")
        q_made, eq_ready, q_ready, t_made = sem("q_made"), sem("eq_ready"), sem("q_ready"), sem("t_made")
        attention_step, x1_ready, x1_turned, x1T_ready = sem("attention_step"), sem("x1_ready"), sem("x1_turned"), sem("x1T_ready")
        h_made, h_ready, y_made, mix_done = sem("h_made"), sem("h_ready"), sem("y_made"), sem("mix_done")
        out_started, gate_step, rows_ready, rows_turned, rowsT_ready = (
            sem("out_started"), sem("gate_step"), sem("rows_ready"), sem("rows_turned"), sem("rowsT_ready"))
        logits_made, gap_ready, ex_ready, both_ready, rank_made, slots_ready = (
            sem("logits_made"), sem("gap_ready"), sem("ex_ready"), sem("both_ready"), sem("rank_made"),
            sem("slots_ready"))
        rows_sent, rows_shift = sem("rows_sent"), sem("rows_shift")
        total_ready, total_made, counts_ready, pads_sent = (sem("total_ready"), sem("total_made"),
                                                            sem("counts_ready"), sem("pads_sent"))
        weights_loaded = [sem(f"weights_loaded{s}") for s in range(2)]
        weights_used = [sem(f"weights_used{s}") for s in range(2)]
        tile_loaded, tile_turned, tileT_ready, meta_ready = (
            sem("tile_loaded"), sem("tile_turned"), sem("tileT_ready"), sem("meta_ready"))
        up_made, act_ready, down_made, result_step, result_ready, added = (
            sem("up_made"), sem("act_ready"), sem("down_made"), sem("result_step"), sem("result_ready"), sem("added"))
        var_ready, rs_ready, minus_ready = sem("var_ready"), sem("rs_ready"), sem("minus_ready")
        tile_added = sem("tile_added")
        relu_k_ready, relu_q_ready = sem("relu_k_ready"), sem("relu_q_ready")
        attention_stats, hidden_stats, row_stats_ready = (
            sem("attention_stats"), sem("hidden_stats"), sem("row_stats_ready"))
        attention_dev, hidden_dev, row_dev_ready = sem("attention_dev"), sem("hidden_dev"), sem("row_dev_ready")
        row_stats_step, row_scale_step = sem("row_stats_step"), sem("row_scale_step")
        x1_step, hidden_step, mix_out_step = sem("x1_step"), sem("hidden_step"), sem("mix_out_step")
        setup_step, dstf_ready, idx_staged, total_done, counts_step = (
            sem("setup_step"), sem("dstf_ready"), sem("idx_staged"), sem("total_done"), sem("counts_step"))

        waited = {e.engine: sem(f"waited{n}") for n, e in enumerate((nc.sync, nc.gpsimd, nc.tensor, nc.vector))}

        ONE = 1

        def alone(eng):
            eng.sem_inc(waited[eng.engine], 1)

        class Chain:

            def __init__(self, eng, s, base=0):
                self.eng, self.s, self.base, self.n = eng, s, base, 0

            def step(self, ins):
                self.n += 1
                ins.then_inc(self.s, 1)

            def wait(self, apart=False):
                self.eng.wait_ge(self.s, self.base + self.n)
                if apart:
                    alone(self.eng)

            def link(self, ins, apart=False):
                self.step(ins)
                self.wait(apart)

        A_STEPS = 2 * LG
        C_STEPS = 2 + 1 + 2 + 1 + 2
        E_STEPS = 3
        F_STEPS = 1 + 2
        D_STEPS = 16 + 3 * LG

        block = ctx.enter_context(nc.Block())

        @block.sync
        def _(sp):
            x_v = a["x"].rearrange("(t p) c -> p t c", p=P)
            sp.dma_start(acc[:, 0:LG, :], x_v[:, 0:LG, :]).then_inc(x_first, 16)
            sp.dma_start(wblk, a["wblk"]).then_inc(msg_w_loaded, 16)
            sp.dma_start(ident[:, :], a["ident"]).then_inc(msg_w_loaded, 16)
            for g in range(1, NT // LG):
                sp.dma_start(acc[:, g * LG:(g + 1) * LG, :], x_v[:, g * LG:(g + 1) * LG, :]).then_inc(x_rest, 16)
            sp.dma_start(vecs[:, :, :], a["vecs"]).then_inc(vecs_loaded, 16)
            for dst, name in ((b1T, "b1T"), (wqT, "wqT"), (wkvT, "wkvT"), (w1T, "w1T"),
                              (w2T, "w2T"), (wg, "wg"), (bg, "bg"), (eb1T, "eb1T"), (eb2, "eb2"), (capcol, "capcol"),
                              (iota8, "iota8"), (padrows, "padrows"), (upper, "upper"), (ones, "ones"),
                              (blockmask, "blockmask"), (nodemask, "nodemask")):
                sp.dma_start(dst[tuple(slice(None) for _ in a[name].shape)], a[name]).then_inc(const_loaded, 16)
            y_v = y_dram.rearrange("(t p r) c -> t p r c", p=P, r=R)

            def store_y(t, j):
                sp.wait_ge(y0_kept, t + (1 + ONE))
                sp.wait_ge(y1_kept, t + (1 + ONE))
                sp.dma_start(y_v[bass.ds(t, 1)].rearrange("o p r c -> (o p) r c"), ys[:, j, :, :])\
                  .then_inc(y_stored[j], 16)
            with sp.Fori(0, NT // LG) as g:
                for j in range(LG):
                    store_y(g * LG + j, j)
            out_v = out.rearrange("(t p) c -> p t c", p=P)
            sp.wait_ge(const_loaded, 16 * 16)
            sp.dma_start(out[NP:NP + P, :], padrows[:, 0:C]).then_inc(out_started, 16)
            sp.wait_ge(kvr_ready, 1)
            sp.wait_ge(mix_done, NT)
            sp.wait_ge(total_ready, 1)
            sp.dma_start(out_v[:, 0:NT, :], acc[:, :, :]).then_inc(out_started, 16)
            sp.wait_ge(counts_ready, 2)
            for e in range(X):
                n = sp.value_load(counti[0:1, e:e + 1], min_val=0, max_val=NP)
                sp.dma_start(slot_dram[bass.ds(n + e * CAP, P), :], padrows[:, :]).then_inc(pads_sent, 16)
            sp.wait_ge(pads_sent, 16 * X)
            sp.wait_ge(rows_sent, 16 * 2 * NT)
            k = sp.alloc_register("sp_tile")
            sp.reg_mov(k, 0)

            def load_tile(row, n):
                sp.wait_ge(tile_turned, n + ONE)
                sp.wait_ge(meta_ready, n + ONE)
                sp.dma_start(xin, slot_dram[bass.ds(row, P), :]).then_inc(tile_loaded, 16)
                sp.wait_ge(tile_loaded, 16 * n + 16)
                alone(sp)
            cnt = sp.alloc_register("sp_count")
            with sp.Fori(0, X) as e:
                sp.load(cnt, tilesi[0:1, bass.ds(e, 1)])
                with sp.Fori(0, sp.snap(cnt, min_val=1, max_val=NT)) as i:
                    n = sp.snap(k, min_val=0, max_val=X * NT)
                    load_tile(e * CAP + i * P, n)
                    sp.reg_add(k, k, 1)
            load_tile(0, sp.snap(k, min_val=0, max_val=X * NT))

        @block.gpsimd
        def _(pool):
            for counted_from_one in (tile_added,):
                pool.sem_inc(counted_from_one, ONE)

            def deviation(i, w):
                pool.wait_ge(var_ready, i + 1)
                pool.tensor_tensor(rs[:, 0:w], var[:, 0:w], minus_half[:, 0:w], ALU.pow).then_inc(rs_ready, 1)

            def keep(t, j):
                pool.wait_ge(xs_ready, t + 1)
                pool.tensor_copy(xn[:, bass.ds(t, 1), :], xs[:, bass.ds(j, 1), :]).then_inc(xn_kept, 1)
                pool.tensor_tensor(acc[:, bass.ds(t, 1), :], acc[:, bass.ds(t, 1), :], vecs[:, 4:5, :],
                                   ALU.add).then_inc(bias_added, 1)
            pool.iota(iota[:, :], pattern=[[1, NP]], base=0, channel_multiplier=0,
                      allow_small_or_imprecise_dtypes=True).then_inc(iota_ready, 1)
            pool.iota(tokid[:, :], pattern=[[P, NT]], base=0, channel_multiplier=1,
                      allow_small_or_imprecise_dtypes=True).then_inc(iota_ready, 1)
            pool.memset(minus_half[:, :], -0.5).then_inc(minus_ready, 1)
            pool.wait_ge(minus_ready, 1)
            deviation(0, LG)
            deviation(1, LG)
            pool.wait_ge(vecs_loaded, 16)
            for j in range(LG):
                keep(j, j)
            deviation(2, LG)
            with pool.Fori(1, NT // LG - 2) as g:
                for j in range(LG):
                    keep(g * LG + j, (g % 2) * LG + j)
                deviation(g + 2, LG)
            with pool.Fori(NT // LG - 2, NT // LG) as g:
                for j in range(LG):
                    keep(g * LG + j, (g % 2) * LG + j)
            pool.wait_ge(ranges_ready, 1)
            pool.dma_start(range_dram, rng3[:, :]).then_inc(ranges_stored, 16)
            pool.wait_ge(ranges_stored, 16)
            pool.dma_start(ranges[:, :], range_dram.rearrange("(o g) k -> o (g k)", o=1)).then_inc(ranges_loaded, 16)
            for j in range(LG):
                pool.wait_ge(y_stored[j], 16 * (NT // LG))
            pool.wait_ge(xn_kept, NT)
            pool.wait_ge(bias_added, NT)
            pool.wait_ge(idx_ready, 1)

            def stage(r, par):
                pool.tensor_copy(gidx[:, par, :], idx[:, bass.ds(r * (SLOTS * GT), SLOTS * GT)])\
                    .then_inc(idx_staged, 1)

            def gather(par, s):
                for j in range(GT):
                    c = s * GT + j
                    pool.indirect_dma_start(
                        out=ring[:, s, j, :], out_offset=None, in_=y_dram[:, :],
                        in_offset=bass.IndirectOffsetOnAxis(ap=gidx[:, par, c:c + 1], axis=0))\
                        .then_inc(gathered[s], 16)

            def gather_round(r, par, groups=SLOTS):
                pool.wait_ge(idx_staged, r + 1)
                for s in range(groups):
                    pool.wait_ge(group_used[s], r + (1 if s >= SLOTS - LAG else 0))
                    if s == SLOTS - 1:
                        stage(r + 1, 1 - par)
                    else:
                        alone(pool)
                    gather(par, s)
            stage(0, 0)
            stage(1, 1)
            pool.wait_ge(idx_staged, 2)
            for s in range(SLOTS):
                gather(0, s)
            gather_round(1, 1)
            with pool.Fori(1, ROUNDS // 2) as k:
                gather_round(k * 2, 0)
                gather_round(k * 2 + 1, 1)
            gather_round(ROUNDS, 0, TAIL)

            def dispatch(g):
                pool.wait_ge(slots_ready, g + 1)
                for c in range(2):
                    for j in range(LG):
                        pool.indirect_dma_start(
                            out=slot_dram[:, :],
                            out_offset=bass.IndirectOffsetOnAxis(ap=sloti[:, g, c, j:j + 1], axis=0),
                            in_=rows[:, g, j, :], in_offset=None).then_inc(rows_sent, 16)
            for g in range(NT // LG):
                dispatch(g)
            pool.wait_ge(out_started, 32)
            k = pool.alloc_register("pool_tile")
            pool.reg_mov(k, 0)
            cnt = pool.alloc_register("pool_count")
            pool.wait_ge(counts_ready, 2)
            with pool.Fori(0, X) as e:
                pool.load(cnt, tilesi[0:1, bass.ds(e, 1)])
                with pool.Fori(0, pool.snap(cnt, min_val=1, max_val=NT)) as i:
                    n = pool.snap(k, min_val=0, max_val=X * NT)
                    pool.wait_ge(result_ready, n + (1 + ONE))
                    alone(pool)
                    pool.indirect_dma_start(
                        out=out[:, :], out_offset=bass.IndirectOffsetOnAxis(ap=toki[:, 0:1], axis=0),
                        in_=yo, in_offset=None, compute_op=ALU.add).then_inc(added, 16)
                    pool.wait_ge(added, 16 * n + 16)
                    pool.sem_inc(tile_added, 1)
                    pool.reg_add(k, k, 1)

        @block.scalar
        def _(act):
            act.dma_start(dstrow[:, :], a["dstrow"]).then_inc(edges_loaded, 16)
            for dst, name in ((srcT, "srcT"), (relT, "relT"), (dstT, "dstT"), (ew, "ewT")):
                act.dma_start(dst[:, :], a[name]).then_inc(edges_loaded, 16)
            for counted_from_one in (xT_kept, xT_ready, y0_kept, v_ready, eq_ready, rowsT_ready, act_ready):
                act.sem_inc(counted_from_one, ONE)

            def turned_kept(t, j, first=False):
                act.wait_ge(xs_turned, t + 1)
                if not first:
                    act.wait_ge(y1_made, t - (LG - 1))
                bank = p45[:, bass.ds(t % 2, 1), 0:C]
                act.activation(xTs[:, j], bank.rearrange("p o (c n) -> p (o c) n", c=CC), ACT.Copy).then_inc(xT_ready, 1)
                act.activation(xnT[:, bass.ds(t, 1)].rearrange("p o c n -> p o (c n)"), bank, ACT.Copy)\
                   .then_inc(xT_kept, 1)

            def message(t, g, j):
                act.wait_ge(y0_made, t + 1)
                if g is not None:
                    act.wait_ge(y_stored[j], g * 16)
                act.activation(ys[:, j, :, 0:P], pg[:, 0:2, :].rearrange("p b (r o) -> p (b r) o", o=P),
                               ACT.Copy).then_inc(y0_kept, 1)
            turned_kept(0, 0, True)
            for j in range(1, LG):
                turned_kept(j, j, True)
                message(j - 1, None, j - 1)
            turned_kept(LG, 0)
            message(LG - 1, None, LG - 1)
            with act.Fori(1, NT // LG - 1) as g:
                for j in range(1, LG + 1):
                    turned_kept(g * LG + j, j % LG)
                    message(g * LG + (j - 1), g, j - 1)
            for t in range(NT - LG, NT):
                if t + 1 < NT:
                    turned_kept(t + 1, (t + 1) % LG)
                message(t, NT // LG - 1, t % LG)
            act.wait_ge(const_loaded, 16 * 16)
            act.wait_ge(zeros_ready, 2)

            def weigh(r, s):
                act.wait_ge(gathered[s], r * (16 * GT) + 16 * GT)
                for j in range(GT):
                    act.activation(ring[:, s, j, :], ring[:, s, j, :], ACT.Copy,
                                   scale=ew[:, bass.ds(r * (SLOTS * GT) + (s * GT + j), 1)]).then_inc(weighed, 1)

            def weigh_ahead(r, s, last=False):
                if not last or s + LEAD < SLOTS + TAIL:
                    weigh(r + (s + LEAD) // SLOTS, (s + LEAD) % SLOTS)

            def keys_turned(t):
                act.wait_ge(kv_made, t + ONE)
                act.activation(kvx, xnT[:, bass.ds(t, 1)].rearrange("p o c n -> p (o c) n"), ACT.Copy)\
                   .then_inc(kvx_ready, 1)

            def keys(t, last=False):
                act.wait_ge(kv_made, t + (1 + ONE))
                act.wait_ge(k_ready, t + ONE)
                act.activation(ek[:, 0:C], p5[:, 0:C], ACT.Relu, scale=-1.0).then_inc(relu_k_ready, 1)
                act.wait_ge(relu_k_ready, t + 1)
                act.activation(ek[:, 0:C], ek[:, 0:C], ACT.Exp, scale=-1.0).then_inc(ek_ready, 1)
                act.wait_ge(kv_summed, t + ONE)
                if last:
                    act.activation(vs[:, :, P], nodemask[:, 0:1].to_broadcast([P, CC]), ACT.Copy)
                act.activation(vs[:, :, 0:P], p5[:, C:2 * C].rearrange("p (c k) -> p c k", c=CC), ACT.Copy)\
                   .then_inc(v_ready, 1)
            act.wait_ge(xT_kept, NT + ONE)
            for j in range(LG):
                act.wait_ge(y_stored[j], 16 * (NT // LG))
            act.activation(vs[:, :, P], ones[:, 0:CC], ACT.Copy)
            keys_turned(0)
            for s in range(LEAD):
                weigh(0, s)
            with act.Fori(0, KEY_ROUNDS) as r:
                for s in range(SLOTS):
                    keys(r * SLOTS + s)
                    keys_turned(r * SLOTS + (s + 1))
                    weigh_ahead(r, s)
            keys(NT - 1, last=True)

            def two(v, w):
                return v.rearrange("p (m n) -> p m n", m=CC)[:, :, 0:w]

            def deviation(stats, seen, var, sd, made):
                act.wait_ge(stats, seen)
                act.activation(sd, var, ACT.Sqrt, bias=eps[:, :]).then_inc(made, 1)

            def mix_q(i, n):
                w = n * P
                act.wait_ge(q_made, i + 1)
                act.wait_ge(q_ready, i + ONE)
                act.activation(two(ek, w), two(p4[:, :], w), ACT.Relu, scale=-1.0).then_inc(relu_q_ready, 1)
                act.wait_ge(relu_q_ready, i + 1)
                act.activation(two(ek, w), two(ek, w), ACT.Exp, scale=-1.0).then_inc(eq_ready, 1)

            def hidden_turned(i, n):
                act.wait_ge(x1_turned, i + 1)
                act.wait_ge(h_made, i + ONE)
                act.activation(x1T[:, 0:n].rearrange("p i c n -> p (i c n)"), p5[:, 0:n * C], ACT.Copy)\
                   .then_inc(x1T_ready, 1)

            def mix_hidden(i, n):
                w = n * P
                act.wait_ge(h_made, i + (1 + ONE))
                act.wait_ge(y_made, i + ONE)
                for m in range(CC):
                    act.activation(hs[:, m, 0:w], p7[:, m * 2 * P:m * 2 * P + w], ACT.Gelu, bias=b1T[:, m:m + 1])\
                       .then_inc(h_ready, 1)

            def mix(i, r, before=True, following=2):
                def between(*groups):
                    for s in groups:
                        weigh_ahead(r, s, last=following == 1)
                between(*((0, ) if before else (0, 1)))
                deviation(attention_stats, i * 2 + 2, mv[:, 0:2, 1], rs[:, 0:2], attention_dev)
                if before:
                    between(1)
                    deviation(hidden_stats, i * 2, mv2[:, 0:2, 1], rs2[:, 0:2], hidden_dev)
                between(2)
                mix_q(i + 1, following)
                between(3)
                hidden_turned(i, 2)
                between(4)
                mix_hidden(i, 2)
                between(5)
            act.wait_ge(k_ready, NT + ONE)
            mix_q(0, 2)
            mix(0, KEY_ROUNDS, before=False)
            with act.Fori(1, NT // 2 - 1) as i:
                mix(i, i + KEY_ROUNDS)
            mix(NT // 2 - 1, ROUNDS - 1, following=1)

            def load_weights(e, s):
                w1, w2 = ew_sets[s]
                act.dma_start(w1, a["ew1"][bass.ds(e, 1)].rearrange("o p c h -> (o p) c h")).then_inc(weights_loaded[s], 16)
                act.dma_start(w2, a["ew2"][bass.ds(e, 1)].rearrange("o p m f -> (o p) m f")).then_inc(weights_loaded[s], 16)

            def turned(g):
                act.wait_ge(logits_made, g + ONE)
                for b, (v, bank) in enumerate(((xfT[:, 0:2], p5[:, :]), (xfT[:, 2:4], p4[:, :]),
                                               (xfT[:, 4:5], pg[:, 3, 0:C]))):
                    act.wait_ge(rows_turned, 3 * g + b + 1)
                    act.activation(v.rearrange("p j c n -> p (j c n)"), bank, ACT.Copy).then_inc(rowsT_ready, 1)

            def gate(g):
                act.wait_ge(gap_ready, g + (1 + ONE))
                act.activation(ex, gap, ACT.Exp).then_inc(ex_ready, 1)

            def normed_rows(g):
                act.wait_ge(rows_shift, g + 1)
                for j in range(LG):
                    act.activation(rows[:, g, j, 0:C], acc[:, g * LG + j, :], ACT.Identity,
                                   bias=shift_by[:, g * LG + j:g * LG + j + 1],
                                   scale=row_dev[:, g * LG + j:g * LG + j + 1]).then_inc(rows_ready, 1)

            def row_deviation(g):
                t = slice(g * LG, (g + 1) * LG)
                deviation(row_stats_ready, LG * (g + 1), row_mv[:, t, 1], row_dev[:, t], row_dev_ready)
            last = NT // 2
            row_deviation(0)
            deviation(attention_stats, NT, mv[:, 0:1, 1], rs[:, 0:1], attention_dev)
            normed_rows(0)
            row_deviation(1)
            turned(0)
            deviation(hidden_stats, NT - 1, mv2[:, 0:2, 1], rs2[:, 0:2], hidden_dev)
            load_weights(0, 0)
            load_weights(1, 1)
            normed_rows(1)
            turned(1)
            gate(0)
            row_deviation(2)
            normed_rows(2)
            hidden_turned(last, 1)
            row_deviation(3)
            gate(1)
            turned(2)
            mix_hidden(last, 1)
            normed_rows(3)
            gate(2)
            turned(3)
            deviation(hidden_stats, NT, mv2[:, 0:1, 1], rs2[:, 0:1], hidden_dev)
            row_deviation(4)
            normed_rows(4)
            gate(3)
            turned(4)
            gate(4)

            k = act.alloc_register("act_tile")
            act.reg_mov(k, 0)
            cnt = act.alloc_register("act_count")
            act.activation(table_use[:, :], eps[:, :], ACT.Gelu)
            act.wait_ge(counts_ready, 2)

            def expert(e):
                act.load(cnt, tilesi[0:1, bass.ds(e, 1)])
                with act.Fori(0, act.snap(cnt, min_val=1, max_val=NT)):
                    n = act.snap(k, min_val=0, max_val=X * NT)
                    act.wait_ge(down_made, n + ONE)
                    for m in range(MC):
                        act.wait_ge(up_made, n * MC + (m + 1))
                        act.activation(h[:, m, :], hbank[m % 4][:, m // 4 * P:m // 4 * P + P], ACT.Gelu,
                                       bias=eb1T[:, bass.ds(e, 1), m:m + 1].rearrange("p a b -> p (a b)"))\
                           .then_inc(act_ready, 1)
                    act.reg_add(k, k, 1)
            with act.Fori(0, X // 2 - 1) as visit:
                for s in range(2):
                    expert(visit * 2 + s)
                    act.wait_ge(weights_used[s], visit + 1)
                    load_weights(visit * 2 + (2 + s), s)
            for s in range(2):
                expert(X - 2 + s)

        @block.tensor
        def _(pe):
            for counted_from_one in (kv_made, kv_summed, h_made, y_made, logits_made, down_made, tile_turned):
                pe.sem_inc(counted_from_one, ONE)
            pe.wait_ge(msg_w_loaded, 32)

            def turn_next(t, j):
                pe.wait_ge(xs_ready, t + 1)
                if not isinstance(t, int) or t >= 2:
                    pe.wait_ge(xT_kept, t - 1 + ONE)
                    pe.wait_ge(xT_ready, t - 1 + ONE)
                for c in range(CC):
                    last = pe.transpose(p45[:, bass.ds(t % 2, 1), c * P:(c + 1) * P].rearrange("p o n -> p (o n)"),
                                        xs[:, j, c * P:(c + 1) * P], ident[:, :])
                last.then_inc(xs_turned, 1)

            def message(t, j):
                pe.wait_ge(xT_ready, t + (1 + ONE))
                for c, kept, made in ((0, y0_kept, y0_made), (1, y1_kept, y1_made)):
                    pe.wait_ge(kept, t + ONE)
                    for b in range(2):
                        last = pe.matmul(pg[:, 2 * c + b, :], xTs[:, j % LG, c, :],
                                         wblk[:, c, b * 4:b * 4 + 4, :].rearrange("p r o -> p (r o)"),
                                         start=True, stop=True)
                    last.then_inc(made, 1)
            turn_next(0, 0)
            with pe.Fori(0, NT // LG // 2) as k:
                for j in range(2 * LG):
                    turn_next(k * (2 * LG) + (j + 1), (j + 1) % (2 * LG))
                    message(k * (2 * LG) + j, j)
            for j in range(LG):
                if j + 1 < LG:
                    turn_next(NT - LG + j + 1, j + 1)
                message(NT - LG + j, j)

            pe.wait_ge(const_loaded, 16 * 16)
            pe.wait_ge(zeros_ready, 2)
            pe.wait_ge(y0_kept, NT + ONE)
            pe.wait_ge(y1_kept, NT + ONE)

            def keys_made(t):
                pe.wait_ge(kvx_ready, t + 1)
                pe.wait_ge(k_ready, t + ONE)
                pe.wait_ge(v_ready, t + ONE)
                for c in range(CC):
                    last = pe.matmul(p5[:, :], kvx[:, c, :], wkvT[:, c, :], start=(c == 0), stop=(c == CC - 1))
                last.then_inc(kv_made, 1)

            def keys_summed(t):
                pe.wait_ge(k_ready, t + (1 + ONE))
                pe.wait_ge(v_ready, t + (1 + ONE))
                for c in range(CC):
                    last = pe.matmul(p6[:, c * KW:c * KW + P + 1], ks[:, c * P:(c + 1) * P], vs[:, c, :],
                                     start=False, stop=False, skip_group_check=True)
                last.then_inc(kv_summed, 1)
            pe.matmul(p6[:, 0:C], zeros[:, 0:P], zeros[:, :], start=True, stop=False, skip_group_check=True)
            pe.matmul(p6[:, C:2 * C], zeros[:, 0:P], zeros[:, :], start=False, stop=False, skip_group_check=True)

            def mix_q(i, n):
                w = n * P
                pe.wait_ge(eq_ready, i + ONE)
                pe.wait_ge(q_ready, i + ONE)
                for m in range(CC):
                    for c in range(CC):
                        last = pe.matmul(p4[:, m * 2 * P:m * 2 * P + w], wqT[:, c, m * P:(m + 1) * P],
                                         xnT[:, bass.ds(2 * i, n), c, :], start=(c == 0), stop=(c == CC - 1))
                last.then_inc(q_made, 1)

            def mix_t(i, n):
                pe.wait_ge(q_ready, i + (1 + ONE))
                for k in range(n):
                    for m in range(CC):
                        last = pe.matmul((p4, p7)[k][:, m * KW:(m + 1) * KW], qs[:, m, k * P:(k + 1) * P],
                                         kvr[:, m, :], start=True, stop=True)
                last.then_inc(t_made, 1)

            def mix_turn(i, n):
                pe.wait_ge(x1_ready, 2 * i + n)
                for k in range(n):
                    for c in range(CC):
                        last = pe.transpose(p5[:, (k * CC + c) * P:(k * CC + c + 1) * P],
                                            x1[:, k, c * P:(c + 1) * P], ident[:, :])
                last.then_inc(x1_turned, 1)

            def mix_hidden(i, n):
                w = n * P
                pe.wait_ge(x1T_ready, i + 1)
                for m in range(CC):
                    for c in range(CC):
                        last = pe.matmul(p7[:, m * 2 * P:m * 2 * P + w], w1T[:, c, m * P:(m + 1) * P],
                                         x1T[:, 0:n, c, :], start=(c == 0), stop=(c == CC - 1))
                last.then_inc(h_made, 1)

            def mix_y(i, n):
                pe.wait_ge(h_ready, CC * (i + 1) if isinstance(i, int) else i * CC + CC)
                for k in range(n):
                    for m in range(CC):
                        pe.matmul(p6[:, k * C:(k + 1) * C], hs[:, m, k * P:(k + 1) * P], w2T[:, m, :],
                                  start=(m == 0), stop=False)
                    last = pe.matmul(p6[:, k * C:(k + 1) * C], ones[0:1, :], vecs[0:1, 2, :], start=False, stop=True)
                last.then_inc(y_made, 1)

            pe.matmul(p7[:, 0:C], zeros[:, 0:P], zeros[:, :], start=True, stop=True).then_inc(onehot_used, 1)
            for k in range(LAG):
                pe.matmul(pg[:, 4 - LAG + k, 0:C], zeros[:, 0:P], zeros[:, :], start=True, stop=True)\
                  .then_inc(pair_done, 1)
            pair = pe.alloc_register("pe_pair")
            pe.reg_mov(pair, 0)
            bounds = [pe.alloc_register(f"pe_bound{k}") for k in range(2 * SLOTS)]

            def load_bounds(r, groups=SLOTS):
                pe.load(bounds[0:2 * groups], ranges[0:1, bass.ds(r * (2 * SLOTS), 2 * groups)])
            pe.wait_ge(ranges_loaded, 16)

            def edges(r, s):
                pe.wait_ge(weighed, r * (SLOTS * GT) + (s * GT + GT))
                alone(pe)
                with pe.Fori(pe.snap(bounds[2 * s], min_val=0, max_val=NT - 1),
                             pe.snap(bounds[2 * s + 1], min_val=1, max_val=NT)):
                    p = pe.snap(pair, min_val=0, max_val=NG * NT)
                    pe.wait_ge(pair_added, p + ONE)
                    for j in range(GT):
                        if j % HALF == 0:
                            pe.wait_ge(onehot_ready, p * (GT // HALF) + (j // HALF + 1))
                        mm = pe.matmul(pg[:, bass.ds(p % 4, 1), 0:C], oh[:, s % 2, j, :], ring[:, s, j, :],
                                       start=(j == 0), stop=(j == GT - 1))
                        if j == HALF - 1:
                            mm.then_inc(onehot_used, 1)
                    mm.then_inc(pair_done, 1)
                    pe.reg_add(pair, pair, 1)

            with pe.Fori(0, KEY_ROUNDS) as r:
                load_bounds(r)
                for s in range(SLOTS):
                    keys_made(r * SLOTS + s)
                    edges(r, s)
                    keys_summed(r * SLOTS + s)

            def mix_round(i, r, following):
                load_bounds(r)
                edges(r, 0)
                pe.wait_ge(h_ready, i * CC)
                mix_t(i, 2)
                edges(r, 1)
                mix_y(i - 1, 2)
                for s in range(2, SLOTS):
                    if s == QUERY_GROUP:
                        pe.wait_ge(attention_stats, i * 2 + 2)
                        mix_q(i + 1, following)
                    if s == SLOTS - 1:
                        mix_turn(i, 2)
                    edges(r, s)
            load_bounds(KEY_ROUNDS)
            keys_made(NT - 1)
            mix_q(0, 2)
            edges(KEY_ROUNDS, 0)
            keys_summed(NT - 1)
            for s in range(1, SLOTS):
                edges(KEY_ROUNDS, s)
                if s == 2:
                    pe.wait_ge(kvr_ready, 1)
                    mix_t(0, 2)
                if s == SLOTS - 2:
                    pe.wait_ge(attention_stats, 2)
                    mix_q(1, 2)
                    mix_turn(0, 2)
            mix_hidden(0, 2)
            with pe.Fori(1, NT // 2 - 1) as i:
                mix_round(i, i + KEY_ROUNDS, 2)
                mix_hidden(i, 2)
            last = NT // 2
            mix_round(last - 1, ROUNDS - 1, 1)
            load_bounds(ROUNDS, TAIL)
            for s in range(TAIL):
                edges(ROUNDS, s)
            mix_t(last, 1)
            mix_hidden(last - 1, 2)
            mix_y(last - 1, 2)

            def rows_turn(g):
                pe.wait_ge(rowsT_ready, 3 * g + ONE)
                for j in range(LG):
                    bank = (p5[:, :], p4[:, :], pg[:, 3, :])[j // 2]
                    pe.wait_ge(rows_ready, LG * g + j + 1)
                    for c in range(CC):
                        q = j % 2 * C + c * P
                        last = pe.transpose(bank[:, q:q + P], rows[:, g, j, c * P:(c + 1) * P], ident[:, :])
                    if j % 2 or j == LG - 1:
                        last.then_inc(rows_turned, 1)

            def gate(g):
                pe.wait_ge(gap_ready, g + ONE)
                for j in range(LG):
                    if j % 2 == 0:
                        pe.wait_ge(rowsT_ready, 3 * g + (j // 2 + 1 + ONE))
                    for c in range(CC):
                        last = pe.matmul(pg[:, 2, j * X:(j + 1) * X], xfT[:, j, c, :], wg[:, c, :],
                                         start=(c == 0), stop=(c == CC - 1))
                last.then_inc(logits_made, 1)

            def rank(g):
                pe.wait_ge(both_ready, g + 1)
                pe.matmul(pg[:, 0, 0:LG * X], upper[:, :], both.rearrange("p j e -> p (j e)"), start=True, stop=False)
                pe.matmul(pg[:, 0, 0:LG * X], ones[:, :], before[:, 0:LG, :].rearrange("p j e -> p (j e)"),
                          start=False, stop=True).then_inc(rank_made, 1)
            rows_turn(0)
            for g in range(NT // LG):
                gate(g)
                if g == 1:
                    mix_turn(last, 1)
                    mix_hidden(last, 1)
                if g == 2:
                    mix_y(last, 1)
                if g + 1 < NT // LG:
                    rows_turn(g + 1)
                rank(g)
            pe.wait_ge(total_made, 1)
            pe.matmul(pg[:, 0, 0:X], ones[:, :], before[:, LG, :], start=True, stop=True).then_inc(total_done, 1)

            def turn(n):
                pe.wait_ge(tile_loaded, 16 * n + 16)
                pe.wait_ge(tileT_ready, n)
                for c in range(CC):
                    last = pe.transpose(p4[:, c * P:(c + 1) * P], xin[:, c * P:(c + 1) * P], ident[:, :])
                last.then_inc(tile_turned, 1)
            k = pe.alloc_register("pe_tile")
            pe.reg_mov(k, 0)
            cnt = pe.alloc_register("pe_count")
            pe.wait_ge(counts_ready, 2)
            turn(0)

            def expert(e, s, visit):
                w1, w2 = ew_sets[s]
                pe.load(cnt, tilesi[0:1, bass.ds(e, 1)])
                pe.wait_ge(weights_loaded[s], 32 * visit + 32)
                alone(pe)
                with pe.Fori(0, pe.snap(cnt, min_val=1, max_val=NT)):
                    n = pe.snap(k, min_val=0, max_val=X * NT)
                    pe.wait_ge(tileT_ready, n + 1)
                    pe.wait_ge(act_ready, n * MC + ONE)
                    for m in range(MC):
                        if m >= 4:
                            pe.wait_ge(act_ready, n * MC + (m - 3 + ONE))
                        for c in range(CC):
                            mm = pe.matmul(hbank[m % 4][:, m // 4 * P:m // 4 * P + P], w1[:, c, m * P:(m + 1) * P],
                                           xeT[:, c, :], start=(c == 0), stop=(c == CC - 1))
                        mm.then_inc(up_made, 1)
                    turn(n + 1)
                    pe.wait_ge(result_ready, n + ONE)
                    for m in range(MC):
                        pe.wait_ge(act_ready, n * MC + (m + 1 + ONE))
                        mm = pe.matmul(pg[:, 2, 0:C], h[:, m, :], w2[:, m, :], start=(m == 0), stop=(m == MC - 1))
                    mm.then_inc(down_made, 1)
                    pe.reg_add(k, k, 1)
                pe.matmul(p7[:, 0:1], zeros[:, 0:P], zeros[:, 0:1], start=True, stop=True).then_inc(weights_used[s], 1)
            with pe.Fori(0, X // 2) as visit:
                expert(visit * 2, 0, visit)
                expert(visit * 2 + 1, 1, visit)

        @block.vector
        def _(dve):
            for counted_from_one in (y1_kept, k_ready, q_ready, gap_ready, pair_added, meta_ready, result_ready):
                dve.sem_inc(counted_from_one, ONE)
            dve.memset(zeros[:, :], 0.0).then_inc(zeros_ready, 1)
            dve.memset(eps[:, :], EPS_LN).then_inc(zeros_ready, 1)

            def norm_stats(g):
                ch = Chain(dve, norm_step, g * A_STEPS)
                w = LG

                def tiles(j):
                    return acc[:, bass.ds(g * LG + j, 1), :].rearrange("p o c -> p (o c)")
                for j in range(w):
                    ch.step(dve.bn_stats(st[:, j, :], tiles(j)))
                ch.wait(apart=True)
                for j in range(w):
                    ch.step(dve.bn_aggr(mv[:, j, :], st[:, j, :]))
                ch.wait()
                dve.tensor_scalar(var[:, 0:w], mv[:, 0:w, 1], EPS_LN, None, ALU.add).then_inc(var_ready, 1)
                assert ch.n == A_STEPS

            def stats(ch, tiles, w, st, mv, done):
                for j in range(w):
                    ch.step(dve.bn_stats(st[:, j, :], tiles(j)))
                ch.wait(apart=True)
                for j in range(w):
                    dve.bn_aggr(mv[:, j, :], st[:, j, :]).then_inc(done, 1)

            def evict(g, j):
                dve.wait_ge(y1_made, g * LG + (j + 1))
                if not isinstance(g, int):
                    dve.wait_ge(y_stored[j], g * 16)
                dve.tensor_copy(ys[:, j, :, P:2 * P], pg[:, 2:4, :].rearrange("p b (r o) -> p (b r) o", o=P))\
                   .then_inc(y1_kept, 1)

            def normed(g, at):
                dve.wait_ge(rs_ready, g + 1)
                if not isinstance(g, int) or g >= 2:
                    dve.wait_ge(xs_turned, g * LG - LG)
                    dve.wait_ge(xn_kept, g * LG - LG)
                for j in range(LG):
                    dve.tensor_scalar(xs[:, bass.ds(at + j, 1), :].rearrange("p o c -> p (o c)"),
                                      acc[:, bass.ds(g * LG + j, 1), :].rearrange("p o c -> p (o c)"),
                                      mv[:, j, 0:1], rs[:, j:j + 1], ALU.subtract, ALU.mult).then_inc(xs_ready, 1)
            dve.wait_ge(x_first, 16)
            norm_stats(0)
            normed(0, 0)
            evict(0, 0)
            dve.wait_ge(x_rest, 16 * (NT // LG - 1))
            norm_stats(1)
            evict(0, 1)
            normed(1, LG)
            evict(0, 2)
            norm_stats(2)
            evict(0, 3)
            normed(2, 0)
            evict(0, 4)
            dve.wait_ge(edges_loaded, 80)
            dve.scalar_tensor_tensor(idx[:, :], srcT[:, :], float(R), relT[:, :], ALU.mult, ALU.add)\
               .then_inc(idx_ready, 1)
            dve.tensor_copy(dstf[:, :], dstT[:, :]).then_inc(dstf_ready, 1)
            ch = Chain(dve, setup_step)
            ch.step(dve.tensor_reduce(rng2[:, 0:1], dstrow[:, :], AX_X, ALU.min))
            ch.link(dve.tensor_reduce(rng2[:, 1:2], dstrow[:, :], AX_X, ALU.max))
            ch.link(dve.tensor_scalar(rng3[:, :], rng2[:, :], P.bit_length() - 1, None, ALU.arith_shift_right))
            dve.tensor_scalar(rng3[:, 1:2], rng3[:, 1:2], 1.0, None, ALU.add).then_inc(ranges_ready, 1)
            with dve.Fori(1, NT // LG - 2) as g:
                for j in range(LG):
                    if j == LG - 2:
                        norm_stats(g + 2)
                    evict(g, j)
                    if j == LG - 2:
                        normed(g + 2, (g % 2) * LG)
            with dve.Fori(NT // LG - 2, NT // LG) as g:
                for j in range(LG):
                    evict(g, j)

            pair = dve.alloc_register("dve_pair")
            dve.reg_mov(pair, 0)
            tiles = [dve.alloc_register(f"dve_tile{k}") for k in range(LAG)]
            for reg in tiles:
                dve.reg_mov(reg, 0)
            started = dve.alloc_register("dve_started")
            dve.reg_mov(started, 0)
            used = dve.alloc_register("dve_used")
            bounds = [dve.alloc_register(f"dve_bound{k}") for k in range(2 * SLOTS)]
            dve.wait_ge(ranges_loaded, 16)
            dve.wait_ge(iota_ready, 2)
            dve.wait_ge(dstf_ready, 1)
            dve.wait_ge(bias_added, NT)
            dve.wait_ge(xn_kept, NT)

            def add_pair(p):
                t = dve.snap(tiles[0], min_val=0, max_val=NT - 1)
                dve.wait_ge(pair_done, p + 1)
                dve.wait_ge(pair_added, p + ONE)
                row = acc[:, bass.ds(t, 1), :]
                dve.tensor_tensor(row, row, pg[:, bass.ds((p + (4 - LAG)) % 4, 1), 0:C], ALU.add)\
                   .then_inc(pair_added, 1)

            def shift(d):
                for k in range(LAG - 1):
                    dve.reg_mov(tiles[k], tiles[k + 1])
                if d is not None:
                    dve.reg_mov(tiles[LAG - 1], d)

            def load_bounds(r, groups=SLOTS):
                dve.load(bounds[0:2 * groups], ranges[0:1, bass.ds(r * (2 * SLOTS), 2 * groups)])

            def edges(r, s):
                dve.reg_mov(used, started)
                dve.reg_mov(started, pair)
                with dve.Fori(dve.snap(bounds[2 * s], min_val=0, max_val=NT - 1),
                              dve.snap(bounds[2 * s + 1], min_val=1, max_val=NT)) as d:
                    p = dve.snap(pair, min_val=0, max_val=NG * NT)
                    free = dve.snap(used, min_val=0, max_val=NG * NT)
                    for j in range(0, GT, HALF):
                        if j == 0:
                            dve.wait_ge(onehot_used, free + 1)
                        else:
                            dve.wait_ge(pair_done, free + LAG)
                        col = r * (SLOTS * GT) + (s * GT + j)
                        dve.tensor_tensor(oh[:, s % 2, j:j + HALF, :],
                                          iota[:, bass.ds(d * P, P)].unsqueeze(1).to_broadcast([P, HALF, P]),
                                          dstf[:, bass.ds(col, HALF)].unsqueeze(2).to_broadcast([P, HALF, P]),
                                          ALU.is_equal).then_inc(onehot_ready, 1)
                    add_pair(p)
                    shift(d)
                    dve.reg_add(pair, pair, 1)
                    dve.reg_mov(used, pair)
                dve.sem_inc(group_used[s - LAG], 1)

            def keys(t):
                dve.wait_ge(ek_ready, t + 1)
                dve.wait_ge(kv_summed, t + ONE)
                dve.wait_ge(v_ready, t + (1 + ONE))
                dve.scalar_tensor_tensor(ks, p5[:, 0:C], 0.0, ek[:, 0:C], ALU.max, ALU.add).then_inc(k_ready, 1)
            with dve.Fori(0, KEY_ROUNDS) as r:
                load_bounds(r)
                for s in range(SLOTS):
                    edges(r, s)
                    keys(r * SLOTS + s)

            def norm_apply(ch, src, n, mean, sd, gain):
                ch.step(dve.reciprocal(sd[:, 0:n], sd[:, 0:n]))
                for k in range(n):
                    ch.step(dve.scalar_tensor_tensor(src[:, k, :], src[:, k, :], mean[:, k, 0:1], vecs[:, gain, :],
                                                     ALU.subtract, ALU.mult))
                ch.wait()

            def two(v, w):
                return v.rearrange("p (m n) -> p m n", m=CC)[:, :, 0:w]

            def mix_q(i, n):
                w = n * P
                dve.wait_ge(eq_ready, i + (1 + ONE))
                dve.scalar_tensor_tensor(qs[:, :, 0:w], two(p4[:, :], w), 0.0, two(ek, w), ALU.max, ALU.add)\
                   .then_inc(q_ready, 1)

            def mix_t(i, n):
                ch = Chain(dve, attention_step, i * C_STEPS)
                dve.wait_ge(t_made, i + 1)
                tt = [(p4, p7)[k][:, 0:CC * KW].rearrange("p (m k) -> p m k", m=CC) for k in range(n)]
                for k in range(n):
                    ch.step(dve.tensor_scalar(z[:, k, :].rearrange("p (m h) -> p m h", m=CC), tt[k][:, :, P:KW],
                                              EPS_ATTN, None, ALU.add))
                ch.wait()
                ch.link(dve.reciprocal(z[:, 0:n, :], z[:, 0:n, :]))
                for k in range(n):
                    zb = z[:, k, :].rearrange("p (m h) -> p m h", m=CC).unsqueeze(3).to_broadcast([P, CC, HC, HD])
                    ch.step(dve.tensor_tensor(u[:, k, :].rearrange("p (m h d) -> p m h d", m=CC, h=HC),
                                              tt[k][:, :, 0:P].rearrange("p m (h d) -> p m h d", h=HC), zb, ALU.mult))
                ch.wait()
                ch.link(dve.tensor_tensor(u[:, 0:n, :], u[:, 0:n, :], xn[:, bass.ds(2 * i, n), :], ALU.add))
                stats(ch, lambda j: u[:, j, :], n, st, mv, attention_stats)
                if n == 2:
                    assert ch.n == C_STEPS, ch.n

            def mix_x1(i, n):
                ch = Chain(dve, x1_step, i * E_STEPS)
                dve.wait_ge(attention_dev, i + 1)
                norm_apply(ch, u, n, mv, rs, 0)
                for k in range(n):
                    dve.scalar_tensor_tensor(x1[:, k, :], u[:, k, :], rs[:, k:k + 1], vecs[:, 1, :],
                                             ALU.mult, ALU.add).then_inc(x1_ready, 1)
                if n == 2:
                    assert ch.n == E_STEPS, ch.n

            def mix_y(i, n):
                ch = Chain(dve, hidden_step, i * F_STEPS)
                dve.wait_ge(y_made, i + (1 + ONE))
                ch.link(dve.tensor_tensor(u2[:, 0:n, :], p6[:, 0:n * C].rearrange("p (i c) -> p i c", i=n),
                                          x1[:, 0:n, :], ALU.add))
                stats(ch, lambda j: u2[:, j, :], n, st2, mv2, hidden_stats)
                if n == 2:
                    assert ch.n == F_STEPS, ch.n

            def mix_out(i, n):
                ch = Chain(dve, mix_out_step, i * E_STEPS)
                dve.wait_ge(hidden_dev, i + 1)
                norm_apply(ch, u2, n, mv2, rs2, 3)
                dve.wait_ge(pair_added, dve.snap(pair, min_val=0, max_val=NG * NT) + ONE)
                for k in range(n):
                    row = acc[:, bass.ds(2 * i + k, 1), :].rearrange("p o c -> p (o c)")
                    dve.scalar_tensor_tensor(row, u2[:, k, :], rs2[:, k:k + 1], row, ALU.mult, ALU.add)\
                       .then_inc(mix_done, 1)
                dve.wait_ge(mix_done, 2 * i + n)

            def mix_round(i, r):
                load_bounds(r)
                mix_q(i, 2)
                edges(r, 0)
                edges(r, 1)
                mix_t(i, 2)
                edges(r, 2)
                mix_y(i - 1, 2)
                edges(r, 3)
                mix_x1(i, 2)
                edges(r, 4)
                mix_out(i - 1, 2)
                edges(r, 5)

            def attention_state():
                dve.wait_ge(kv_summed, NT + ONE)
                for c in range(CC):
                    dve.tensor_tensor(kvr[:, c, 0:P], p6[:, c * KW:c * KW + P], blockmask[:, 0:P], ALU.mult)\
                       .then_inc(setup_step, 1)
                    dve.tensor_tensor(kvr[:, c, P:KW], blockmask[:, P:KW],
                                      p6[:, c * KW + P:c * KW + P + 1].to_broadcast([P, HC]), ALU.mult).then_inc(setup_step, 1)
                dve.wait_ge(setup_step, 3 + 2 * CC)
                alone(dve)
                dve.engine_nop().then_inc(kvr_ready, 1)

            load_bounds(KEY_ROUNDS)
            edges(KEY_ROUNDS, 0)
            keys(NT - 1)
            edges(KEY_ROUNDS, 1)
            attention_state()
            mix_q(0, 2)
            edges(KEY_ROUNDS, 2)
            edges(KEY_ROUNDS, 3)
            mix_t(0, 2)
            edges(KEY_ROUNDS, 4)
            mix_x1(0, 2)
            edges(KEY_ROUNDS, 5)
            with dve.Fori(1, NT // 2) as i:
                mix_round(i, i + KEY_ROUNDS)
            last = NT // 2
            load_bounds(ROUNDS, TAIL)
            mix_q(last, 1)
            for s in range(TAIL):
                edges(ROUNDS, s)
            for k in range(LAG):
                add_pair(dve.snap(pair, min_val=0, max_val=NG * NT))
                shift(None)
                dve.reg_add(pair, pair, 1)

            def bc(v, n):
                return v.unsqueeze(1).to_broadcast([P, n, X])
            cd = Chain(dve, counts_step)
            cd.link(dve.memset(before[:, LG, :], 0.0))
            cd.link(dve.memset(rows[:, :, :, C:ROW], 0.0))
            for g in range(NT // LG):
                cd.step(dve.tensor_copy(rows[:, g, :, TOK], tokid[:, g * LG:(g + 1) * LG]))

            def rows_scale(g):
                t = slice(g * LG, (g + 1) * LG)
                dve.wait_ge(row_dev_ready, g + 1)
                cr.link(dve.reciprocal(row_dev[:, t], row_dev[:, t]))
                cr.step(dve.scalar_tensor_tensor(shift_by[:, t], row_mv[:, t, 0], -1.0, row_dev[:, t], ALU.mult, ALU.mult))
                cr.wait()
                alone(dve)
                dve.engine_nop().then_inc(rows_shift, 1)

            def dispatch(g):
                ch = Chain(dve, gate_step, g * D_STEPS)
                dve.wait_ge(logits_made, g + (1 + ONE))
                ch.link(dve.tensor_tensor(lg, pg[:, 2, 0:LG * X].rearrange("p (j e) -> p j e", j=LG), bc(bg[:, :], LG),
                                          ALU.add), apart=True)
                for j in range(LG):
                    ch.step(dve.max(mx[:, j, :], lg[:, j, :]))
                ch.wait(apart=True)
                for j in range(LG):
                    ch.step(dve.max_index(ix[:, j, :], mx[:, j, :], lg[:, j, :]))
                ch.step(dve.tensor_tensor(gap, mx[:, :, 1], mx[:, :, 0], ALU.subtract))
                ch.wait()
                alone(dve)
                dve.engine_nop().then_inc(gap_ready, 1)
                ch.link(dve.tensor_copy(rows[:, g, :, EX:EX + 2], ix[:, :, 0:2]))
                for k, o1 in ((0, oh1), (1, oh2)):
                    ch.step(dve.tensor_tensor(o1, bc(iota8[:, :], LG),
                                              rows[:, g, :, EX + k:EX + k + 1].to_broadcast([P, LG, X]), ALU.is_equal))
                ch.wait()
                ch.step(dve.tensor_tensor(both, oh1, oh2, ALU.add))
                ch.link(dve.tensor_copy(before[:, 0, :], before[:, LG, :]))
                for j in range(LG):
                    ins = dve.tensor_tensor(before[:, j + 1, :], before[:, j, :], both[:, j, :], ALU.add)
                    ch.link(ins)
                alone(dve)
                dve.engine_nop().then_inc(both_ready, 1)
                dve.wait_ge(ex_ready, g + 1)
                ch.link(dve.tensor_scalar(den, ex, 1.0, None, ALU.add))
                ch.link(dve.reciprocal(rows[:, g, :, WT], den))
                ch.step(dve.tensor_tensor(rows[:, g, :, WT + 1], ex, rows[:, g, :, WT], ALU.mult))
                dve.wait_ge(rank_made, g + 1)
                ch.link(dve.tensor_tensor(place, pg[:, 0, 0:LG * X].rearrange("p (j e) -> p j e", j=LG),
                                          bc(capcol[:, :], LG), ALU.add))
                for k, o1 in ((0, oh1), (1, oh2)):
                    ch.link(dve.tensor_tensor(pick, o1, place, ALU.mult))
                    ch.link(dve.tensor_reduce(slotf[:, k, :], pick, AX_X, ALU.add))
                ch.link(dve.tensor_copy(sloti[:, g, :, :], slotf))
                alone(dve)
                dve.engine_nop().then_inc(slots_ready, 1)
                assert ch.n == D_STEPS, ch.n
            def row_stats(g):
                stats(cs, lambda j: acc[:, g * LG + j, :], LG, st, row_mv[:, g * LG:(g + 1) * LG, :], row_stats_ready)
            cs, cr = Chain(dve, row_stats_step), Chain(dve, row_scale_step)
            row_stats(0)
            mix_t(last, 1)
            rows_scale(0)
            row_stats(1)
            mix_y(last - 1, 2)
            mix_x1(last, 1)
            mix_out(last - 1, 2)
            rows_scale(1)
            dispatch(0)
            row_stats(2)
            rows_scale(2)
            row_stats(3)
            dispatch(1)
            rows_scale(3)
            dispatch(2)
            mix_y(last, 1)
            mix_out(last, 1)
            alone(dve)
            dve.engine_nop().then_inc(total_ready, 1)
            row_stats(4)
            rows_scale(4)
            dispatch(3)
            dispatch(4)
            alone(dve)
            dve.engine_nop().then_inc(total_made, 1)
            dve.wait_ge(total_done, 1)
            cd.link(dve.tensor_copy(countf, pg[:, 0, 0:X]))
            dve.tensor_copy(counti[:, :], countf).then_inc(counts_ready, 1)
            cd.link(dve.tensor_scalar(countf, countf, float(P - 1), float(P), ALU.add, ALU.max))
            cd.link(dve.tensor_copy(tilesi[:, :], countf))
            dve.tensor_scalar(tilesi[:, :], tilesi[:, :], P.bit_length() - 1, None, ALU.arith_shift_right)\
               .then_inc(counts_ready, 1)

            k = dve.alloc_register("dve_tile")
            dve.reg_mov(k, 0)
            cnt = dve.alloc_register("dve_count")
            dve.wait_ge(counts_ready, 2)

            def turned(n):
                dve.wait_ge(tile_turned, n + (1 + ONE))
                dve.tensor_copy(xeT.rearrange("p c n -> p (c n)"), p4[:, 0:C]).then_inc(tileT_ready, 1)

            def meta_kept(n):
                dve.wait_ge(tile_loaded, 16 * n + 16)
                dve.tensor_copy(meta, xin[:, C:ROW]).then_inc(meta_ready, 1)
            turned(0)
            meta_kept(0)

            M_STEPS = 6

            def expert(e, s, visit):
                dve.load(cnt, tilesi[0:1, bass.ds(e, 1)])
                with dve.Fori(0, dve.snap(cnt, min_val=1, max_val=NT)):
                    n = dve.snap(k, min_val=0, max_val=X * NT)
                    ch = Chain(dve, result_step, n * M_STEPS)
                    dve.wait_ge(meta_ready, n + (1 + ONE))
                    ch.link(dve.tensor_scalar(same, meta[:, EX - C:EX - C + 2], iota8[:, bass.ds(e, 1)], None,
                                              ALU.is_equal))
                    ch.link(dve.tensor_tensor(wsel[:, 0:2], same, meta[:, WT - C:WT - C + 2], ALU.mult))
                    ch.link(dve.tensor_tensor(wsel[:, 2:3], wsel[:, 0:1], wsel[:, 1:2], ALU.add))
                    dve.wait_ge(up_made, n * MC + MC)
                    turned(n + 1)
                    dve.wait_ge(tile_added, n + ONE)
                    ch.link(dve.tensor_copy(toki[:, :], meta[:, TOK - C:TOK - C + 1]))
                    meta_kept(n + 1)
                    dve.wait_ge(down_made, n + (1 + ONE))
                    ch.link(dve.tensor_tensor(yt, pg[:, 2, 0:C], eb2[:, bass.ds(e, 1), :].rearrange("p o c -> p (o c)"),
                                              ALU.add))
                    ch.link(dve.tensor_scalar(yo, yt, wsel[:, 2:3], None, ALU.mult))
                    alone(dve)
                    dve.engine_nop().then_inc(result_ready, 1)
                    assert ch.n == M_STEPS
                    dve.reg_add(k, k, 1)
            with dve.Fori(0, X // 2) as visit:
                expert(visit * 2, 0, visit)
                expert(visit * 2 + 1, 1, visit)


def kernel(**inputs):
    import numpy as np
    import concourse.bacc as bacc
    from concourse.bass_utils import run_bass_kernel_spmd

    g = {k: np.ascontiguousarray(np.asarray(v)) for k, v in inputs.items()}
    f32 = np.float32

    def pad(v, n, fill=0):
        o = np.full((n,) + v.shape[1:], fill, v.dtype)
        o[:v.shape[0]] = v
        return o

    def turned(v):
        return np.ascontiguousarray(v.reshape(GP * GT, P).T)

    def chunks(w, n):
        return np.ascontiguousarray(w.reshape(n, P, -1).transpose(1, 0, 2))

    def rows(v):
        return np.ascontiguousarray(np.broadcast_to(v, (P,) + v.shape))

    src, rel = (pad(g[k], GP * GT * P) for k in ("src", "edge_type_8"))
    dst = pad(g["dst"], GP * GT * P, N - 1)
    gw = g["L0_gnn_weight"].reshape(R, CC, HC, HD, HD)
    wblk = np.zeros((P, CC, R, P), f32)
    for c in range(CC):
        for b in range(HC):
            for r in range(R):
                wblk[b * HD:(b + 1) * HD, c, r, b * HD:(b + 1) * HD] = gw[r, c, b]
    wqkv = g["L0_mix_Wqkv"].T
    blockmask = np.zeros((P, KW), f32)
    for b in range(HC):
        blockmask[b * HD:(b + 1) * HD, b * HD:(b + 1) * HD] = 1
        blockmask[b * HD:(b + 1) * HD, P + b] = 1
    padrows = np.zeros((P, ROW), f32)
    padrows[:, TOK] = NP + np.arange(P)
    padrows[:, EX:EX + 2] = -1
    arrays = {
        "x": pad(g["x"], NP),
        "srcT": turned(src), "relT": turned(rel), "dstT": turned(dst), "ewT": turned(pad(g["edge_weight"], GP * GT * P)),
        "dstrow": np.ascontiguousarray(dst.reshape(GP, GT * P)[0:NG]),
        "wblk": wblk,
        "ident": np.eye(P, dtype=f32), "upper": np.triu(np.ones((P, P), f32), 1), "ones": np.ones((P, P), f32),
        "blockmask": blockmask,
        "nodemask": (np.arange(NP - P, NP) < N).astype(f32).reshape(P, 1),
        "vecs": rows(np.stack([g["L0_mix_ln1_g"], g["L0_mix_ln1_b"], g["L0_mix_b2"], g["L0_mix_ln2_g"],
                               g["L0_mix_ln2_b"]])),
        "b1T": np.ascontiguousarray(g["L0_mix_b1"].reshape(CC, P).T),
        "wqT": chunks(wqkv[:, 0:C], CC), "wkvT": chunks(wqkv[:, C:3 * C], CC),
        "w1T": chunks(g["L0_mix_W1"].T, CC), "w2T": chunks(g["L0_mix_W2"].T, CC),
        "wg": chunks(g["L0_ffn_Wg"], CC), "bg": rows(g["L0_ffn_bg"]),
        "eb1T": np.ascontiguousarray(g["L0_ffn_b1"].reshape(X, MC, P).transpose(2, 0, 1)),
        "capcol": rows(np.arange(X, dtype=f32) * CAP), "iota8": rows(np.arange(X, dtype=f32)),
        "padrows": padrows,
        "ew1": np.ascontiguousarray(g["L0_ffn_W1"].reshape(X, CC, P, HID).transpose(0, 2, 1, 3)),
        "ew2": np.ascontiguousarray(g["L0_ffn_W2"].reshape(X, MC, P, C).transpose(0, 2, 1, 3)),
        "eb2": rows(g["L0_ffn_b2"]),
    }
    nc = bacc.Bacc("TRN2", target_bir_lowering=False, num_devices=1)
    args = {n: nc.dram_tensor(f"in_{n}", v.shape, mybir.dt.from_np(v.dtype), kind="ExternalInput").ap()
            for n, v in arrays.items()}
    out = nc.dram_tensor("out", [NP + P, C], F32, kind="ExternalOutput").ap()
    build(nc, args, out)
    r = run_bass_kernel_spmd(nc, [{f"in_{n}": v for n, v in arrays.items()}], core_ids=[0])
    return r.results[0]["out"][0:N]
```
